# Optimizing a Trainium2 kernel written in Bass

```python
import numpy as np
import jax
import jax.numpy as jnp

def _softmax(x, axis=-1):
    return jax.nn.softmax(x, axis=axis)

def _gelu(x):
    return jax.nn.gelu(x, approximate=True)

def _silu(x):
    return jax.nn.silu(x)

def _sigmoid(x):
    return jax.nn.sigmoid(x)

def _layernorm(x, axis=-1, eps=1e-05):
    m = jnp.mean(x, axis=axis, keepdims=True)
    v = jnp.var(x, axis=axis, keepdims=True)
    return (x - m) / jnp.sqrt(v + eps)

def _scatter_add(tgt, idx, src, axis=0):
    return tgt.at[idx].add(src)

def _segment_sum(src, seg, n):
    return jax.ops.segment_sum(src, seg, n)
kernel_name = 'mk_gps_d1_gnn_r8_0d03de'

def setup_inputs(seed: int=0):
    np.random.seed(seed)
    _w = jnp.asarray

    def _rec_inputs():
        import jax
        import jax.numpy as jnp
        _gk = jax.random.key(seed)
        x = -0.0003713 + 1 * jax.random.normal(jax.random.fold_in(_gk, 1), (6250, 256), jnp.float32)
        src = jax.random.randint(jax.random.fold_in(_gk, 2), (100000,), 0, 6250, jnp.int32)
        dst = jax.random.randint(jax.random.fold_in(_gk, 3), (100000,), 0, 6250, jnp.int32)
        _o = jnp.argsort(dst, stable=True)
        src = src[_o]
        dst = dst[_o]
        return (x, src, dst)
    x, src, dst = _rec_inputs()

    def _L0_gnn_setup():
        import jax, jax.numpy as jnp
        import numpy as np
        N, E, D_IN, D_OUT = (6250, 200000, 256, 256)
        key = jax.random.key(seed)
        k1, k2, k3, k4, k5, k6 = jax.random.split(key, 6)
        x = jax.random.normal(k1, (N, D_IN), dtype=jnp.float32)
        edge_index = jax.random.randint(k2, (2, E), 0, N, dtype=jnp.int64)
        s = 1.0 / np.sqrt(D_IN)
        W1 = jax.random.uniform(k3, (D_OUT, D_IN), minval=-s, maxval=s, dtype=jnp.float32)
        b1 = jax.random.uniform(k4, (D_OUT,), minval=-s, maxval=s, dtype=jnp.float32)
        W2 = jax.random.uniform(k5, (D_OUT, D_IN), minval=-s, maxval=s, dtype=jnp.float32)
        b2 = jax.random.uniform(k6, (D_OUT,), minval=-s, maxval=s, dtype=jnp.float32)
        return {'x': x, 'W1': W1, 'b1': b1, 'W2': W2, 'b2': b2, 'edge_index': edge_index}
    _L0_gnn_all = _L0_gnn_setup()
    _L0_gnn_in = {k: v for k, v in _L0_gnn_all.items() if k in ('W1', 'b1', 'W2', 'b2')}
    del _L0_gnn_all

    def _L0_mix_setup():
        import jax, jax.numpy as jnp
        import numpy as np
        EPS = 1e-05

        def _layernorm(x, weight, bias):
            mean = jnp.mean(x, axis=-1, keepdims=True)
            std = jnp.std(x, axis=-1, keepdims=True, ddof=1)
            out = (x - mean) / (std + EPS)
            return weight * out + bias
        key = jax.random.key(seed)
        B, N, C = (4, 4096, 256)
        H, hc = (8, C // 8)
        kx, = jax.random.split(key, 1)
        x = jax.random.normal(kx, (B, N, C), dtype=jnp.float32)
        return {'x': x, 'kln_weight': jnp.ones((H, 1, hc), dtype=jnp.float32), 'kln_bias': jnp.zeros((H, 1, hc), dtype=jnp.float32), 'vln_weight': jnp.ones((H, 1, hc), dtype=jnp.float32), 'vln_bias': jnp.zeros((H, 1, hc), dtype=jnp.float32)}
    _L0_mix_all = _L0_mix_setup()
    _L0_mix_in = {k: v for k, v in _L0_mix_all.items() if k in ('kln_weight', 'kln_bias', 'vln_weight', 'vln_bias')}
    del _L0_mix_all

    def _L0_ffn_setup():
        import math
        import jax, jax.numpy as jnp
        import numpy as np
        CAPACITY_FACTOR = 1.25
        key = jax.random.key(seed)
        ks = jax.random.split(key, 5)
        B, L, D, F, E = (8, 1024, 256, 1024, 8)
        h = jax.random.normal(ks[0], (B, L, D), dtype=jnp.float32)
        gate_w = jax.random.normal(ks[1], (D, E), dtype=jnp.float32) * 0.02
        gate_b = jnp.zeros((E,), dtype=jnp.float32)
        w1 = jax.random.normal(ks[2], (E, D, F), dtype=jnp.float32) * (1.0 / math.sqrt(D))
        b1 = jnp.zeros((E, F), dtype=jnp.float32)
        w2 = jax.random.normal(ks[3], (E, F, D), dtype=jnp.float32) * (1.0 / math.sqrt(F))
        b2 = jnp.zeros((E, D), dtype=jnp.float32)
        return {'h': h, 'gate_w': gate_w, 'gate_b': gate_b, 'w1': w1, 'b1': b1, 'w2': w2, 'b2': b2}
    _L0_ffn_all = _L0_ffn_setup()
    _L0_ffn_in = {k: v for k, v in _L0_ffn_all.items() if k in ('gate_w', 'gate_b', 'w1', 'b1', 'w2', 'b2')}
    del _L0_ffn_all
    return {'x': x, 'src': src, 'dst': dst, 'L0_gnn_W1': _L0_gnn_in['W1'], 'L0_gnn_b1': _L0_gnn_in['b1'], 'L0_gnn_W2': _L0_gnn_in['W2'], 'L0_gnn_b2': _L0_gnn_in['b2'], 'L0_mix_kln_weight': _L0_mix_in['kln_weight'], 'L0_mix_kln_bias': _L0_mix_in['kln_bias'], 'L0_mix_vln_weight': _L0_mix_in['vln_weight'], 'L0_mix_vln_bias': _L0_mix_in['vln_bias'], 'L0_ffn_gate_w': _L0_ffn_in['gate_w'], 'L0_ffn_gate_b': _L0_ffn_in['gate_b'], 'L0_ffn_w1': _L0_ffn_in['w1'], 'L0_ffn_b1': _L0_ffn_in['b1'], 'L0_ffn_w2': _L0_ffn_in['w2'], 'L0_ffn_b2': _L0_ffn_in['b2']}

def reference(x, src, dst, L0_gnn_W1, L0_gnn_b1, L0_gnn_W2, L0_gnn_b2, L0_mix_kln_weight, L0_mix_kln_bias, L0_mix_vln_weight, L0_mix_vln_bias, L0_ffn_gate_w, L0_ffn_gate_b, L0_ffn_w1, L0_ffn_b1, L0_ffn_w2, L0_ffn_b2):
    import jax
    import jax.numpy as jnp

    def _L0_gnn_ref(x, W1, b1, W2, b2, edge_index):
        import jax, jax.numpy as jnp
        import numpy as np
        N, E, D_IN, D_OUT = (6250, 200000, 256, 256)
        dst = edge_index[0]
        nbr = edge_index[1]
        n = x.shape[0]
        agg = jax.ops.segment_sum(x[nbr], dst, num_segments=n)
        cnt = jax.ops.segment_sum(jnp.ones((nbr.shape[0],), x.dtype), dst, num_segments=n)
        mean = agg / jnp.maximum(cnt, 1.0)[:, None]
        return x @ W1.T + b1 + mean @ W2.T + b2

    def _L0_mix_ref(x, kln_weight, kln_bias, vln_weight, vln_bias):
        import jax, jax.numpy as jnp
        import numpy as np
        EPS = 1e-05

        def _layernorm(x, weight, bias):
            mean = jnp.mean(x, axis=-1, keepdims=True)
            std = jnp.std(x, axis=-1, keepdims=True, ddof=1)
            out = (x - mean) / (std + EPS)
            return weight * out + bias
        B, N, C = x.shape
        H = kln_weight.shape[0]
        hc = C // H
        qkv = x.reshape(B, N, H, hc).transpose(0, 2, 1, 3)
        q = qkv
        k = _layernorm(qkv, kln_weight, kln_bias)
        v = _layernorm(qkv, vln_weight, vln_bias)
        kv = jnp.einsum('bhnd,bhne->bhde', k, v) / N
        out = jnp.einsum('bhnd,bhde->bhne', q, kv)
        out = out.transpose(0, 2, 1, 3).reshape(B, N, C)
        return out + x

    def _L0_ffn_ref(h, gate_w, gate_b, w1, b1, w2, b2):
        import math
        import jax, jax.numpy as jnp
        import numpy as np
        CAPACITY_FACTOR = 1.25
        B, L, D = h.shape
        E = gate_w.shape[1]
        T = B * L
        C = max(1, math.ceil(CAPACITY_FACTOR * T / E))
        x = h.reshape(T, D)
        logits = x @ gate_w + gate_b
        probs = jax.nn.softmax(logits, axis=-1)
        idx = jnp.argmax(probs, axis=-1)
        prb = jnp.take_along_axis(probs, idx[:, None], axis=1)[:, 0]
        one_hot = jax.nn.one_hot(idx, E, dtype=jnp.float32)
        pos = (jnp.cumsum(one_hot, axis=0) * one_hot).sum(-1).astype(jnp.int32) - 1
        kept = pos < C
        pos_safe = jnp.where(kept, pos, C)
        buf = jnp.zeros((E, C, D), dtype=h.dtype).at[idx, pos_safe].set(x, mode='drop')
        hmid = jax.nn.relu(jnp.einsum('ecd,edf->ecf', buf, w1) + b1[:, None, :])
        ybuf = jnp.einsum('ecf,efd->ecd', hmid, w2) + b2[:, None, :]
        pos_g = jnp.minimum(pos, C - 1)
        y_tok = ybuf[idx, pos_g] * (prb * kept)[:, None]
        y = y_tok.reshape(B, L, D)
        y = jnp.nan_to_num(y, nan=0.0, posinf=10000.0, neginf=-10000.0)
        return y
    edge_index = jnp.stack([src, dst])
    xn = _layernorm(x, axis=-1)
    x = x + _L0_gnn_ref(xn, L0_gnn_W1, L0_gnn_b1, L0_gnn_W2, L0_gnn_b2, edge_index) + _L0_mix_ref(xn[None], L0_mix_kln_weight, L0_mix_kln_bias, L0_mix_vln_weight, L0_mix_vln_bias)[0]
    x = x + _L0_ffn_ref(_layernorm(x, axis=-1)[None], L0_ffn_gate_w, L0_ffn_gate_b, L0_ffn_w1, L0_ffn_b1, L0_ffn_w2, L0_ffn_b2)[0]
    return x

_drawn_inputs = setup_inputs


def setup_inputs(seed=0):
    import zlib

    import numpy as np

    out = dict(_drawn_inputs(seed))
    spreads = {'L0_mix_kln_weight': (1.0, 0.2),
     'L0_mix_kln_bias': (0.0, 0.454),
     'L0_mix_vln_weight': (1.0, 0.2),
     'L0_mix_vln_bias': (0.0, 0.457),
     'L0_ffn_gate_b': (0.0, 0.1),
     'L0_ffn_b1': (0.0, 0.8),
     'L0_ffn_b2': (0.0, 0.8)}
    factors = {'L0_gnn_b1': 4.728, 'L0_gnn_b2': 4.367}
    for name, (base, spread) in spreads.items():
        noise = np.random.default_rng([zlib.crc32(name.encode()), seed]).standard_normal(out[name].shape)
        drawn = base * np.exp(spread * noise) if base else spread * noise
        out[name] = jnp.asarray(drawn.astype(out[name].dtype))
    for name, factor in factors.items():
        out[name] = (out[name] * factor).astype(out[name].dtype)
    return out
```

```python
from contextlib import ExitStack

import concourse.bass as bass
from concourse import mybir

ALU = mybir.AluOpType
ACT = mybir.ActivationFunctionType
AX = mybir.AxisListType
F32 = mybir.dt.float32
F16 = mybir.dt.float16
BF16 = mybir.dt.bfloat16
I32 = mybir.dt.int32
U32 = mybir.dt.uint32
U16 = mybir.dt.uint16
ds = bass.ds

P = 128
N, D = 6250, 256
NB = -(-N // P)
LASTROWS = N - (NB - 1) * P
LD = 4
E = 100000
EP = 125
EC = E // EP
HEADS, HC = 8, 32
NX, F = 8, 1024
FT = F // P
CAP = 977
TM, TQ = 123, 4
HALF = TM * TQ
CAPR = 2 * HALF
PARTS = 2048.0
QR = 4
GR = 16
SR = 4
KR = 8
CW = 4
CU = 16
AGW = D + 1
LN_EPS, HEAD_EPS = 1e-5, 1e-5


def chunk_plan():
    plan, c0, t0 = [], 0, 0
    for cols in (128, 304, 368):
        tiles = (cols * EP + NB * (P - 1)) // P
        tiles = -(-tiles // GR) * GR
        plan.append((c0, cols, t0, tiles))
        c0 += cols
        t0 += tiles
    assert c0 == EC
    return plan


CHUNKS = chunk_plan()
TILES = sum(c[3] for c in CHUNKS)
WMAX = max(c[1] for c in CHUNKS)
TMAX = max(c[3] for c in CHUNKS)
B7 = 7
NQ = 7
assert NB % NQ == 0 and NB // NQ % 2 == 1 and CAPR >= CAP and EP * EC == E and TMAX <= 512 and NB % B7 == 0


def phases():
    out = []
    for c, (_, cols, _, _) in enumerate(CHUNKS):
        left = CHUNKS[c - 1][3] // GR if c else 0
        sorts = cols // CU
        out += [(c, "count", NB // B7, 0, False), (c, "place", 1, 0, False)]
        if left:
            out += [(c, "rank", NB // B7, 1, True), (c, "split", 1, 0, False)]
            left -= NB // B7
            out += [(c, "sort", left - 1, 1, True), (c, "sort", 1, 1, False),
                    (c, "sort", sorts - left, 0, False)]
        else:
            out += [(c, "rank", NB // B7, 0, False), (c, "split", 1, 0, False),
                    (c, "sort", sorts, 0, False)]
        out += [(c, "decode", 1, 0, False)]
    last, left = len(CHUNKS), CHUNKS[-1][3] // GR
    out += [(last, "heads", NB // LD, 1, True), (last, "tail", 1, 1, True), (last, "kv", 1, 0, False)]
    left -= NB // LD + 1
    assert left == NB // LD + 1
    return out + [(last, "own", left - 1, 1, True), (last, "own", 1, 1, False)]


PHASES = phases()


class Tally:

    def __init__(self, sem):
        self.sem, self.base, self.i, self.k, self.j = sem, 0, 0, 0, 0

    def loop(self, i, k):
        self.base, self.i, self.k, self.j = self.base + self.j, i, k, 0

    def end(self, n):
        assert self.j == self.k, (self.sem, self.j, self.k)
        self.base, self.i, self.k, self.j = self.base + n * self.k, 0, 0, 0

    def add(self, ins):
        ins.then_inc(self.sem, 1)
        self.j += 1

    def value(self, back=0):
        return self.i * self.k + (self.base + self.j - back)


def repeat(eng, n, body, first=0):
    if n == 1:
        body(first)
    elif n > 1:
        with eng.Fori(0, n) as i:
            body(i + first if first else i)


def build_program(nc, x, src, dst, w1t, w2t, gb1, gb2, kw, kb, vw, vb, gate_w, gate_b, f1, fb1, f2, fb2, out):
    dram = {
        "tab": nc.dram_tensor("xn_parts", (NB * P, 2 * D), F16, kind="Internal").ap(),
        "buf": nc.dram_tensor("expert_rows", (NX * CAPR + NB * P, D), F32, kind="Internal").ap(),
        "ybuf": nc.dram_tensor("expert_out", (NX * CAPR + P, D), F32, kind="Internal").ap(),
    }
    with ExitStack() as ctx:
        def sb(name, shape, dt):
            return ctx.enter_context(nc.sbuf_tensor(name, shape, dt))

        k = {
            "X": sb("X", [P, NB * D], F32),
            "AGG": sb("AGG", [P, NB * AGW], F32),
            "ident": sb("ident", [P, P], F32),
            "upper": sb("upper", [P, P], F32),
            "upinc": sb("upinc", [P, P], F32),
            "ones": sb("ones", [P, P], F32),
            "eps": sb("eps", [P, 1], F32),
            "W1": sb("W1", [P, 2 * D], F32),
            "W2": sb("W2", [P, 2 * D], F32),
            "brow": sb("brow", [P, D], F32),
            "gw": sb("gw", [P, 2 * NX], F32),
            "gb": sb("gb", [P, NX], F32),
            "iota8": sb("iota8", [P, NX], F32),
            "dummy": sb("spare_rows", [P, NB], F32),
            "psum": [ctx.enter_context(nc.psum_tensor(f"bank{i}", [P, 512], F32)) for i in range(8)],
            "zst": ctx.enter_context(nc.semaphore("expert_rows_zeroed")),
        }
        with ExitStack() as c:
            edges(nc, c, k, dram, x, src, dst, w1t, w2t, gb1, gb2, kw, kb, vw, vb, gate_w, gate_b)
        with ExitStack() as c2:
            k["gidx"] = c2.enter_context(nc.sbuf_tensor("gidx", [P, NB], I32))
            k["kp"] = c2.enter_context(nc.sbuf_tensor("kp", [P, NB], F32))
            with ExitStack() as c:
                nodes(nc, c, k, dram, x)
            with ExitStack() as c:
                experts(nc, c, k, dram, f1, fb1, f2, fb2)
            with ExitStack() as c:
                outputs(nc, c, k, dram, out)


def edges(nc, ctx, kk, dram, x, src, dst, w1t, w2t, gb1, gb2, kw, kb, vw, vb, gate_w, gate_b):
    def sb(name, shape, dt):
        return ctx.enter_context(nc.sbuf_tensor(name, shape, dt))

    def sem(name):
        return ctx.enter_context(nc.semaphore(name))

    tab, buf, ybuf = dram["tab"], dram["buf"], dram["ybuf"]
    X, AGG, ident, upper, upinc, ones, eps = (kk[n] for n in ("X", "AGG", "ident", "upper", "upinc", "ones", "eps"))
    W1, W2, brow, gw, gb = (kk[n] for n in ("W1", "W2", "brow", "gw", "gb"))
    bank = kk["psum"]
    psA, psV, psP, psG, psQ = bank[0:2], bank[2:4], bank[4], bank[5:7], bank[7]
    zst = kk["zst"]

    G = sb("G", [P, GR * 2 * D], F16)
    ones16 = sb("ones16", [P, 2], F16)
    zero16 = sb("zero16", [P, P], F16)
    zero32 = sb("zero32", [P, P], F32)
    iota_i = sb("iota_i", [P, TMAX], I32)
    iota_t = sb("iota_t", [P, TMAX], F16)
    iota_1 = sb("iota_1", [P, P], F16)
    iota_b = sb("iota_b", [P, NB], F32)
    lnst = sb("lnst", [P, 2 * LD * 6], F32)
    lnmv = sb("lnmv", [P, 2 * LD * 2], F32)
    lnsd = sb("lnsd", [P, 2 * LD], F32)
    lnrs = sb("lnrs", [P, 2 * LD], F32)
    TB = G[:, 0:2 * LD * 2 * D]
    mask = sb("mask", [P, 2 * WMAX], BF16)
    work = sb("work", [P, 8 * EC], BF16)
    srci = work[:, 0:2 * EC].bitcast(I32)
    dsti = work[:, 2 * EC:4 * EC].bitcast(I32)
    tmpi = work[:, 4 * EC:6 * EC].bitcast(I32)
    tmpj = work[:, 6 * EC:8 * EC].bitcast(I32)
    cen = work[:, 0:2 * LD * D].bitcast(F32)
    sqr = work[:, 2 * LD * D:4 * LD * D].bitcast(F32)
    KW = P + 1
    xs, xts = cen[:, 0:2 * D], cen[:, 2 * D:4 * D]
    kn = work[:, 4 * LD * D:4 * LD * D + 2 * LD * 2 * KW].bitcast(F32)
    blk = sb("blk", [P, EC], BF16)
    v1 = sb("v1", [P, EC], F32)
    v2 = sb("v2", [P, EC], F32)
    onesw = sb("onesw", [P, WMAX], BF16)
    cum = sb("cum", [P, 2 * WMAX], F32)
    pos = sb("pos", [P, WMAX], F32)
    tf = sb("tf", [P, WMAX], F32)
    posi = cum[:, 0:WMAX].bitcast(I32)
    tli = cum[:, WMAX:2 * WMAX].bitcast(I32)
    cnt = sb("cnt", [P, NB], F32)
    mi = sb("mi", [P, 2 * NB], I32)
    mrow = sb("mrow", [P, NB], F32)
    mend = sb("mend", [P, NB], F32)
    base = sb("base", [P, NB], F32)
    mcol = sb("mcol", [P, 4], F32)
    mcoli = sb("mcoli", [P, 4], I32)
    ge = sb("ge", [P, TMAX], F16)
    LH = sb("LH", [P, KR * P], F16)
    LV = sb("LV", [P, KR * 2 * P], F16)
    HT = sb("HT", [P, KR * TMAX], F16)
    DI = sb("DI", [P, 4 * TMAX], I32)
    idx = sb("idx", [P, TILES], I32)
    srcl = sb("srcl", [P, TILES], F32)
    buck = sb("buck", [1, TILES], I32)
    idxr = sb("idxr", [P, GR], I32)
    S = sb("S", [P, SR * P], F16)
    here = sb("here", [P, 4 * GR], F32)
    srch, posh, tfh, v1h = (here[:, n * GR:(n + 1) * GR] for n in range(4))
    hv = sb("hv", [P, 2 * 2], F32)
    hrow = sb("hrow", [P, 2 * D], F32)
    b2r = sb("b2r", [P, D], F32)
    hs = sb("hs", [P, LD * HEADS], F32)
    hm = sb("hm", [P, LD * HEADS], F32)
    hq = sb("hq", [P, LD * HEADS], F32)
    hr = sb("hr", [P, LD * HEADS], F32)
    kvw = sb("kvw", [P, 6 * P], F32)

    s_par, s_edge, s_x, s_xl = sem("parameters_loaded"), sem("edges_loaded"), sem("x_loaded"), sem("x_last_loaded")
    s_pc, s_dc = sem("pool_constants"), sem("vector_constants")
    s_v = sem("vector_steps")
    s_pad = sem("x_padding_zero")
    s_stat, s_sd, s_xn, s_hi, s_lo = sem("ln_statistics"), sem("ln_std"), sem("xn_ready"), sem("high_part"), sem("low_part")
    s_tb = [sem("parts_stored_0"), sem("parts_stored_1")]
    s_tbc = sem("parts_read")
    s_cnt, s_pre, s_mc, s_ec, s_ge, s_bk = (sem(n) for n in (
        "bucket_counts", "bucket_prefix", "tile_counts", "tile_ends", "tiles_past_ends", "tile_buckets"))
    s_lh, s_lv, s_ht, s_col, s_sx, s_dec = (sem(n) for n in (
        "lane_onehot", "lane_values", "tile_onehot", "columns_sorted", "sort_closed", "sort_read"))
    s_idx = sem("indices_ready")
    s_srch, s_posh = sem("sources_at_hand"), sem("places_at_hand")
    s_g = [sem(f"gathered_{i}") for i in range(GR)]
    s_S, s_tile, s_ev = sem("source_onehot"), sem("tile_summed"), sem("tile_added")
    s_cen, s_sq, s_ss, s_hstd, s_kn, s_kg = (sem(n) for n in (
        "heads_centred", "heads_squared", "heads_variance", "heads_std", "heads_normal", "heads_multiplied"))
    s_zero = sem("sums_zero")
    s_kv = sem("key_values_in_w1")
    s_xs, s_xt, s_xtc, s_xp, s_xa = (sem(n) for n in (
        "xn_placed", "xn_transposed", "xn_t_copied", "xn_products", "xn_products_added"))
    s_dg, s_se = sem("heads_sums_diagonal"), sem("heads_sums_row")
    s_past = sem("past_a_wait")

    block = ctx.enter_context(nc.Block())
    PAR = 16 * 16

    @block.sync
    def _(sp):
        sp.dma_start(srci[0:EP, :], src.rearrange("(p t) -> p t", p=EP)).then_inc(s_edge, 16)
        sp.dma_start(dsti[0:EP, :], dst.rearrange("(p t) -> p t", p=EP)).then_inc(s_edge, 16)
        sp.wait_ge(s_pad, 1)
        sp.dma_start(X[0:LASTROWS, (NB - 1) * D:NB * D], x[(NB - 1) * P:N, :]).then_inc(s_xl, 16)

        sp.sem_inc(s_x, 16)
        with sp.Fori(0, NB // (2 * LD)) as i:
            sp.wait_ge(s_x, i * 16 + 16)
            sp.dma_start(X[:, ds(i * (2 * LD * D), 2 * LD * D)].rearrange("p (j d) -> p j d", d=D),
                         x[ds(i * (2 * LD * P), 2 * LD * P), :].rearrange("(j p) d -> p j d", p=P)).then_inc(s_x, 16)
        sp.wait_ge(s_zero, 1)
        half = 31 * P
        for j in range(2):
            sp.dma_start(buf[j * half:(j + 1) * half, :].rearrange("(p r) d -> p (r d)", p=P),
                         AGG[:, 0:31 * D]).then_inc(zst, 16)
        sp.dma_start(ybuf[NX * CAPR:NX * CAPR + P, :], AGG[:, 0:D]).then_inc(zst, 16)
        sp.wait_ge(zst, 48)

    @block.gpsimd
    def _(pool):
        pool.iota(iota_i[:, :], [[1, TMAX]], base=0, channel_multiplier=0).then_inc(s_pc, 1)
        pool.memset(ones[:, :], 1.0).then_inc(s_pc, 1)
        pool.memset(ident[:, :], 0.0).then_inc(s_pc, 1)
        pool.wait_ge(s_pc, 3)
        pool.affine_select(out=ident[:, :], in_=ident[:, :], compare_op=ALU.not_equal, fill=1.0, base=0,
                           pattern=[[-1, P]], channel_multiplier=1).then_inc(s_pc, 1)
        pool.affine_select(out=upper[:, :], in_=ones[:, :], compare_op=ALU.is_gt, fill=0.0, base=0,
                           pattern=[[1, P]], channel_multiplier=-1).then_inc(s_pc, 1)
        pool.affine_select(out=upinc[:, :], in_=ones[:, :], compare_op=ALU.is_ge, fill=0.0, base=0,
                           pattern=[[1, P]], channel_multiplier=-1).then_inc(s_pc, 1)
        pool.iota(mi[:, 0:NB], [[P, NB]], base=NX * CAPR, channel_multiplier=1).then_inc(s_pc, 1)

        def store(h, nb, rows, low):
            pool.wait_ge(s_lo, low)
            o = h * LD * 2 * D
            pool.dma_start(tab[rows, :].rearrange("(j p) d -> p j d", p=P),
                           TB[:, o:o + nb * 2 * D].rearrange("p (j d) -> p j d", j=nb)).then_inc(s_tb[h], 16)

        with pool.Fori(0, NB // (2 * LD)) as i:
            for h in range(2):
                store(h, LD, ds((i * 2 + h) * (LD * P), LD * P), i * 2 + (h + 1))
        n = NB // (2 * LD)
        store(0, 1, slice((NB - 1) * P, NB * P), 2 * n + 1)
        pool.wait_ge(s_tb[0], 16 * (n + 1))
        pool.wait_ge(s_tb[1], 16 * n)

        g0 = 0
        for c, step, its, groups, _ in PHASES:
            if not groups:
                continue

            def gather(i, g0=g0):
                for s in range(GR):
                    if s % QR == 0:
                        pool.wait_ge(s_idx, i * (GR // QR) + (GR // QR * g0 + s // QR + 1))
                        pool.wait_ge(s_tile, i * GR + (GR * g0 + s + QR))
                        pool.sem_inc(s_past, 1)
                    pool.indirect_dma_start(G[:, s * 2 * D:(s + 1) * 2 * D], None, tab,
                                            bass.IndirectOffsetOnAxis(ap=idxr[:, s:s + 1], axis=0)).then_inc(s_g[s], 16)
            repeat(pool, its, gather)
            g0 += its

    @block.scalar
    def _(act):
        for a, b in ((W1, w1t), (W2, w2t)):
            act.dma_start(a[:, :].rearrange("p (k o) -> p k o", k=2), b.rearrange("(k p) o -> p k o", p=P)).then_inc(s_par, 16)
        act.dma_start(brow[:, :], gb1.rearrange("(a n) -> a n", a=1).partition_broadcast(P)).then_inc(s_par, 16)
        act.dma_start(b2r[:, :], gb2.rearrange("(a n) -> a n", a=1).partition_broadcast(P)).then_inc(s_par, 16)
        act.dma_start(gw[:, :].rearrange("p (k o) -> p k o", k=2), gate_w.rearrange("(k p) o -> p k o", p=P)).then_inc(s_par, 16)
        act.dma_start(gb[:, :], gate_b.rearrange("(a n) -> a n", a=1).partition_broadcast(P)).then_inc(s_par, 16)
        for n, col in enumerate((kw, kb)):
            flat = col.rearrange("h a c -> (h a c)").rearrange("(k p a) -> k p a", k=2, a=1)
            for h in range(2):
                act.dma_start(hv[:, 2 * h + n:2 * h + n + 1], flat[h]).then_inc(s_par, 16)
        for n, row in enumerate((vw, vb)):
            act.dma_start(hrow[:, n * D:(n + 1) * D],
                          row.rearrange("h a c -> a (h c)").partition_broadcast(P)).then_inc(s_par, 16)
        act.wait_ge(s_dc, 1)

        def norm(h, nb, at, k):
            act.wait_ge(s_stat, k)
            act.activation(lnsd[:, h * LD:h * LD + nb], lnmv[:, 2 * h * LD + 1:2 * (h * LD + nb):2], ACT.Sqrt,
                           bias=eps[:, :]).then_inc(s_sd, 1)

        def high(h, nb, at, k, last):
            act.wait_ge(s_xn, k)
            act.wait_ge(s_tb[h], last)
            o = h * LD * 2 * D
            act.activation(TB[:, o:o + nb * 2 * D].rearrange("p (j d) -> p j d", j=nb)[:, :, 0:D],
                           X[:, at].rearrange("p (j d) -> p j d", j=nb), ACT.Copy, scale=PARTS).then_inc(s_hi, 1)

        n = NB // (2 * LD)
        norm(0, LD, None, 1)
        norm(1, LD, None, 2)
        act.wait_ge(s_xn, 1)
        for h in range(2):
            act.wait_ge(s_xn, h + 1)
            o = h * LD * 2 * D
            act.activation(TB[:, o:o + LD * 2 * D].rearrange("p (j d) -> p j d", j=LD)[:, :, 0:D],
                           X[:, h * LD * D:(h + 1) * LD * D].rearrange("p (j d) -> p j d", j=LD), ACT.Copy,
                           scale=PARTS).then_inc(s_hi, 1)
        with act.Fori(1, n) as i:
            for h in range(2):
                norm(h, LD, None, i * 2 + (h + 1))
            for h in range(2):
                high(h, LD, ds((i * 2 + h) * (LD * D), LD * D), i * 2 + (h + 1), i * 16)
        norm(0, 1, None, 2 * n + 1)
        high(0, 1, slice((NB - 1) * D, NB * D), 2 * n + 1, 16 * n)

        t = Tally(s_col)
        k0, b0 = 0, 0
        for c, step, its, groups, _ in PHASES:
            if step == "sort":
                c0 = CHUNKS[c][0]

                def values(i, k0=k0, groups=groups):
                    for j in range(CU):
                        q = j % KR
                        col = i * CU + (k0 + j)
                        if j % CW == 0:
                            act.wait_ge(s_lh, col + CW)
                        for n, v in enumerate((v1, v2)):
                            if n == 0 and not groups and j % 2:
                                continue
                            ins = act.activation(LV[0:EP, (2 * q + n) * P:(2 * q + n + 1) * P], LH[0:EP, q * P:(q + 1) * P],
                                                 ACT.Copy, scale=v[0:EP, ds(col, 1)])
                        ins.then_inc(s_lv, 1)
                repeat(act, its, values)
                k0 += its * CU
            elif step in ("heads", "tail"):
                m0 = 0 if step == "heads" else NB // LD
                nb = LD if step == "heads" else 1

                def heads(i, m0=m0, nb=nb):
                    act.wait_ge(s_cen, i + (m0 + 1))
                    act.activation(sqr[:, 0:nb * D], cen[:, 0:nb * D], ACT.Square).then_inc(s_sq, 1)
                    act.wait_ge(s_ss, i + (m0 + 1))
                    act.activation(hq[:, 0:nb * HEADS], hq[:, 0:nb * HEADS], ACT.Sqrt, scale=1.0 / (HC - 1)).then_inc(s_hstd, 1)
                repeat(act, its, heads)
            elif step == "kv":
                act.wait_ge(s_kv, 1)
            elif step == "own":
                def own(i, b0=b0, nb=LD if its > 1 else 1):
                    for j in range(nb):
                        h, b = j % 2, i * LD + (b0 + j)
                        act.wait_ge(s_xt, b + 1)
                        act.activation(xs[:, h * D:(h + 1) * D], X[:, ds(b * D, D)], ACT.Copy).then_inc(s_xs, 1)
                        act.wait_ge(s_xt, b + 3)
                        act.wait_ge(s_xp, b + 1)
                        act.activation(xts[:, h * D:(h + 1) * D], psV[h][:, 0:D], ACT.Copy).then_inc(s_xtc, 1)
                repeat(act, its, own)
                b0 += its * LD

    @block.tensor
    def _(pe):
        pe.wait_ge(s_pc, 7)
        pe.wait_ge(s_dc, 2)
        pe.sem_inc(s_col, KR)
        pe.sem_inc(s_tile, GR)
        pe.sem_inc(s_kg, 1)
        pe.sem_inc(s_xt, 2)
        pe.sem_inc(s_xp, 2)
        t0, k0, m0, b0 = 0, 0, 0, 0
        for c, step, its, groups, _ in PHASES:
            if step == "place":
                _, cols, ch0, tiles = CHUNKS[c]
                pe.wait_ge(s_cnt, c + 1)
                pe.matmul(psP[:, 0:NB], upper[0:EP, :], cnt[0:EP, :], start=True, stop=True)
                pe.matmul(psP[:, 64:64 + NB], ones[0:EP, :], cnt[0:EP, :], start=True, stop=True)
                pe.matmul(psQ[0:NB, 0:1], cnt[0:EP, :], ones[0:EP, 0:1], start=True, stop=True).then_inc(s_pre, 1)
                pe.wait_ge(s_mc, c + 1)
                pe.matmul(psQ[0:NB, 0:1], upinc[0:NB, 0:NB], mcol[0:NB, 0:1], start=True, stop=True).then_inc(s_ec, 1)
                pe.wait_ge(s_ge, c + 1)
                pe.matmul(psQ[0:1, 0:tiles], ones16[0:NB, 0:1], ge[0:NB, 0:tiles], start=True, stop=True).then_inc(s_bk, 1)
                if c:
                    pe.wait_ge(s_dec, c)
                for n in range(2):
                    pe.matmul(psV[n][:, 0:tiles], zero16[0:EP, :], iota_t[0:EP, 0:tiles], start=True, stop=False,
                              skip_group_check=True)

            def tiles_of(i, s, t0=t0):
                t = i * GR + (t0 + s)
                q = s % SR
                pe.wait_ge(s_g[s], (i + (t0 // GR + 1)) * 16)
                pe.wait_ge(s_S, t + 1)
                pe.wait_ge(s_ev, t + 1)
                lhs = S[:, q * P:(q + 1) * P]
                o = s * 2 * D
                pe.matmul(psA[s % 2][:, 0:D], lhs, G[:, o:o + D], start=True, stop=False)
                pe.matmul(psA[s % 2][:, 0:D], lhs, G[:, o + D:o + 2 * D], start=False, stop=True)
                pe.matmul(psA[s % 2][:, D:D + 1], lhs, ones16[:, 0:1], start=True, stop=True).then_inc(s_tile, 1)

            def column(i, j, k0=k0, tiles=CHUNKS[min(c, len(CHUNKS) - 1)][3]):
                q = j % KR
                col = i * CU + (k0 + j)
                if j % CW == 0:
                    pe.wait_ge(s_lv, col + CW)
                    pe.wait_ge(s_ht, col + (CW + GR))
                for n in range(2):
                    ins = pe.matmul(psV[n][:, 0:tiles], LV[0:EP, (2 * q + n) * P:(2 * q + n + 1) * P],
                                    HT[0:EP, q * TMAX:q * TMAX + tiles], start=False, stop=False, skip_group_check=True)
                ins.then_inc(s_col, 1)

            def products(pieces):
                for piece in pieces:
                    for j, h in ((piece // 2, piece % 2),):
                        o = (j * 2 + h) * KW
                        ins = pe.matmul(psG[h][:, 0:KW], kn[:, o:o + P], kn[:, o:o + KW], start=False, stop=False,
                                        skip_group_check=True)
                return ins

            if step == "heads":
                pe.wait_ge(s_par, 16 * 12)
                for h in range(2):
                    pe.matmul(psG[h][:, 0:KW], zero32[:, :], W1[:, 0:KW], start=True, stop=False,
                              skip_group_check=True)

            def own(i, s, b0=b0):
                h, b = s // 4 % 2, i * LD + (b0 + s // 4)
                if s % 4 == 0:
                    pe.wait_ge(s_xs, b + 1)
                    pe.wait_ge(s_xtc, b + 1)
                    for n in range(2):
                        ins = pe.transpose(psV[h][:, n * P:(n + 1) * P], xs[:, h * D + n * P:h * D + (n + 1) * P], ident[:, :])
                    ins.then_inc(s_xt, 1)
                elif s % 4 == 2:
                    pe.wait_ge(s_xtc, b + 3)
                    pe.wait_ge(s_xa, b + 1)
                    for n in range(2):
                        ins = pe.matmul(psG[h][:, 0:D], xts[:, h * D + n * P:h * D + (n + 1) * P],
                                        W1[:, n * D:(n + 1) * D], start=(n == 0), stop=(n == 1))
                    ins.then_inc(s_xp, 1)

            def body(i, step=step, groups=groups, its=its):
                for s in range(GR if groups or step == "sort" else 0):
                    if groups:
                        tiles_of(i, s)
                    if step == "own" and s < 4 * (LD if its > 1 else 1):
                        own(i, s)
                    if step == "sort":
                        column(i, s)
                    if step in ("heads", "tail") and s >= 10:
                        pieces = (1 if step == "tail" else LD) * 2
                        per = -(-pieces // 6)
                        if s == 10:
                            pe.wait_ge(s_kn, i + (m0 + 1))
                        mine = range(min((s - 10) * per, pieces), min((s - 9) * per, pieces))
                        if mine:
                            ins = products(mine)
                            if mine[-1] == pieces - 1:
                                ins.then_inc(s_kg, 1)

            if step == "kv":
                for h in range(2):
                    ins = pe.matmul(psG[h][:, 0:KW], zero32[:, :], W1[:, 0:KW], start=False, stop=True,
                                    skip_group_check=True)
                ins.then_inc(s_kg, 1)
                for h in range(2):
                    pe.wait_ge(s_dg, h + 1)
                    pe.matmul(psP[:, h * P:(h + 1) * P], ones[:, :], kvw[:, (4 + h) * P:(5 + h) * P], start=True,
                              stop=True).then_inc(s_se, 1)
                pe.wait_ge(s_kv, 1)
            if groups or step == "sort":
                repeat(pe, its, body)
                b0 += its * LD if step == "own" else 0
                t0 += its * GR * groups
                k0 += its * CU if step == "sort" else 0
                m0 += its if step in ("heads", "tail") else 0
            if step == "decode":
                for n in range(2):
                    ins = pe.matmul(psV[n][:, 0:CHUNKS[c][3]], zero16[0:EP, :], iota_t[0:EP, 0:CHUNKS[c][3]],
                                    start=False, stop=True, skip_group_check=True)
                ins.then_inc(s_sx, 1)

    @block.vector
    def _(v):
        step_count = Tally(s_v)
        step = step_count.add

        def wait(back=0):
            v.wait_ge(s_v, step_count.value(back))

        v.memset(eps[:, :], LN_EPS).then_inc(s_dc, 1)
        v.memset(X[:, (NB - 1) * D:NB * D], 0.0).then_inc(s_pad, 1)
        v.memset(zero16[:, :], 0.0)
        v.memset(zero32[:, :], 0.0)
        v.memset(ones16[:, :], 1.0)
        v.memset(onesw[:, :], 1.0)
        v.memset(pos[:, :], 0.0)
        v.wait_ge(s_pc, 7)
        v.tensor_copy(iota_t[:, :], iota_i[:, :])
        v.tensor_scalar(iota_1[:, :], iota_i[:, 0:P], 1.0, None, ALU.add)
        v.tensor_copy(iota_b[:, :], iota_i[:, 0:NB])
        v.tensor_copy(kk["dummy"][:, :], mi[:, 0:NB])
        v.tensor_scalar(kk["iota8"][:, :], iota_i[:, 0:NX], -1.0, float(NX), ALU.mult, ALU.add)
        v.memset(LH[:, :], 0.0).then_inc(s_dc, 1)
        v.memset(AGG[:, :], 0.0).then_inc(s_zero, 1)
        v.sem_inc(s_ht, GR)
        v.sem_inc(s_ev, 2)

        def stats(h, nb, at):
            for j in range(nb):
                q = h * LD + j
                step(v.bn_stats(lnst[:, 6 * q:6 * q + 6], X[:, at(j)]))
            wait()
            v.sem_inc(s_past, 1)
            for j in range(nb):
                q = h * LD + j
                ins = v.bn_aggr(lnmv[:, 2 * q:2 * q + 2], lnst[:, 6 * q:6 * q + 6])
            ins.then_inc(s_stat, 1)

        def normal(h, nb, at, k):
            v.wait_ge(s_sd, k)
            step(v.reciprocal(lnrs[:, h * LD:h * LD + nb], lnsd[:, h * LD:h * LD + nb]))
            wait()
            for j in range(nb):
                q = h * LD + j
                ins = v.tensor_scalar(X[:, at(j)], X[:, at(j)], lnmv[:, 2 * q:2 * q + 1], lnrs[:, q:q + 1],
                                      ALU.subtract, ALU.mult)
            ins.then_inc(s_xn, 1)

        def low(h, nb, at, k):
            v.wait_ge(s_xn, k)
            v.wait_ge(s_hi, k)
            o = h * LD * 2 * D
            tb = TB[:, o:o + nb * 2 * D].rearrange("p (j d) -> p j d", j=nb)
            v.scalar_tensor_tensor(out=tb[:, :, D:2 * D], in0=X[:, at].rearrange("p (j d) -> p j d", j=nb),
                                   scalar=PARTS, in1=tb[:, :, 0:D], op0=ALU.mult, op1=ALU.subtract).then_inc(s_lo, 1)

        n = NB // (2 * LD)

        with v.Fori(0, n) as i:
            step_count.loop(i, 2 * LD + 2)
            v.wait_ge(s_x, i * 16 + 32)
            for h in range(2):
                stats(h, LD, lambda j: ds(i * (2 * LD * D) + (h * LD + j) * D, D))
            for h in range(2):
                normal(h, LD, lambda j: ds(i * (2 * LD * D) + (h * LD + j) * D, D), i * 2 + (h + 1))
            for h in range(2):
                low(h, LD, ds(i * (2 * LD * D) + h * LD * D, LD * D), i * 2 + (h + 1))
        step_count.end(n)
        v.wait_ge(s_xl, 16)
        stats(0, 1, lambda j: slice((NB - 1) * D, NB * D))
        normal(0, 1, lambda j: slice((NB - 1) * D, NB * D), 2 * n + 1)
        low(0, 1, slice((NB - 1) * D, NB * D), 2 * n + 1)

        v.wait_ge(s_edge, 32)
        step(v.tensor_scalar(tmpi[0:EP, :], srci[0:EP, :], 7, None, ALU.logical_shift_right))
        step(v.tensor_scalar(tmpj[0:EP, :], dsti[0:EP, :], 3, None, ALU.logical_shift_right))
        wait()
        v.tensor_copy(blk[0:EP, :], tmpi[0:EP, :])
        step(v.tensor_copy(v1[0:EP, :], tmpj[0:EP, :]))
        wait()
        v.tensor_scalar(tmpi[0:EP, :], srci[0:EP, :], P - 1, None, ALU.bitwise_and)
        step(v.tensor_scalar(tmpj[0:EP, :], dsti[0:EP, :], 7, None, ALU.bitwise_and))
        wait()
        step(v.tensor_scalar(v2[0:EP, :], tmpj[0:EP, :], 256.0, 1.0, ALU.mult, ALU.add))
        wait()
        step(v.tensor_tensor(v2[0:EP, :], v2[0:EP, :], tmpi[0:EP, :], ALU.add))
        wait()

        def source_onehot(i, s, t0):
            q = s % SR
            v.tensor_scalar(S[:, q * P:(q + 1) * P], iota_1[:, :], srch[:, s:s + 1], None, ALU.is_equal).then_inc(s_S, 1)

        offsets = []

        def add_tile(i, s, t0):
            t = i * GR + (t0 + s)
            v.wait_ge(s_tile, t + (GR + 1))
            v.wait_ge(s_ev, t + 2)
            o = offsets[s]
            v.tensor_tensor(AGG[:, ds(o, AGW)], AGG[:, ds(o, AGW)], psA[s % 2][:, 0:AGW], ALU.add).then_inc(s_ev, 1)

        def fetch(i, k, g0):
            v.tensor_copy(idxr[:, QR * k:QR * k + QR], idx[:, ds(i * GR + (g0 * GR + QR * k), QR)]).then_inc(s_idx, 1)

        def tile(i, s, t0, ahead):
            if s == 0:
                offsets[:] = nc.values_load_multi_w_load_instructions(
                    buck[0:1, ds(i * GR + t0, GR)], engines=[mybir.EngineType.DVE], min_val=0, max_val=(NB - 1) * AGW,
                    skip_runtime_bounds_check_because="the place step clamps the tiles' blocks to NB - 1")[1]
                v.tensor_copy(srch, srcl[:, ds(i * GR + t0, GR)]).then_inc(s_srch, 1)
                v.wait_ge(s_srch, i + (t0 // GR + 1))
                source_onehot(i, 0, t0)
                source_onehot(i, 1, t0)
            if s + 2 < GR:
                source_onehot(i, s + 2, t0)
            add_tile(i, s, t0)
            if ahead and s % QR == QR - 1:
                fetch(i, s // QR, t0 // GR + 1)

        v.sem_inc(s_xtc, 2)
        v.sem_inc(s_xa, 2)
        t0, k0, m0, b0 = 0, 0, 0, 0
        v.memset(kn[:, P:LD * 2 * KW:KW], 1.0)
        v.wait_ge(zst, 48)
        for c, name, its, groups, ahead in PHASES:
            if c < len(CHUNKS):
                c0, cols, ch0, tiles = CHUNKS[c]
            if name == "count":
                def count(i):
                    for j in range(B7):
                        o = j % KR * TMAX
                        wait(2)
                        step(v.tensor_scalar(HT[0:EP, o:o + cols], blk[0:EP, c0:c0 + cols],
                                              iota_b[0:EP, ds(i * B7 + j, 1)], 0.0, ALU.is_equal, ALU.add,
                                              accum_out=cnt[0:EP, ds(i * B7 + j, 1)]))
                with v.Fori(0, its) as i:
                    step_count.loop(i, B7)
                    count(i)
                step_count.end(its)
                v.wait_ge(s_v, step_count.value())
                step(v.memset(mcol[:, :], 0.0))
                wait()
                v.memset(mcoli[:, :], 0).then_inc(s_cnt, 1)
            elif name == "place":
                v.wait_ge(s_pre, c + 1)
                v.tensor_scalar(mi[:, 0:NB], psP[:, 64:64 + NB], float(P - 1), None, ALU.add)
                step(v.tensor_scalar(mcoli[0:NB, 0:1], psQ[0:NB, 0:1], float(P - 1), None, ALU.add))
                wait()
                v.tensor_scalar(mi[:, NB:2 * NB], mi[:, 0:NB], 7, None, ALU.logical_shift_right)
                step(v.tensor_scalar(mcoli[0:NB, 1:2], mcoli[0:NB, 0:1], 7, None, ALU.logical_shift_right))
                wait()
                step(v.tensor_copy(mrow[:, :], mi[:, NB:2 * NB]))
                v.tensor_copy(mcol[0:NB, 0:1], mcoli[0:NB, 1:2]).then_inc(s_mc, 1)
                wait()
                step(v.tensor_tensor_scan(mend[:, :], ones[:, 0:NB], mrow[:, :], 0.0, ALU.mult, ALU.add))
                wait()
                step(v.tensor_tensor(mrow[:, :], mend[:, :], mrow[:, :], ALU.subtract))
                wait()
                step(v.scalar_tensor_tensor(out=base[0:EP, :], in0=mrow[0:EP, :], scalar=float(P), in1=psP[0:EP, 0:NB],
                                            op0=ALU.mult, op1=ALU.add))
                wait()
                step(v.tensor_scalar(base[0:EP, :], base[0:EP, :], -1.0, None, ALU.add))
                v.wait_ge(s_ec, c + 1)
                step(v.tensor_copy(mcol[0:NB, 2:3], psQ[0:NB, 0:1]))
                wait()
                v.tensor_scalar(ge[0:NB, 0:tiles], iota_t[0:NB, 0:tiles], mcol[0:NB, 2:3], None, ALU.is_ge).then_inc(s_ge, 1)
                v.wait_ge(s_bk, c + 1)
                step(v.tensor_scalar(buck[0:1, ch0:ch0 + tiles], psQ[0:1, 0:tiles], float(NB - 1), float(AGW),
                                     ALU.min, ALU.mult))
                wait()
            elif name == "rank":
                def rank(i, groups=groups, ahead=ahead, t0=t0):
                    first = step_count.j
                    for j in range(B7 + 1):
                        if j < B7:
                            q = j % 2
                            m = mask[0:EP, q * WMAX:q * WMAX + cols]
                            wait()
                            step(v.tensor_scalar(m, blk[0:EP, c0:c0 + cols], iota_b[0:EP, ds(i * B7 + j, 1)], None,
                                                 ALU.is_equal))
                            wait()
                            step(v.tensor_tensor_scan(cum[0:EP, q * WMAX:q * WMAX + cols], onesw[0:EP, 0:cols], m,
                                                      base[0:EP, ds(i * B7 + j, 1)], ALU.mult, ALU.add))
                        if groups:
                            for s in range(2 * j, 2 * j + 2):
                                tile(i, s, t0, ahead)
                        if j:
                            q = (j - 1) % 2
                            m = mask[0:EP, q * WMAX:q * WMAX + cols]
                            wait(1 if j < B7 else 0)
                            v.sem_inc(s_past, 1)
                            step(v.copy_predicated(pos[0:EP, 0:cols], m.bitcast(U16), cum[0:EP, q * WMAX:q * WMAX + cols]))
                with v.Fori(0, its) as i:
                    step_count.loop(i, 3 * B7)
                    rank(i)
                step_count.end(its)
            elif name == "split":
                wait()
                step(v.tensor_copy(posi[0:EP, 0:cols], pos[0:EP, 0:cols]))
                wait()
                step(v.tensor_scalar(tli[0:EP, 0:cols], posi[0:EP, 0:cols], 7, None, ALU.logical_shift_right))
                wait()
                step(v.tensor_copy(tf[0:EP, 0:cols], tli[0:EP, 0:cols]))
                wait()
                step(v.tensor_scalar(tli[0:EP, 0:cols], posi[0:EP, 0:cols], P - 1, None, ALU.bitwise_and))
                wait()
                step(v.tensor_copy(pos[0:EP, 0:cols], tli[0:EP, 0:cols]))
                wait()
            elif name == "sort":
                def sort(i, groups=groups, ahead=ahead, t0=t0, k0=k0):
                    v.wait_ge(s_ht, i * CU + (k0 + GR))
                    v.tensor_copy(posh[0:EP, :], pos[0:EP, ds(i * CU + (k0 - c0), CU)])
                    if not groups:
                        v.tensor_copy(v1h[0:EP, :], v1[0:EP, ds(i * CU + k0, CU)])
                    v.tensor_copy(tfh[0:EP, :], tf[0:EP, ds(i * CU + (k0 - c0), CU)]).then_inc(s_posh, 1)
                    v.wait_ge(s_posh, i + (k0 // CU + 1))

                    def operands(j):
                        if j % CW == 0:
                            v.wait_ge(s_col, i * CU + (k0 + j + CW))
                        for n in range(j, j + CW):
                            q = n % KR
                            v.tensor_scalar(LH[0:EP, q * P:(q + 1) * P], iota_t[0:EP, 0:P],
                                            posh[0:EP, n:n + 1], None, ALU.is_equal).then_inc(s_lh, 1)
                        for n in range(j + 1, j + CW, 2) if not groups else ():
                            q = n % KR
                            v.tensor_scalar(LV[0:EP, 2 * q * P:(2 * q + 1) * P], iota_t[0:EP, 0:P],
                                            posh[0:EP, n:n + 1], v1h[0:EP, n:n + 1], ALU.is_equal, ALU.mult)
                        for n in range(j, j + CW):
                            q = n % KR
                            v.tensor_scalar(HT[0:EP, q * TMAX:q * TMAX + tiles], iota_t[0:EP, 0:tiles],
                                            tfh[0:EP, n:n + 1], None, ALU.is_equal).then_inc(s_ht, 1)

                    operands(0)
                    for j in range(CU):
                        if groups:
                            if j % CW == 0 and j + CW < CU:
                                operands(j + CW)
                            tile(i, j, t0, ahead)
                        elif j % CW == 0 and j:
                            operands(j)
                repeat(v, its, sort)
            elif name == "decode":
                v.wait_ge(s_sx, c + 1)
                a, b, d, e = (DI[:, n * TMAX:n * TMAX + tiles] for n in range(4))
                v.tensor_copy(a, psV[0][:, 0:tiles])
                step(v.tensor_copy(b, psV[1][:, 0:tiles]))
                wait()
                v.tensor_scalar(d, a, 3, None, ALU.logical_shift_left)
                step(v.tensor_scalar(e, b, 8, None, ALU.logical_shift_right))
                wait()
                step(v.tensor_tensor(idx[:, ch0:ch0 + tiles], d, e, ALU.bitwise_or))
                step(v.tensor_scalar(a, b, 255, None, ALU.bitwise_and))
                wait()
                v.tensor_copy(srcl[:, ch0:ch0 + tiles], a).then_inc(s_dec, 1)
                v.wait_ge(s_dec, c + 1)
                v.wait_ge(s_tile, ch0 + GR)
                for n in range(GR // QR):
                    fetch(0, n, ch0 // GR)
            elif name in ("heads", "tail"):
                nb = LD if name == "heads" else 1
                nh = nb * HEADS

                def heads(i, s):
                    w = slice(0, nb * D)
                    h3 = lambda ap: ap.rearrange("p (g d) -> p g d", d=HC)
                    wide = lambda ap: ap.unsqueeze(2).to_broadcast([P, nh, HC])
                    xb = X[:, ds((i + m0) * (LD * D), nb * D)] if name == "heads" else X[:, m0 * LD * D:m0 * LD * D + nb * D]
                    if s == 0:
                        step(v.tensor_reduce(hs[:, 0:nh], h3(xb), AX.X, ALU.add))
                    elif s == 1:
                        wait()
                        step(v.tensor_scalar(hm[:, 0:nh], hs[:, 0:nh], 1.0 / HC, None, ALU.mult))
                    elif s == 2:
                        wait()
                        v.tensor_tensor(h3(cen[:, w]), h3(xb), wide(hm[:, 0:nh]), ALU.subtract).then_inc(s_cen, 1)
                    elif s == 4:
                        v.wait_ge(s_sq, i + (m0 + 1))
                        v.tensor_reduce(hq[:, 0:nh], h3(sqr[:, w]), AX.X, ALU.add).then_inc(s_ss, 1)
                    elif s == 6:
                        v.wait_ge(s_hstd, i + (m0 + 1))
                        step(v.tensor_scalar(hs[:, 0:nh], hq[:, 0:nh], HEAD_EPS, None, ALU.add))
                    elif s == 7:
                        wait()
                        step(v.reciprocal(hr[:, 0:nh], hs[:, 0:nh]))
                    elif s == 8:
                        wait()
                        v.wait_ge(s_kg, i + (m0 + 1))
                        v.tensor_tensor(kn[:, 0:nb * 2 * KW].rearrange("p (k w) -> p k w", w=KW)[:, :, 0:P].rearrange(
                            "p k (g d) -> p k g d", d=HC), cen[:, w].rearrange("p (k g d) -> p k g d", d=HC, k=nb * 2),
                            hr[:, 0:nh].rearrange("p (k g) -> p k g", k=nb * 2).unsqueeze(3).to_broadcast(
                                [P, nb * 2, P // HC, HC]), ALU.mult).then_inc(s_kn, 1)

                def body(i, t0=t0, ahead=ahead):
                    for s in range(GR):
                        tile(i, s, t0, ahead)
                        if s < 10:
                            heads(i, s)
                if its > 1:
                    with v.Fori(0, its) as i:
                        step_count.loop(i, 4)
                        body(i)
                    step_count.end(its)
                else:
                    body(0)
                m0 += its
            elif name == "kv":
                v.wait_ge(s_par, 16 * 12)
                v.wait_ge(s_kg, NB // LD + 3)
                step(v.tensor_tensor(brow[:, :], brow[:, :], b2r[:, :], ALU.add))
                for h in range(2):
                    v.tensor_scalar(kvw[:, (4 + h) * P:(5 + h) * P], ident[:, :], psG[h][:, P:P + 1], None, ALU.mult).then_inc(s_dg, 1)
                v.wait_ge(s_se, 2)
                for h in range(2):
                    g, se, sd_ = psG[h][:, 0:P], psP[:, h * P:(h + 1) * P], psG[h][:, P:P + 1]
                    vwr, vbr = hrow[:, h * P:(h + 1) * P], hrow[:, D + h * P:D + (h + 1) * P]
                    kwc, kbc = hv[:, 2 * h:2 * h + 1], hv[:, 2 * h + 1:2 * h + 2]
                    t_ = [kvw[:, n * P:(n + 1) * P] for n in range(4)]
                    step(v.tensor_scalar(t_[0], se, kbc, None, ALU.mult))
                    step(v.tensor_scalar(mcol[:, 0:1], sd_, kwc, None, ALU.mult))
                    wait()
                    step(v.scalar_tensor_tensor(out=t_[1], in0=g, scalar=kwc, in1=t_[0], op0=ALU.mult, op1=ALU.add))
                    step(v.scalar_tensor_tensor(out=mcol[:, 1:2], in0=kbc, scalar=float(N), in1=mcol[:, 0:1],
                                                op0=ALU.mult, op1=ALU.add))
                    wait()
                    step(v.tensor_tensor(t_[2], t_[1], vwr, ALU.mult))
                    wait()
                    step(v.scalar_tensor_tensor(out=t_[3], in0=vbr, scalar=mcol[:, 1:2], in1=t_[2], op0=ALU.mult, op1=ALU.add))
                    wait()
                    for a in range(0, P, HC):
                        w = W1[a:a + HC, h * D + h * P + a:h * D + h * P + a + HC]
                        step(v.scalar_tensor_tensor(out=w, in0=t_[3][a:a + HC, a:a + HC], scalar=1.0 / N, in1=w,
                                                    op0=ALU.mult, op1=ALU.add))
                    wait()
                v.memset(mcol[:, :], 0.0).then_inc(s_kv, 1)
            elif name == "own":
                def body(i, t0=t0, ahead=ahead, b0=b0, nb=LD if its > 1 else 1):
                    for s in range(GR):
                        tile(i, s, t0, ahead)
                        if (s % 4 == 0 and 0 < s <= 4 * (nb - 1)) or s == (GR - 1 if nb == LD else 3):
                            j = -(-s // 4) - 1
                            b = i * LD + (b0 + j)
                            v.wait_ge(s_xp, b + 3)
                            v.tensor_tensor(X[:, ds(b * D, D)], X[:, ds(b * D, D)], psG[j % 2][:, 0:D], ALU.add).then_inc(s_xa, 1)
                repeat(v, its, body)
                b0 += its * LD
            t0 += its * GR * groups
            k0 += its * CU if name == "sort" else 0


def nodes(nc, ctx, kk, dram, x):
    def sb(name, shape, dt):
        return ctx.enter_context(nc.sbuf_tensor(name, shape, dt))

    def sem(name):
        return ctx.enter_context(nc.semaphore(name))

    X, AGG, ident, ones, eps, W2, brow, gw, gb = (kk[n] for n in (
        "X", "AGG", "ident", "ones", "eps", "W2", "brow", "gw", "gb"))
    bank = kk["psum"]
    psT, psM, psU, psL = bank[0:2], bank[2:4], bank[4:6], bank[6:8]
    LW = NQ * NX
    PT, PD = 64, 128
    rcn = sb("rcn", [P, NB], F32)
    xr = sb("xr", [P, 2 * NQ * D], F32)
    xlast = sb("xlast", [P, D], F32)
    mean = sb("mean", [P, 2 * D], F32)
    mt = sb("mt", [P, 2 * D], F32)
    tmp = sb("tmp", [P, 2 * D], F32)
    nst = sb("nst", [P, NQ * 6], F32)
    nmv = sb("nmv", [P, NQ * 2], F32)
    nsd = sb("nsd", [P, NQ], F32)
    nrs = sb("nrs", [P, NQ], F32)
    nmr = sb("nmr", [P, NQ], F32)
    X2 = sb("X2", [P, 2 * NQ * D], F32)
    ut = sb("ut", [P, 2 * D], F32)
    less = sb("less", [P, P], F32)
    seg = sb("seg", [P, LW], F32)
    carry = sb("carry", [P, NX], F32)
    lg, r0, r1, r2, r3, r4 = (sb(f"route{n}", [P, LW], F32) for n in range(6))
    q = [sb(f"rnode{n}", [P, NQ], F32) for n in range(9)]
    sidx = sb("sidx", [P, 2 * NQ], I32)

    s_xr = [sem("x_again_0"), sem("x_again_1")]
    s_rc, s_xb, s_mean, s_tr, s_mt, s_mm, s_xm, s_x1 = (sem(n) for n in (
        "count_reciprocals", "x_with_bias", "mean_ready", "mean_transposed", "mean_t_copied", "mean_products",
        "mean_products_added", "x1_ready"))
    s_v, s_nv, s_ns, s_nr, s_x2, s_u, s_ut, s_lg = (sem(n) for n in (
        "node_steps", "x1_variance", "x1_std", "x1_scale", "x1_normal", "x1n_transposed", "x1n_t_copied", "logits"))
    s_mx, s_ex, s_oh, s_pf, s_rt, s_sl = (sem(n) for n in (
        "logit_max", "logit_exp", "expert_onehot", "expert_prefix", "prefix_read", "slots_ready"))
    s_xf, s_xl = sem("x1_normal_slots_free"), sem("last_x_again")
    s_sc = [sem("rows_scattered_0"), sem("rows_scattered_1")]
    s_past = sem("past_a_wait_node")
    block = ctx.enter_context(nc.Block())
    NT = NB // NQ

    def batches(body):
        def run(eng, tally=None, per=0):
            for t in (0, 1):
                body(t, t % 2, True, t >= 1, False)
            n = (NT - 3) // 2
            with eng.Fori(0, n) as i:
                if tally:
                    tally.loop(i, per)
                for a in range(2):
                    body(i * 2 + (2 + a), a, True, True, True)
            if tally:
                tally.end(n)
            for t in range(2 + 2 * n, NT + 2):
                body(t, t % 2, t < NT, t <= NT, True)
        return run

    @block.sync
    def _(sp):
        def load(t, p, a, b, c):
            if not a:
                return
            sp.wait_ge(s_x1, t * NQ + 1)
            o = p * NQ * D
            if isinstance(t, int) and t == NT - 1:
                sp.dma_start(xr[:, o:o + (NQ - 1) * D].rearrange("p (j d) -> p j d", d=D),
                             x[t * NQ * P:(NB - 1) * P, :].rearrange("(j p) d -> p j d", p=P)).then_inc(s_xr[p], 16)
            else:
                sp.dma_start(xr[:, o:o + NQ * D].rearrange("p (j d) -> p j d", d=D),
                             x[ds(t * (NQ * P), NQ * P), :].rearrange("(j p) d -> p j d", p=P)).then_inc(s_xr[p], 16)
        sp.wait_ge(s_x1, 1)
        sp.dma_start(xlast[0:LASTROWS, :], x[(NB - 1) * P:N, :]).then_inc(s_xl, 16)
        batches(load)(sp)

    @block.scalar
    def _(act):
        act.wait_ge(s_rc, 1)

        def body(t, p, a, b, c):
            m = (t - 1) * NQ if b else 0
            if b:
                act.wait_ge(s_nv, t)
                act.activation(nsd[:, :], nmv[:, 1:2 * NQ:2], ACT.Sqrt, bias=eps[:, :]).then_inc(s_ns, 1)
            for j in range(NQ):
                h, g = (p + j) % 2, (p + 1 + j) % 2
                if a:
                    act.wait_ge(s_tr, t * NQ + (j + 1))
                    act.activation(mean[:, h * D:(h + 1) * D], AGG[:, ds((t * NQ + j) * AGW, D)], ACT.Copy,
                                   scale=rcn[:, ds(t * NQ + j, 1)]).then_inc(s_mean, 1)
                if b:
                    if j == 0:
                        act.wait_ge(s_nr, t)
                        act.wait_ge(s_xf, t)
                    o = ((1 - p) * NQ + j) * D
                    act.activation(X2[:, o:o + D], X[:, ds((m + j) * D, D)], ACT.Identity, bias=nmr[:, j:j + 1],
                                   scale=nrs[:, j:j + 1]).then_inc(s_x2, 1)
                if a:
                    act.wait_ge(s_tr, t * NQ + (j + 3))
                    act.wait_ge(s_mm, t * NQ + (j + 1))
                    act.activation(mt[:, h * D:(h + 1) * D], psT[h][:, 0:D], ACT.Copy).then_inc(s_mt, 1)
                if c and j == 1:
                    act.wait_ge(s_mx, t - 1)
                    act.activation(r3[:, :], r3[:, :], ACT.Exp).then_inc(s_ex, 1)
        batches(body)(act)

    @block.tensor
    def _(pe):
        for s in (s_tr, s_mm, s_u):
            pe.sem_inc(s, 2)

        def body(t, p, a, b, c):
            m = (t - 1) * NQ if b else 0
            for j in range(NQ):
                h, g = (p + j) % 2, (p + 1 + j) % 2
                n = t * NQ + j
                if a:
                    pe.wait_ge(s_mean, n + 1)
                    pe.wait_ge(s_mt, n + 1)
                    for k in range(2):
                        ins = pe.transpose(psT[h][:, k * P:(k + 1) * P], mean[:, h * D + k * P:h * D + (k + 1) * P], ident[:, :])
                    ins.then_inc(s_tr, 1)
                if b:
                    pe.wait_ge(s_x2, m + (j + 1))
                    pe.wait_ge(s_ut, m + (j + 1))
                    o = ((1 - p) * NQ + j) * D
                    for k in range(2):
                        ins = pe.transpose(psU[g][:, k * P:(k + 1) * P], X2[:, o + k * P:o + (k + 1) * P], ident[:, :])
                    ins.then_inc(s_u, 1)
                if c and j == 3:
                    pe.wait_ge(s_oh, t - 1)
                    pe.matmul(psL[p][:, PT:PT + LW], ones[:, :], r1[:, :], start=True, stop=True)
                    pe.matmul(psL[p][:, PD:PD + LW], less[:, :], r1[:, :], start=True, stop=True).then_inc(s_pf, 1)
                if a:
                    pe.wait_ge(s_mt, n + 3)
                    pe.wait_ge(s_xm, n + 1)
                    for k in range(2):
                        ins = pe.matmul(psM[h][:, 0:D], mt[:, h * D + k * P:h * D + (k + 1) * P],
                                        W2[:, k * D:(k + 1) * D], start=(k == 0), stop=(k == 1))
                    ins.then_inc(s_mm, 1)
                if b:
                    pe.wait_ge(s_ut, m + (j + 3))
                    if j == 0:
                        pe.wait_ge(s_rt, t)
                    for k in range(2):
                        ins = pe.matmul(psL[1 - p][:, j * NX:(j + 1) * NX], ut[:, g * D + k * P:g * D + (k + 1) * P],
                                        gw[:, k * NX:(k + 1) * NX], start=(k == 0), stop=(k == 1))
                    ins.then_inc(s_lg, 1)
        batches(body)(pe)

    @block.vector
    def _(v):
        count = Tally(s_v)
        step = count.add

        def wait():
            v.wait_ge(s_v, count.value())
        v.memset(xlast[:, :], 0.0)
        v.memset(xr[:, :], 0.0).then_inc(s_x1, NQ + 1)
        for s in (s_mt, s_ut, s_xm, s_rt):
            v.sem_inc(s, 2)
        v.memset(seg[:, :], 1.0)
        v.memset(carry[:, :], 0.0)
        v.tensor_scalar(less[:, :], kk["upper"][:, :], -1.0, None, ALU.add)
        step(v.tensor_scalar(rcn[:, :], AGG[:, D:NB * AGW:AGW], 1.0, PARTS, ALU.max, ALU.mult))
        wait()
        step(v.memset(seg[:, 0:LW:NQ], 0.0))
        v.reciprocal(rcn[:, :], rcn[:, :]).then_inc(s_rc, 1)

        g3 = lambda ap: ap.rearrange("p (b e) -> p b e", e=NX)
        wide = lambda ap: ap.unsqueeze(2).to_broadcast([P, NQ, NX])
        io8 = kk["iota8"][:, :].unsqueeze(1).to_broadcast([P, NQ, NX])

        def route(t, p, s):
            mine = ds(t * NQ, NQ)
            if s:
                wait()
            if s == 0:
                v.wait_ge(s_lg, t * NQ + NQ)
                step(v.tensor_tensor(g3(lg[:, :]), g3(psL[p][:, 0:LW]), gb[:, :].unsqueeze(1).to_broadcast([P, NQ, NX]), ALU.add))
            elif s == 1:
                step(v.tensor_reduce(q[0][:, :], g3(lg[:, :]), AX.X, ALU.max))
            elif s == 2:
                v.tensor_tensor(g3(r3[:, :]), g3(lg[:, :]), wide(q[0][:, :]), ALU.subtract).then_inc(s_mx, 1)
            elif s == 3:
                step(v.tensor_tensor(g3(r0[:, :]), g3(lg[:, :]), wide(q[0][:, :]), ALU.is_equal))
            elif s == 4:
                step(v.tensor_tensor(g3(r0[:, :]), g3(r0[:, :]), io8, ALU.mult))
            elif s == 5:
                step(v.tensor_reduce(q[1][:, :], g3(r0[:, :]), AX.X, ALU.max))
            elif s == 6:
                v.tensor_tensor(g3(r1[:, :]), io8, wide(q[1][:, :]), ALU.is_equal).then_inc(s_oh, 1)
            elif s == 7:
                v.wait_ge(s_ex, t + 1)
                step(v.tensor_reduce(q[2][:, :], g3(r3[:, :]), AX.X, ALU.add))
            elif s == 8:
                step(v.reciprocal(q[3][:, :], q[2][:, :]))
            elif s == 9:
                v.wait_ge(s_pf, t + 1)
                step(v.tensor_copy(r2[:, :].rearrange("p (e b) -> p b e", b=NQ), g3(psL[p][:, PT:PT + LW])))
            elif s == 10:
                step(v.tensor_tensor(r2[:, 0:LW:NQ], r2[:, 0:LW:NQ], carry[:, :], ALU.add))
            elif s == 11:
                step(v.tensor_tensor_scan(r4[:, :], seg[:, :], r2[:, :], 0.0, ALU.mult, ALU.add))
            elif s == 12:
                step(v.tensor_copy(carry[:, :], r4[:, NQ - 1:LW:NQ]))
            elif s == 13:
                v.tensor_tensor(g3(r0[:, :]), r4[:, :].rearrange("p (e b) -> p b e", b=NQ), g3(psL[p][:, PD:PD + LW]),
                                ALU.add).then_inc(s_rt, 1)
            elif s == 14:
                v.wait_ge(s_rt, t + 3)
                step(v.tensor_tensor(r0[:, :], r0[:, :], r1[:, :], ALU.mult))
            elif s == 15:
                step(v.tensor_reduce(q[4][:, :], g3(r0[:, :]), AX.X, ALU.add))
            elif s == 16:
                step(v.tensor_scalar(q[5][:, :], q[4][:, :], float(CAP), None, ALU.is_lt))
                step(v.tensor_scalar(q[6][:, :], q[1][:, :], -float(CAPR), float(NX * CAPR), ALU.mult, ALU.add))
            elif s == 17:
                step(v.tensor_tensor(kk["kp"][:, mine], q[5][:, :], q[3][:, :], ALU.mult))
                step(v.tensor_tensor(q[7][:, :], q[4][:, :], q[6][:, :], ALU.add))
            elif s == 18:
                step(v.scalar_tensor_tensor(out=q[0][:, :], in0=q[7][:, :], scalar=-float(NX * CAPR), in1=q[5][:, :],
                                            op0=ALU.add, op1=ALU.mult))
                step(v.tensor_tensor(q[8][:, :], q[7][:, :], kk["dummy"][:, mine], ALU.subtract))
            elif s == 19:
                step(v.tensor_scalar(kk["gidx"][:, mine], q[0][:, :], float(NX * CAPR), None, ALU.add))
                step(v.tensor_tensor(q[8][:, :], q[8][:, :], q[5][:, :], ALU.mult))
            elif s == 20:
                v.tensor_tensor(sidx[:, p * NQ:(p + 1) * NQ], q[8][:, :], kk["dummy"][:, mine], ALU.add).then_inc(s_sl, 1)

        def body(t, p, a, b, c):
            m = (t - 1) * NQ if b else 0
            if b:
                v.wait_ge(s_ns, t)
                step(v.reciprocal(nrs[:, :], nsd[:, :]))
                wait()
                v.scalar_tensor_tensor(out=nmr[:, :], in0=nmv[:, 0:2 * NQ:2], scalar=-1.0, in1=nrs[:, :],
                                       op0=ALU.mult, op1=ALU.mult).then_inc(s_nr, 1)
            for j in range(NQ + 2):
                h, g = (p + j) % 2, (p + 1 + j) % 2
                n = t * NQ + j
                if b and j < NQ:
                    v.wait_ge(s_u, m + (j + 3))
                    if j > 1 or not (isinstance(t, int) and t == 1):
                        v.wait_ge(s_lg, m + (j - 1))
                    v.tensor_copy(ut[:, g * D:(g + 1) * D], psU[g][:, 0:D]).then_inc(s_ut, 1)
                if a and 1 <= j <= NQ:
                    if j == 1:
                        v.wait_ge(s_xb, t + 1)
                    v.wait_ge(s_xm, n + 2)
                    o = (p * NQ + j - 1) * D
                    own = xlast[:, :] if isinstance(t, int) and t == NT - 1 and j == NQ else xr[:, o:o + D]
                    v.tensor_tensor(X[:, ds((n - 1) * D, D)], tmp[:, (1 - h) * D:(2 - h) * D], own,
                                    ALU.add).then_inc(s_x1, 1)
                if a and j >= 2:
                    v.wait_ge(s_x1, n + NQ)
                    v.sem_inc(s_past, 1)
                    step(v.bn_stats(nst[:, 6 * (j - 2):6 * (j - 1)], X[:, ds((n - 2) * D, D)]))
                if c and j < NQ:
                    for s in range(3):
                        route(t - 2, p, 3 * j + s)
                if a and j < NQ:
                    v.wait_ge(s_mm, n + 3)
                    v.tensor_tensor(tmp[:, h * D:(h + 1) * D], psM[h][:, 0:D], X[:, ds(n * D, D)], ALU.add).then_inc(s_xm, 1)
            if a:
                wait()
                v.sem_inc(s_past, 1)
                for j in range(NQ):
                    ins = v.bn_aggr(nmv[:, 2 * j:2 * j + 2], nst[:, 6 * j:6 * j + 6])
                ins.then_inc(s_nv, 1)
        batches(body)(v, count, 2 * (1 + NQ + 21))

    @block.gpsimd
    def _(pool):
        def bias(t, p):
            o = p * NQ * D
            pool.wait_ge(s_xr[p], (t + (2 - p)) * 8)
            pool.tensor_tensor(xr[:, o:o + NQ * D].rearrange("p (j d) -> p j d", d=D),
                               xr[:, o:o + NQ * D].rearrange("p (j d) -> p j d", d=D),
                               brow[:, :].unsqueeze(1).to_broadcast([P, NQ, D]), ALU.add).then_inc(s_xb, 1)

        def body(t, p, a, b, c):
            if not isinstance(t, int) or t + 1 < NT:
                bias(t + 1, 1 - p)
            if c:
                pool.wait_ge(s_sl, t - 1)
                pool.sem_inc(s_past, 1)
                for j in range(NQ):
                    rows = LASTROWS if isinstance(t, int) and t == NT + 1 and j == NQ - 1 else P
                    k = p * NQ + j
                    pool.indirect_dma_start(dram["buf"], bass.IndirectOffsetOnAxis(ap=sidx[0:rows, k:k + 1], axis=0),
                                            X2[0:rows, k * D:(k + 1) * D], None).then_inc(s_sc[p], 16)
                pool.wait_ge(s_sc[p], (t - p) * (8 * NQ))
                pool.sem_inc(s_xf, 1)
        pool.sem_inc(s_xf, 2)
        bias(0, 0)
        pool.wait_ge(s_xl, 16)
        pool.tensor_tensor(xlast[:, :], xlast[:, :], brow[:, :], ALU.add)
        batches(body)(pool)


def experts(nc, ctx, kk, dram, f1, fb1, f2, fb2):
    def sb(name, shape, dt):
        return ctx.enter_context(nc.sbuf_tensor(name, shape, dt))

    def sem(name):
        return ctx.enter_context(nc.semaphore(name))

    ident, bank = kk["ident"], kk["psum"]
    buf, ybuf = dram["buf"], dram["ybuf"]
    w1 = sb("w1", [P, 2 * 2 * F], F32)
    w2 = sb("w2", [P, 2 * FT * D], F32)
    b2 = sb("b2", [P, 2 * D], F32)
    b1r = sb("b1r", [NX * FT, P], F32)
    b1c = sb("b1c", [P, NX * FT], F32)
    xb = sb("xb", [P, 2 * TQ * D], F32)
    xt = sb("xt", [P, 2 * HALF], F32)
    ht = sb("ht", [P, FT * HALF], F32)
    yb = sb("yb", [P, 2 * TQ * D], F32)
    nn = sb("nn", [P, TQ * D], U32)
    zr = sb("zr", [P, TQ * D], F32)
    s_w = [sem("weights_0"), sem("weights_1")]
    s_b = sem("first_biases")
    s_bt, s_bc = sem("first_biases_t"), sem("first_biases_copied")
    s_xb = [sem("rows_0"), sem("rows_1")]
    s_t, s_xt, s_h, s_r, s_y, s_ys, s_vs = (sem(n) for n in (
        "rows_transposed", "rows_t_copied", "hidden_product", "hidden_ready", "out_product", "out_copied", "expert_steps"))
    s_past = sem("past_a_wait_2")
    s_free = sem("out_slot_free")
    s_yd, s_zr = sem("out_sums"), sem("zeros_ready")
    s_st = [sem("out_stored_0"), sem("out_stored_1")]
    block = ctx.enter_context(nc.Block())
    psT, psH, psY = bank[0:2], bank[2:4], bank[4:6]

    def halves(eng, body, n=NX // 2):
        with eng.Fori(0, n) as i:
            for a in range(4):
                body(i, a)

    @block.sync
    def _(sp):
        sp.dma_start(b1r[:, :], fb1.rearrange("e (f p) -> (e f) p", p=P)).then_inc(s_b, 16)

        def weights(e, q):
            sp.dma_start(w1[:, q * 2 * F:(q + 1) * 2 * F].rearrange("p (k f) -> p k f", k=2),
                         f1[ds(e, 1), :, :].rearrange("a (k p) f -> p (a k) f", p=P)).then_inc(s_w[q], 16)
            sp.dma_start(w2[:, q * FT * D:(q + 1) * FT * D].rearrange("p (f d) -> p f d", f=FT),
                         f2[ds(e, 1), :, :].rearrange("a (f p) d -> p (a f) d", p=P)).then_inc(s_w[q], 16)
            sp.dma_start(b2[:, q * D:(q + 1) * D], fb2[ds(e, 1), :].partition_broadcast(P)).then_inc(s_w[q], 16)

        def load(i, a):
            if a % 2 == 0:
                sp.wait_ge(s_ys, i * 4 + (a + 2))
                weights(i * 2 + a // 2, a // 2)
            sp.wait_ge(s_t, i * 4 + (a + 1))
            sp.dma_start(xb[0:TM, a % 2 * TQ * D:(a % 2 + 1) * TQ * D],
                         buf[ds((i * 4 + a) * HALF, HALF), :].rearrange("(p m) d -> p (m d)", m=TQ)).then_inc(s_xb[a % 2], 16)
        halves(sp, load)

    @block.tensor
    def _(pe):
        pe.sem_inc(s_t, 2)
        pe.wait_ge(s_b, 16)
        pe.transpose(bank[6][:, 0:NX * FT], b1r[:, :], ident[0:NX * FT, 0:NX * FT]).then_inc(s_bt, 1)

        def half(i, a):
            n = i * 4 + a
            q, h = a // 2, a % 2
            pe.wait_ge(s_xb[h], (i * 2 + (q + 1)) * 16)
            pe.wait_ge(s_xt, n + 1)
            for m in range(TQ):
                for k in range(2):
                    ins = pe.transpose(psT[k][:, m * TM:(m + 1) * TM],
                                       xb[0:TM, h * TQ * D + m * D + k * P:h * TQ * D + m * D + (k + 1) * P],
                                       ident[0:TM, 0:TM])
            ins.then_inc(s_t, 1)
            if h == 0:
                pe.wait_ge(s_w[q], i * 48 + 48)
            pe.wait_ge(s_xt, n + 2)
            for f in range(FT):
                pe.wait_ge(s_r, n * FT + (f + 1))
                for k in range(2):
                    ins = pe.matmul(psH[f % 2][:, 0:HALF], w1[:, (q * 2 + k) * F + f * P:(q * 2 + k) * F + (f + 1) * P],
                                    xt[:, k * HALF:(k + 1) * HALF], start=(k == 0), stop=(k == 1))
                ins.then_inc(s_h, 1)
            for m in range(TQ):
                pe.wait_ge(s_y, n * TQ + (m + 1))
                for f in range(FT):
                    if m == 0:
                        pe.wait_ge(s_r, n * FT + (f + 3))
                    ins = pe.matmul(psY[m % 2][0:TM, 0:D], ht[:, f * HALF + m * TM:f * HALF + (m + 1) * TM],
                                    w2[:, (q * FT + f) * D:(q * FT + f + 1) * D], start=(f == 0), stop=(f == FT - 1))
                ins.then_inc(s_yd, 1)
        halves(pe, half)

    @block.scalar
    def _(act):
        act.sem_inc(s_xt, 1)
        act.sem_inc(s_r, 2)
        act.wait_ge(s_bt, 1)
        act.activation(b1c[:, :], bank[6][:, 0:NX * FT], ACT.Copy).then_inc(s_bc, 1)
        act.wait_ge(s_bc, 1)

        def half(i, a):
            n = i * 4 + a
            act.wait_ge(s_t, n + 3)
            act.wait_ge(s_h, n * FT + 1)
            for k in range(2):
                ins = act.activation(xt[:, k * HALF:(k + 1) * HALF], psT[k][:, 0:HALF], ACT.Copy)
            ins.then_inc(s_xt, 1)
            act.wait_ge(s_yd, n * TQ + 1)
            for f in range(FT):
                act.wait_ge(s_h, n * FT + (f + 2))
                act.sem_inc(s_past, 1)
                act.activation(ht[:, f * HALF:(f + 1) * HALF], psH[f % 2][:, 0:HALF], ACT.Relu,
                               bias=b1c[:, ds((i * 2 + a // 2) * FT + f, 1)]).then_inc(s_r, 1)
        halves(act, half)

    @block.vector
    def _(v):
        v.sem_inc(s_y, 2)
        v.sem_inc(s_ys, 4)
        v.sem_inc(s_h, 1)
        v.sem_inc(s_yd, 1)
        v.memset(zr[:, :], 0.0).then_inc(s_zr, 1)
        v.wait_ge(s_zr, 1)

        def half(i, a):
            n = i * 4 + a
            q, h = a // 2, a % 2
            y = yb[0:TM, h * TQ * D:(h + 1) * TQ * D]
            v.wait_ge(s_free, n + 1)
            for m in range(TQ):
                v.wait_ge(s_yd, n * TQ + (m + 2))
                v.tensor_tensor(y[:, m * D:(m + 1) * D], psY[m % 2][0:TM, 0:D], b2[0:TM, q * D:(q + 1) * D],
                                ALU.add).then_inc(s_y, 1)
            v.wait_ge(s_y, n * TQ + (TQ + 2))
            v.tensor_tensor(nn[0:TM, :], y, y, ALU.not_equal).then_inc(s_vs, 1)
            v.wait_ge(s_vs, n + 1)
            v.sem_inc(s_past, 1)
            v.copy_predicated(y, nn[0:TM, :], zr[0:TM, :]).then_inc(s_ys, 1)
        halves(v, half)

    @block.gpsimd
    def _(pool):
        pool.sem_inc(s_free, 2)

        def half(i, a):
            h = a % 2
            pool.wait_ge(s_ys, i * 4 + (a + 5))
            pool.dma_start(ybuf[ds((i * 4 + a) * HALF, HALF), :].rearrange("(p m) d -> p (m d)", m=TQ),
                           yb[0:TM, h * TQ * D:(h + 1) * TQ * D]).then_inc(s_st[h], 16)
            pool.wait_ge(s_st[h], (i * 2 + (a // 2 + 1)) * 16)
            pool.sem_inc(s_free, 1)
        halves(pool, half)


def outputs(nc, ctx, kk, dram, out):
    def sb(name, shape, dt):
        return ctx.enter_context(nc.sbuf_tensor(name, shape, dt))

    def sem(name):
        return ctx.enter_context(nc.semaphore(name))

    X, gidx, kp = kk["X"], kk["gidx"], kk["kp"]
    Y = sb("Y", [P, NB * D], F32)
    Z = sb("Z", [P, 4 * D], F32)
    lim = sb("lim", [P, 4 * D], F32)
    inf = sb("inf", [P, 4 * D], U32)
    R = 4
    s_y = [sem(f"row_gathered_{n}") for n in range(R)]
    s_z, s_c, s_i, s_o = (sem(n) for n in ("scaled", "clamped", "infinite_mask_and_set", "out_rows"))
    s_past = sem("past_a_wait_3")
    s_st = sem("out_stored")
    block = ctx.enter_context(nc.Block())

    def blocks(eng, body):
        with eng.Fori(0, NB // R) as i:
            for h in range(R):
                body(i * R + h, h, i * 16 + 16)
        body(NB - 1, 0, 16 * (NB // R + 1))

    @block.gpsimd
    def _(pool):
        for b in range(NB):
            if b >= R:
                pool.wait_ge(s_y[b % R], 16 * (b // R))
            pool.indirect_dma_start(Y[:, b * D:(b + 1) * D], None, dram["ybuf"],
                                    bass.IndirectOffsetOnAxis(ap=gidx[:, b:b + 1], axis=0)).then_inc(s_y[b % R], 16)

    @block.scalar
    def _(act):
        def body(b, h, k):
            act.wait_ge(s_y[h], k)
            act.wait_ge(s_o, b + 1)
            act.activation(Z[:, h * D:(h + 1) * D], Y[:, ds(b * D, D)], ACT.Copy, scale=kp[:, ds(b, 1)]).then_inc(s_z, 1)
        blocks(act, body)

    @block.vector
    def _(v):
        v.sem_inc(s_o, R)

        def body(b, h, k):
            w = slice(h * D, (h + 1) * D)
            y = Z[:, w]
            v.wait_ge(s_z, b + 1)
            v.wait_ge(s_o, b + 1)
            v.tensor_scalar(inf[:, w], y, 0.0, 0.0, ALU.mult, ALU.not_equal).then_inc(s_i, 1)
            v.tensor_scalar(lim[:, w], y, -10000.0, 10000.0, ALU.max, ALU.min).then_inc(s_c, 1)
            v.wait_ge(s_c, b + 1)
            v.sem_inc(s_past, 1)
            v.copy_predicated(y, inf[:, w], lim[:, w]).then_inc(s_i, 1)
            v.wait_ge(s_i, b * 2 + 2)
            v.tensor_tensor(X[:, ds(b * D, D)], X[:, ds(b * D, D)], y, ALU.add).then_inc(s_o, 1)
        blocks(v, body)

    @block.sync
    def _(sp):
        with sp.Fori(0, NB // R) as i:
            sp.wait_ge(s_o, i * R + 2 * R)
            sp.dma_start(out[ds(i * (R * P), R * P), :].rearrange("(j p) d -> p j d", p=P),
                         X[:, ds(i * (R * D), R * D)].rearrange("p (j d) -> p j d", j=R)).then_inc(s_st, 16)
        sp.wait_ge(s_o, NB + R)
        sp.dma_start(out[(NB - 1) * P:N, :], X[0:LASTROWS, (NB - 1) * D:NB * D]).then_inc(s_st, 16)
        sp.wait_ge(s_st, 16 * (NB // R + 1))


def kernel(x, src, dst, L0_gnn_W1, L0_gnn_b1, L0_gnn_W2, L0_gnn_b2, L0_mix_kln_weight, L0_mix_kln_bias,
           L0_mix_vln_weight, L0_mix_vln_bias, L0_ffn_gate_w, L0_ffn_gate_b, L0_ffn_w1, L0_ffn_b1, L0_ffn_w2,
           L0_ffn_b2):
    import numpy as np
    import concourse.bacc as bacc
    from concourse.bass_utils import run_bass_kernel_spmd

    arrays = {
        "x": x, "src": src, "dst": dst,
        "w1t": np.asarray(L0_gnn_W1).T, "w2t": np.asarray(L0_gnn_W2).T, "gb1": L0_gnn_b1, "gb2": L0_gnn_b2,
        "kw": L0_mix_kln_weight, "kb": L0_mix_kln_bias, "vw": L0_mix_vln_weight, "vb": L0_mix_vln_bias,
        "gate_w": L0_ffn_gate_w, "gate_b": L0_ffn_gate_b,
        "f1": L0_ffn_w1, "fb1": L0_ffn_b1, "f2": L0_ffn_w2, "fb2": L0_ffn_b2,
    }
    arrays = {name: np.ascontiguousarray(a) for name, a in arrays.items()}
    nc = bacc.Bacc("TRN2", target_bir_lowering=False, num_devices=1)
    args = {name: nc.dram_tensor(name, a.shape, mybir.dt.from_np(a.dtype), kind="ExternalInput").ap()
            for name, a in arrays.items()}
    out = nc.dram_tensor("out", (N, D), F32, kind="ExternalOutput").ap()
    build_program(nc, **args, out=out)
    r = run_bass_kernel_spmd(nc, [arrays], core_ids=[0])
    return r.results[0]["out"]
```

```python
from contextlib import ExitStack

import concourse.bass as bass
from concourse import mybir

ALU = mybir.AluOpType
ACT = mybir.ActivationFunctionType
AX = mybir.AxisListType
F32 = mybir.dt.float32
F16 = mybir.dt.float16
BF16 = mybir.dt.bfloat16
I32 = mybir.dt.int32
U32 = mybir.dt.uint32
U16 = mybir.dt.uint16
ds = bass.ds

P = 128
N, D = 6250, 256
NB = -(-N // P)
LASTROWS = N - (NB - 1) * P
LD = 4
E = 100000
EP = 125
EC = E // EP
HEADS, HC = 8, 32
NX, F = 8, 1024
FT = F // P
CAP = 977
TM, TQ = 123, 4
HALF = TM * TQ
CAPR = 2 * HALF
PARTS = 2048.0
QR = 4
GR = 16
SR = 4
KR = 8
CW = 4
CU = 16
AGW = D + 1
LN_EPS, HEAD_EPS = 1e-5, 1e-5


def chunk_plan():
    plan, c0, t0 = [], 0, 0
    for cols in (128, 416, 256):
        tiles = (cols * EP + NB * (P - 1)) // P
        tiles = -(-tiles // GR) * GR
        plan.append((c0, cols, t0, tiles))
        c0 += cols
        t0 += tiles
    assert c0 == EC
    return plan


CHUNKS = chunk_plan()
TILES = sum(c[3] for c in CHUNKS)
WMAX = max(c[1] for c in CHUNKS)
TMAX = max(c[3] for c in CHUNKS)
B7 = 7
NQ = 7
XR = 4
assert NB % NQ == 0 and NB // NQ % 2 == 1 and CAPR >= CAP and EP * EC == E and TMAX <= 512 and NB % B7 == 0


def phases():
    out, heads, late = [], NB // LD, NB // LD + 1
    for c, (_, cols, _, _) in enumerate(CHUNKS):
        left = CHUNKS[c - 1][3] // GR if c else 0
        sorts = cols // CU
        out += [(c, "count", NB // B7, 0, False), (c, "place", 1, 0, False),
                (c, "rank", NB // B7, min(left, 1), left > 0), (c, "split", 1, 0, False)]
        left -= min(left, NB // B7)
        early = heads + 1 - (CHUNKS[-1][3] // GR - late) if c == len(CHUNKS) - 1 else 0
        with_sort = left - early
        assert with_sort <= sorts and early != 1
        if with_sort:
            out += [(c, "sort", with_sort - 1, 1, True), (c, "sort", 1, 1, early > 0)]
        if early > 0:
            out += [(c, "heads", early - 1, 1, True), (c, "heads", 1, 1, False)]
            heads -= early
        out += [(c, "sort", sorts - with_sort, 0, False), (c, "decode", 1, 0, False)]
    last = len(CHUNKS)
    return out + [(last, "heads", heads, 1, True), (last, "tail", 1, 1, True), (last, "kv", 1, 0, False),
                  (last, "own", late - 1, 1, True), (last, "own", 1, 1, False)]


PHASES = phases()


class Tally:

    def __init__(self, sem):
        self.sem, self.base, self.i, self.k, self.j = sem, 0, 0, 0, 0

    def loop(self, i, k):
        self.base, self.i, self.k, self.j = self.base + self.j, i, k, 0

    def end(self, n):
        assert self.j == self.k, (self.sem, self.j, self.k)
        self.base, self.i, self.k, self.j = self.base + n * self.k, 0, 0, 0

    def add(self, ins):
        ins.then_inc(self.sem, 1)
        self.j += 1

    def value(self, back=0):
        return self.i * self.k + (self.base + self.j - back)


def repeat(eng, n, body, first=0):
    if n == 1:
        body(first)
    elif n > 1:
        with eng.Fori(0, n) as i:
            body(i + first if first else i)


def build_program(nc, x, src, dst, w1t, w2t, gb1, gb2, kw, kb, vw, vb, gate_w, gate_b, f1, fb1, f2, fb2, out):
    dram = {
        "tab": nc.dram_tensor("xn_parts", (NB * P, 2 * D), F16, kind="Internal").ap(),
        "buf": nc.dram_tensor("expert_rows", (NX * CAPR + NB * P, D), F32, kind="Internal").ap(),
        "ybuf": nc.dram_tensor("expert_out", (NX * CAPR + P, D), F32, kind="Internal").ap(),
    }
    with ExitStack() as ctx:
        def sb(name, shape, dt):
            return ctx.enter_context(nc.sbuf_tensor(name, shape, dt))

        k = {
            "X": sb("X", [P, NB * D], F32),
            "AGG": sb("AGG", [P, NB * AGW], F32),
            "ident": sb("ident", [P, P], F32),
            "upper": sb("upper", [P, P], F32),
            "upinc": sb("upinc", [P, P], F32),
            "ones": sb("ones", [P, P], F32),
            "eps": sb("eps", [P, 1], F32),
            "W1": sb("W1", [P, 2 * D], F32),
            "W2": sb("W2", [P, 2 * D], F32),
            "brow": sb("brow", [P, D], F32),
            "gw": sb("gw", [P, 2 * NX], F32),
            "gb": sb("gb", [P, NX], F32),
            "iota8": sb("iota8", [P, NX], F32),
            "dummy": sb("spare_rows", [P, NB], F32),
            "psum": [ctx.enter_context(nc.psum_tensor(f"bank{i}", [P, 512], F32)) for i in range(8)],
            "zst": ctx.enter_context(nc.semaphore("expert_rows_zeroed")),
        }
        with ExitStack() as c:
            edges(nc, c, k, dram, x, src, dst, w1t, w2t, gb1, gb2, kw, kb, vw, vb, gate_w, gate_b)
        with ExitStack() as c2:
            k["gidx"] = c2.enter_context(nc.sbuf_tensor("gidx", [P, NB], I32))
            k["kp"] = c2.enter_context(nc.sbuf_tensor("kp", [P, NB], F32))
            with ExitStack() as c:
                nodes(nc, c, k, dram, x)
            with ExitStack() as c:
                experts(nc, c, k, dram, f1, fb1, f2, fb2)
            with ExitStack() as c:
                outputs(nc, c, k, dram, out)


def edges(nc, ctx, kk, dram, x, src, dst, w1t, w2t, gb1, gb2, kw, kb, vw, vb, gate_w, gate_b):
    def sb(name, shape, dt):
        return ctx.enter_context(nc.sbuf_tensor(name, shape, dt))

    def sem(name):
        return ctx.enter_context(nc.semaphore(name))

    tab, buf, ybuf = dram["tab"], dram["buf"], dram["ybuf"]
    X, AGG, ident, upper, upinc, ones, eps = (kk[n] for n in ("X", "AGG", "ident", "upper", "upinc", "ones", "eps"))
    W1, W2, brow, gw, gb = (kk[n] for n in ("W1", "W2", "brow", "gw", "gb"))
    bank = kk["psum"]
    psA, psV, psP, psG, psQ = bank[0:2], bank[2:4], bank[4], bank[5:7], bank[7]
    zst = kk["zst"]

    G = sb("G", [P, GR * 2 * D], F16)
    ones16 = sb("ones16", [P, 2], F16)
    zero16 = sb("zero16", [P, P], F16)
    zero32 = sb("zero32", [P, P], F32)
    iota_i = sb("iota_i", [P, TMAX], I32)
    iota_t = sb("iota_t", [P, TMAX], F16)
    iota_1 = sb("iota_1", [P, P], F16)
    iota_b = sb("iota_b", [P, NB], F32)
    lnst = sb("lnst", [P, 2 * LD * 6], F32)
    lnmv = sb("lnmv", [P, 2 * LD * 2], F32)
    lnsd = sb("lnsd", [P, 2 * LD], F32)
    lnrs = sb("lnrs", [P, 2 * LD], F32)
    lnmr = sb("lnmr", [P, 2 * LD], F32)
    TB = G[:, 0:2 * LD * 2 * D]
    b7 = sb("b7", [P, B7], F32)
    n7 = sb("n7", [P, B7], F32)
    mask = sb("mask", [P, B7 * WMAX], BF16)
    work = sb("work", [P, 8 * EC], BF16)
    srci = work[:, 0:2 * EC].bitcast(I32)
    dsti = work[:, 2 * EC:4 * EC].bitcast(I32)
    tmpi = work[:, 4 * EC:6 * EC].bitcast(I32)
    tmpj = work[:, 6 * EC:8 * EC].bitcast(I32)
    cen = work[:, 0:2 * LD * D].bitcast(F32)
    sqr = work[:, 2 * LD * D:4 * LD * D].bitcast(F32)
    KW = P + 1
    xs, xts = cen[:, 0:2 * D], cen[:, 2 * D:4 * D]
    kn = work[:, 4 * LD * D:4 * LD * D + 2 * LD * 2 * KW].bitcast(F32)
    blk = sb("blk", [P, EC], BF16)
    v1 = sb("v1", [P, EC], F32)
    v2 = sb("v2", [P, EC], F32)
    onesw = sb("onesw", [P, WMAX], BF16)
    cum = sb("cum", [P, 2 * WMAX], F32)
    pos = sb("pos", [P, WMAX], F32)
    tf = sb("tf", [P, WMAX], F32)
    posi = cum[:, 0:WMAX].bitcast(I32)
    tli = cum[:, WMAX:2 * WMAX].bitcast(I32)
    cnt = sb("cnt", [P, NB], F32)
    mi = sb("mi", [P, 2 * NB], I32)
    mrow = sb("mrow", [P, NB], F32)
    mend = sb("mend", [P, NB], F32)
    base = sb("base", [P, NB], F32)
    mcol = sb("mcol", [P, 4], F32)
    mcoli = sb("mcoli", [P, 4], I32)
    ge = sb("ge", [P, TMAX], F16)
    LH = sb("LH", [P, KR * P], F16)
    LV = sb("LV", [P, KR * 2 * P], F16)
    HT = sb("HT", [P, KR * TMAX], F16)
    DI = sb("DI", [P, 4 * TMAX], I32)
    idx = sb("idx", [P, TILES], I32)
    srcl = sb("srcl", [P, TILES], F32)
    buck = sb("buck", [1, TILES], I32)
    idxr = sb("idxr", [P, GR], I32)
    S = sb("S", [P, SR * P], F16)
    here = sb("here", [P, 4 * GR], F32)
    srch, posh, tfh, v1h = (here[:, n * GR:(n + 1) * GR] for n in range(4))
    hv = sb("hv", [P, 2 * 2], F32)
    hrow = sb("hrow", [P, 2 * D], F32)
    b2r = sb("b2r", [P, D], F32)
    hs = sb("hs", [P, LD * HEADS], F32)
    hm = sb("hm", [P, LD * HEADS], F32)
    hq = sb("hq", [P, LD * HEADS], F32)
    hr = sb("hr", [P, LD * HEADS], F32)
    kvw = sb("kvw", [P, 6 * P], F32)

    s_par, s_edge, s_x, s_xl = sem("parameters_loaded"), sem("edges_loaded"), sem("x_loaded"), sem("x_last_loaded")
    s_pc, s_dc = sem("pool_constants"), sem("vector_constants")
    s_v = sem("vector_steps")
    s_pad = sem("x_padding_zero")
    s_nrm = sem("ln_scale")
    s_stat, s_sd, s_xn, s_hi, s_lo = sem("ln_statistics"), sem("ln_std"), sem("xn_ready"), sem("high_part"), sem("low_part")
    s_tb = [sem("parts_stored_0"), sem("parts_stored_1")]
    s_tbc = sem("parts_read")
    s_cnt, s_pre, s_mc, s_ec, s_ge, s_bk = (sem(n) for n in (
        "bucket_counts", "bucket_prefix", "tile_counts", "tile_ends", "tiles_past_ends", "tile_buckets"))
    s_lh, s_lv, s_ht, s_col, s_sx, s_dec = (sem(n) for n in (
        "lane_onehot", "lane_values", "tile_onehot", "columns_sorted", "sort_closed", "sort_read"))
    s_idx = sem("indices_ready")
    s_srch, s_posh = sem("sources_at_hand"), sem("places_at_hand")
    s_g = [sem(f"gathered_{i}") for i in range(GR)]
    s_S, s_tile, s_ev = sem("source_onehot"), sem("tile_summed"), sem("tile_added")
    s_cen, s_sq, s_ss, s_hstd, s_kn, s_kg = (sem(n) for n in (
        "heads_centred", "heads_squared", "heads_variance", "heads_std", "heads_normal", "heads_multiplied"))
    s_zero = sem("sums_zero")
    s_kv = sem("key_values_in_w1")
    s_xs, s_xt, s_xtc, s_xp, s_xa = (sem(n) for n in (
        "xn_placed", "xn_transposed", "xn_t_copied", "xn_products", "xn_products_added"))
    s_dg, s_se = sem("heads_sums_diagonal"), sem("heads_sums_row")
    s_past = sem("past_a_wait")

    block = ctx.enter_context(nc.Block())
    PAR = 16 * 16

    @block.sync
    def _(sp):
        sp.dma_start(srci[0:EP, :], src.rearrange("(p t) -> p t", p=EP)).then_inc(s_edge, 16)
        sp.dma_start(dsti[0:EP, :], dst.rearrange("(p t) -> p t", p=EP)).then_inc(s_edge, 16)
        sp.wait_ge(s_pad, 1)
        sp.dma_start(X[0:LASTROWS, (NB - 1) * D:NB * D], x[(NB - 1) * P:N, :]).then_inc(s_xl, 16)

        sp.sem_inc(s_x, 16)
        with sp.Fori(0, NB // (2 * LD)) as i:
            sp.wait_ge(s_x, i * 16 + 16)
            sp.dma_start(X[:, ds(i * (2 * LD * D), 2 * LD * D)].rearrange("p (j d) -> p j d", d=D),
                         x[ds(i * (2 * LD * P), 2 * LD * P), :].rearrange("(j p) d -> p j d", p=P)).then_inc(s_x, 16)
        sp.wait_ge(s_zero, 1)
        sp.wait_ge(s_tb[0], 16 * (NB // (2 * LD) + 1))
        half = 31 * P
        for j in range(2):
            sp.dma_start(buf[j * half:(j + 1) * half, :].rearrange("(p r) d -> p (r d)", p=P),
                         AGG[:, 0:31 * D]).then_inc(zst, 16)
        sp.dma_start(ybuf[NX * CAPR:NX * CAPR + P, :], AGG[:, 0:D]).then_inc(zst, 16)
        sp.wait_ge(zst, 48)

    @block.gpsimd
    def _(pool):
        pool.iota(iota_i[:, :], [[1, TMAX]], base=0, channel_multiplier=0).then_inc(s_pc, 1)
        pool.memset(ones[:, :], 1.0).then_inc(s_pc, 1)
        pool.memset(ident[:, :], 0.0).then_inc(s_pc, 1)
        pool.wait_ge(s_pc, 3)
        pool.affine_select(out=ident[:, :], in_=ident[:, :], compare_op=ALU.not_equal, fill=1.0, base=0,
                           pattern=[[-1, P]], channel_multiplier=1).then_inc(s_pc, 1)
        pool.affine_select(out=upper[:, :], in_=ones[:, :], compare_op=ALU.is_gt, fill=0.0, base=0,
                           pattern=[[1, P]], channel_multiplier=-1).then_inc(s_pc, 1)
        pool.affine_select(out=upinc[:, :], in_=ones[:, :], compare_op=ALU.is_ge, fill=0.0, base=0,
                           pattern=[[1, P]], channel_multiplier=-1).then_inc(s_pc, 1)
        pool.iota(mi[:, 0:NB], [[P, NB]], base=NX * CAPR, channel_multiplier=1).then_inc(s_pc, 1)

        def store(h, nb, rows, low):
            pool.wait_ge(s_lo, low)
            o = h * LD * 2 * D
            pool.dma_start(tab[rows, :].rearrange("(j p) d -> p j d", p=P),
                           TB[:, o:o + nb * 2 * D].rearrange("p (j d) -> p j d", j=nb)).then_inc(s_tb[h], 16)

        with pool.Fori(0, NB // (2 * LD)) as i:
            for h in range(2):
                store(h, LD, ds((i * 2 + h) * (LD * P), LD * P), i * 2 + (h + 1))
        n = NB // (2 * LD)
        store(0, 1, slice((NB - 1) * P, NB * P), 2 * n + 1)
        pool.wait_ge(s_tb[0], 16 * (n + 1))
        pool.wait_ge(s_tb[1], 16 * n)

        g0 = 0
        for c, step, its, groups, _ in PHASES:
            if not groups:
                continue

            def gather(i, g0=g0):
                for s in range(GR):
                    if s % QR == 0:
                        pool.wait_ge(s_idx, i * (GR // QR) + (GR // QR * g0 + s // QR + 1))
                        pool.wait_ge(s_tile, i * GR + (GR * g0 + s + QR))
                        pool.sem_inc(s_past, 1)
                    pool.indirect_dma_start(G[:, s * 2 * D:(s + 1) * 2 * D], None, tab,
                                            bass.IndirectOffsetOnAxis(ap=idxr[:, s:s + 1], axis=0)).then_inc(s_g[s], 16)
            repeat(pool, its, gather)
            g0 += its

    @block.scalar
    def _(act):
        for a, b in ((W1, w1t), (W2, w2t)):
            act.dma_start(a[:, :].rearrange("p (k o) -> p k o", k=2), b.rearrange("(k p) o -> p k o", p=P)).then_inc(s_par, 16)
        act.dma_start(brow[:, :], gb1.rearrange("(a n) -> a n", a=1).partition_broadcast(P)).then_inc(s_par, 16)
        act.dma_start(b2r[:, :], gb2.rearrange("(a n) -> a n", a=1).partition_broadcast(P)).then_inc(s_par, 16)
        act.dma_start(gw[:, :].rearrange("p (k o) -> p k o", k=2), gate_w.rearrange("(k p) o -> p k o", p=P)).then_inc(s_par, 16)
        act.dma_start(gb[:, :], gate_b.rearrange("(a n) -> a n", a=1).partition_broadcast(P)).then_inc(s_par, 16)
        for n, col in enumerate((kw, kb)):
            flat = col.rearrange("h a c -> (h a c)").rearrange("(k p a) -> k p a", k=2, a=1)
            for h in range(2):
                act.dma_start(hv[:, 2 * h + n:2 * h + n + 1], flat[h]).then_inc(s_par, 16)
        for n, row in enumerate((vw, vb)):
            act.dma_start(hrow[:, n * D:(n + 1) * D],
                          row.rearrange("h a c -> a (h c)").partition_broadcast(P)).then_inc(s_par, 16)
        act.wait_ge(s_dc, 1)

        def std(h, nb, k):
            act.wait_ge(s_stat, k)
            act.activation(lnsd[:, h * LD:h * LD + nb], lnmv[:, 2 * h * LD + 1:2 * (h * LD + nb):2], ACT.Sqrt,
                           bias=eps[:, :]).then_inc(s_sd, 1)

        def normal(h, nb, at, k, last):
            act.wait_ge(s_nrm, k)
            act.sem_inc(s_past, 1)
            for j in range(nb):
                q = h * LD + j
                ins = act.activation(X[:, at(j)], X[:, at(j)], ACT.Identity, bias=lnmr[:, q:q + 1], scale=lnrs[:, q:q + 1])
            ins.then_inc(s_xn, 1)
            act.wait_ge(s_xn, k)
            if last is not None:
                act.wait_ge(s_tb[h], last)
            act.sem_inc(s_past, 1)
            o = h * LD * 2 * D
            act.activation(TB[:, o:o + nb * 2 * D].rearrange("p (j d) -> p j d", j=nb)[:, :, 0:D],
                           X[:, at(None)].rearrange("p (j d) -> p j d", j=nb), ACT.Copy, scale=PARTS).then_inc(s_hi, 1)

        n = NB // (2 * LD)

        def pair(i, first):
            for h in range(2):
                std(h, LD, i * 2 + (h + 1))
            for h in range(2):
                o = (i * 2 + h) * (LD * D)
                normal(h, LD, lambda j: ds(o, LD * D) if j is None else ds(o + j * D, D), i * 2 + (h + 1),
                       None if first else i * 16)
        pair(0, True)
        with act.Fori(1, n) as i:
            pair(i, False)
        std(0, 1, 2 * n + 1)
        normal(0, 1, lambda j: slice((NB - 1) * D, NB * D), 2 * n + 1, 16 * n)

        k0, m0, b0 = 0, 0, 0
        for c, step, its, groups, _ in PHASES:
            if step == "sort":
                c0 = CHUNKS[c][0]

                def values(i, k0=k0, groups=groups):
                    for j in range(CU):
                        q = j % KR
                        col = i * CU + (k0 + j)
                        if j % CW == 0:
                            act.wait_ge(s_lh, col + CW)
                        for n, v in enumerate((v1, v2)):
                            if n == 0 and not groups and j % 2:
                                continue
                            ins = act.activation(LV[0:EP, (2 * q + n) * P:(2 * q + n + 1) * P], LH[0:EP, q * P:(q + 1) * P],
                                                 ACT.Copy, scale=v[0:EP, ds(col, 1)])
                        ins.then_inc(s_lv, 1)
                repeat(act, its, values)
                k0 += its * CU
            elif step in ("heads", "tail"):
                nb = LD if step == "heads" else 1

                def heads(i, m0=m0, nb=nb):
                    act.wait_ge(s_cen, i + (m0 + 1))
                    act.activation(sqr[:, 0:nb * D], cen[:, 0:nb * D], ACT.Square).then_inc(s_sq, 1)
                    act.wait_ge(s_ss, i + (m0 + 1))
                    act.activation(hq[:, 0:nb * HEADS], hq[:, 0:nb * HEADS], ACT.Sqrt, scale=1.0 / (HC - 1)).then_inc(s_hstd, 1)
                repeat(act, its, heads)
                m0 += its
            elif step == "kv":
                act.wait_ge(s_kv, 1)
            elif step == "own":
                def own(i, b0=b0, nb=LD if its > 1 else 1):
                    for j in range(nb):
                        h, b = j % 2, i * LD + (b0 + j)
                        act.wait_ge(s_xt, b + 1)
                        act.activation(xs[:, h * D:(h + 1) * D], X[:, ds(b * D, D)], ACT.Copy).then_inc(s_xs, 1)
                        act.wait_ge(s_xt, b + 3)
                        act.wait_ge(s_xp, b + 1)
                        act.activation(xts[:, h * D:(h + 1) * D], psV[h][:, 0:D], ACT.Copy).then_inc(s_xtc, 1)
                repeat(act, its, own)
                b0 += its * LD

    @block.tensor
    def _(pe):
        pe.wait_ge(s_pc, 7)
        pe.wait_ge(s_dc, 2)
        pe.sem_inc(s_col, KR)
        pe.sem_inc(s_tile, GR)
        pe.sem_inc(s_kg, 1)
        pe.sem_inc(s_xt, 2)
        pe.sem_inc(s_xp, 2)
        t0, k0, m0, b0 = 0, 0, 0, 0
        for c, step, its, groups, _ in PHASES:
            if step == "place":
                _, cols, ch0, tiles = CHUNKS[c]
                pe.wait_ge(s_cnt, c + 1)
                pe.matmul(psP[:, 0:NB], upper[0:EP, :], cnt[0:EP, :], start=True, stop=True)
                pe.matmul(psP[:, 64:64 + NB], ones[0:EP, :], cnt[0:EP, :], start=True, stop=True)
                pe.matmul(psQ[0:NB, 0:1], cnt[0:EP, :], ones[0:EP, 0:1], start=True, stop=True).then_inc(s_pre, 1)
                pe.wait_ge(s_mc, c + 1)
                pe.matmul(psQ[0:NB, 0:1], upinc[0:NB, 0:NB], mcol[0:NB, 0:1], start=True, stop=True).then_inc(s_ec, 1)
                pe.wait_ge(s_ge, c + 1)
                pe.matmul(psQ[0:1, 0:tiles], ones16[0:NB, 0:1], ge[0:NB, 0:tiles], start=True, stop=True).then_inc(s_bk, 1)
                if c:
                    pe.wait_ge(s_dec, c)
                for n in range(2):
                    pe.matmul(psV[n][:, 0:tiles], zero16[0:EP, :], iota_t[0:EP, 0:tiles], start=True, stop=False,
                              skip_group_check=True)

            def tiles_of(i, s, t0=t0):
                t = i * GR + (t0 + s)
                q = s % SR
                pe.wait_ge(s_g[s], (i + (t0 // GR + 1)) * 16)
                pe.wait_ge(s_S, t + 1)
                pe.wait_ge(s_ev, t + 1)
                lhs = S[:, q * P:(q + 1) * P]
                o = s * 2 * D
                pe.matmul(psA[s % 2][:, 0:D], lhs, G[:, o:o + D], start=True, stop=False)
                pe.matmul(psA[s % 2][:, 0:D], lhs, G[:, o + D:o + 2 * D], start=False, stop=True)
                pe.matmul(psA[s % 2][:, D:D + 1], lhs, ones16[:, 0:1], start=True, stop=True).then_inc(s_tile, 1)

            def column(i, j, k0=k0, tiles=CHUNKS[min(c, len(CHUNKS) - 1)][3]):
                q = j % KR
                col = i * CU + (k0 + j)
                if j % CW == 0:
                    pe.wait_ge(s_lv, col + CW)
                    pe.wait_ge(s_ht, col + (CW + GR))
                for n in range(2):
                    ins = pe.matmul(psV[n][:, 0:tiles], LV[0:EP, (2 * q + n) * P:(2 * q + n + 1) * P],
                                    HT[0:EP, q * TMAX:q * TMAX + tiles], start=False, stop=False, skip_group_check=True)
                ins.then_inc(s_col, 1)

            def products(pieces):
                for piece in pieces:
                    for j, h in ((piece // 2, piece % 2),):
                        o = (j * 2 + h) * KW
                        ins = pe.matmul(psG[h][:, 0:KW], kn[:, o:o + P], kn[:, o:o + KW], start=False, stop=False,
                                        skip_group_check=True)
                return ins

            if step == "heads" and m0 == 0:
                pe.wait_ge(s_par, 16 * 12)
                for h in range(2):
                    pe.matmul(psG[h][:, 0:KW], zero32[:, :], W1[:, 0:KW], start=True, stop=False,
                              skip_group_check=True)

            def own(i, s, b0=b0):
                h, b = s // 4 % 2, i * LD + (b0 + s // 4)
                if s % 4 == 0:
                    pe.wait_ge(s_xs, b + 1)
                    pe.wait_ge(s_xtc, b + 1)
                    for n in range(2):
                        ins = pe.transpose(psV[h][:, n * P:(n + 1) * P], xs[:, h * D + n * P:h * D + (n + 1) * P], ident[:, :])
                    ins.then_inc(s_xt, 1)
                elif s % 4 == 2:
                    pe.wait_ge(s_xtc, b + 3)
                    pe.wait_ge(s_xa, b + 1)
                    for n in range(2):
                        ins = pe.matmul(psG[h][:, 0:D], xts[:, h * D + n * P:h * D + (n + 1) * P],
                                        W1[:, n * D:(n + 1) * D], start=(n == 0), stop=(n == 1))
                    ins.then_inc(s_xp, 1)

            def body(i, step=step, groups=groups, its=its):
                for s in range(GR if groups or step == "sort" else 0):
                    if groups:
                        tiles_of(i, s)
                    if step == "own" and s < 4 * (LD if its > 1 else 1):
                        own(i, s)
                    if step == "sort":
                        column(i, s)
                    if step in ("heads", "tail") and s >= 10:
                        pieces = (1 if step == "tail" else LD) * 2
                        per = -(-pieces // 6)
                        if s == 10:
                            pe.wait_ge(s_kn, i + (m0 + 1))
                        mine = range(min((s - 10) * per, pieces), min((s - 9) * per, pieces))
                        if mine:
                            ins = products(mine)
                            if mine[-1] == pieces - 1:
                                ins.then_inc(s_kg, 1)

            if step == "kv":
                for h in range(2):
                    ins = pe.matmul(psG[h][:, 0:KW], zero32[:, :], W1[:, 0:KW], start=False, stop=True,
                                    skip_group_check=True)
                ins.then_inc(s_kg, 1)
                for h in range(2):
                    pe.wait_ge(s_dg, h + 1)
                    pe.matmul(psP[:, h * P:(h + 1) * P], ones[:, :], kvw[:, (4 + h) * P:(5 + h) * P], start=True,
                              stop=True).then_inc(s_se, 1)
                pe.wait_ge(s_kv, 1)
            if groups or step == "sort":
                repeat(pe, its, body)
                b0 += its * LD if step == "own" else 0
                t0 += its * GR * groups
                k0 += its * CU if step == "sort" else 0
                m0 += its if step in ("heads", "tail") else 0
            if step == "decode":
                for n in range(2):
                    ins = pe.matmul(psV[n][:, 0:CHUNKS[c][3]], zero16[0:EP, :], iota_t[0:EP, 0:CHUNKS[c][3]],
                                    start=False, stop=True, skip_group_check=True)
                ins.then_inc(s_sx, 1)

    @block.vector
    def _(v):
        step_count = Tally(s_v)
        step = step_count.add

        def wait(back=0):
            v.wait_ge(s_v, step_count.value(back))

        v.memset(eps[:, :], LN_EPS).then_inc(s_dc, 1)
        v.memset(X[:, (NB - 1) * D:NB * D], 0.0).then_inc(s_pad, 1)
        v.memset(zero16[:, :], 0.0)
        v.memset(zero32[:, :], 0.0)
        v.memset(ones16[:, :], 1.0)
        v.memset(onesw[:, :], 1.0)
        v.memset(pos[:, :], 0.0)
        v.wait_ge(s_pc, 7)
        v.tensor_copy(iota_t[:, :], iota_i[:, :])
        v.tensor_scalar(iota_1[:, :], iota_i[:, 0:P], 1.0, None, ALU.add)
        v.tensor_copy(iota_b[:, :], iota_i[:, 0:NB])
        v.tensor_copy(kk["dummy"][:, :], mi[:, 0:NB])
        v.tensor_scalar(kk["iota8"][:, :], iota_i[:, 0:NX], -1.0, float(NX), ALU.mult, ALU.add)
        v.memset(LH[:, :], 0.0).then_inc(s_dc, 1)
        v.memset(AGG[:, :], 0.0).then_inc(s_zero, 1)
        v.sem_inc(s_ht, GR)
        v.sem_inc(s_ev, 2)

        def stats(h, nb, at):
            for j in range(nb):
                q = h * LD + j
                step(v.bn_stats(lnst[:, 6 * q:6 * q + 6], X[:, at(j)]))
            wait()
            v.sem_inc(s_past, 1)
            for j in range(nb):
                q = h * LD + j
                ins = v.bn_aggr(lnmv[:, 2 * q:2 * q + 2], lnst[:, 6 * q:6 * q + 6])
            ins.then_inc(s_stat, 1)

        def scale(h, nb, k):
            v.wait_ge(s_sd, k)
            step(v.reciprocal(lnrs[:, h * LD:h * LD + nb], lnsd[:, h * LD:h * LD + nb]))
            wait()
            v.scalar_tensor_tensor(out=lnmr[:, h * LD:h * LD + nb], in0=lnmv[:, 2 * h * LD:2 * (h * LD + nb):2],
                                   scalar=-1.0, in1=lnrs[:, h * LD:h * LD + nb], op0=ALU.mult, op1=ALU.mult).then_inc(s_nrm, 1)

        def low(h, nb, at, k):
            v.wait_ge(s_hi, k)
            o = h * LD * 2 * D
            tb = TB[:, o:o + nb * 2 * D].rearrange("p (j d) -> p j d", j=nb)
            v.scalar_tensor_tensor(out=tb[:, :, D:2 * D], in0=X[:, at].rearrange("p (j d) -> p j d", j=nb),
                                   scalar=PARTS, in1=tb[:, :, 0:D], op0=ALU.mult, op1=ALU.subtract).then_inc(s_lo, 1)

        n = NB // (2 * LD)

        def pair(i, back):
            v.wait_ge(s_x, i * 16 + 32)
            for h in range(2):
                stats(h, LD, lambda j: ds(i * (2 * LD * D) + (h * LD + j) * D, D))
            if back:
                for h in range(2):
                    low(h, LD, ds(i * (2 * LD * D) + (h - 2) * (LD * D), LD * D), i * 2 + (h - 1))
            for h in range(2):
                scale(h, LD, i * 2 + (h + 1))
        pair(0, False)
        with v.Fori(0, n - 1) as i:
            step_count.loop(i, 2 * LD + 2)
            pair(i + 1, True)
        step_count.end(n - 1)
        v.wait_ge(s_xl, 16)
        stats(0, 1, lambda j: slice((NB - 1) * D, NB * D))
        scale(0, 1, 2 * n + 1)
        for h in range(2):
            low(h, LD, slice((2 * n - 2 + h) * LD * D, (2 * n - 1 + h) * LD * D), 2 * n - 1 + h)
        low(0, 1, slice((NB - 1) * D, NB * D), 2 * n + 1)

        v.wait_ge(s_edge, 32)
        step(v.tensor_scalar(tmpi[0:EP, :], srci[0:EP, :], 7, None, ALU.logical_shift_right))
        step(v.tensor_scalar(tmpj[0:EP, :], dsti[0:EP, :], 3, None, ALU.logical_shift_right))
        wait()
        v.tensor_copy(blk[0:EP, :], tmpi[0:EP, :])
        step(v.tensor_copy(v1[0:EP, :], tmpj[0:EP, :]))
        wait()
        v.tensor_scalar(tmpi[0:EP, :], srci[0:EP, :], P - 1, None, ALU.bitwise_and)
        step(v.tensor_scalar(tmpj[0:EP, :], dsti[0:EP, :], 7, None, ALU.bitwise_and))
        wait()
        step(v.tensor_scalar(v2[0:EP, :], tmpj[0:EP, :], 256.0, 1.0, ALU.mult, ALU.add))
        wait()
        step(v.tensor_tensor(v2[0:EP, :], v2[0:EP, :], tmpi[0:EP, :], ALU.add))
        wait()

        def source_onehot(i, s, t0):
            q = s % SR
            v.tensor_scalar(S[:, q * P:(q + 1) * P], iota_1[:, :], srch[:, s:s + 1], None, ALU.is_equal).then_inc(s_S, 1)

        offsets = []

        def add_tile(i, s, t0):
            t = i * GR + (t0 + s)
            v.wait_ge(s_tile, t + (GR + 1))
            v.wait_ge(s_ev, t + 2)
            o = offsets[s]
            v.tensor_tensor(AGG[:, ds(o, AGW)], AGG[:, ds(o, AGW)], psA[s % 2][:, 0:AGW], ALU.add).then_inc(s_ev, 1)

        def fetch(i, k, g0):
            v.tensor_copy(idxr[:, QR * k:QR * k + QR], idx[:, ds(i * GR + (g0 * GR + QR * k), QR)]).then_inc(s_idx, 1)

        def tile(i, s, t0, ahead):
            if s == 0:
                offsets[:] = nc.values_load_multi_w_load_instructions(
                    buck[0:1, ds(i * GR + t0, GR)], engines=[mybir.EngineType.DVE], min_val=0, max_val=(NB - 1) * AGW,
                    skip_runtime_bounds_check_because="the place step clamps the tiles' blocks to NB - 1")[1]
                v.tensor_copy(srch, srcl[:, ds(i * GR + t0, GR)]).then_inc(s_srch, 1)
                v.wait_ge(s_srch, i + (t0 // GR + 1))
                source_onehot(i, 0, t0)
                source_onehot(i, 1, t0)
            if s + 2 < GR:
                source_onehot(i, s + 2, t0)
            add_tile(i, s, t0)
            if ahead and s % QR == QR - 1:
                fetch(i, s // QR, t0 // GR + 1)

        v.sem_inc(s_xtc, 2)
        v.sem_inc(s_xa, 2)
        t0, k0, m0, b0 = 0, 0, 0, 0
        v.memset(kn[:, P:LD * 2 * KW:KW], 1.0)
        for c, name, its, groups, ahead in PHASES:
            if c < len(CHUNKS):
                c0, cols, ch0, tiles = CHUNKS[c]
            if name == "count":
                if c == 1:
                    v.wait_ge(zst, 48)

                def count(i):
                    step(v.tensor_copy(b7[0:EP, :], iota_b[0:EP, ds(i * B7, B7)]))
                    wait()
                    for j in range(B7):
                        o = j * WMAX
                        ins = v.tensor_scalar(mask[0:EP, o:o + cols], blk[0:EP, c0:c0 + cols], b7[0:EP, j:j + 1], 0.0,
                                              ALU.is_equal, ALU.add, accum_out=n7[0:EP, j:j + 1])
                    step(ins)
                    wait()
                    step(v.tensor_copy(cnt[0:EP, ds(i * B7, B7)], n7[0:EP, :]))
                with v.Fori(0, its) as i:
                    step_count.loop(i, 3)
                    count(i)
                step_count.end(its)
                v.wait_ge(s_v, step_count.value())
                step(v.memset(mcol[:, :], 0.0))
                wait()
                v.memset(mcoli[:, :], 0).then_inc(s_cnt, 1)
            elif name == "place":
                v.wait_ge(s_pre, c + 1)
                v.tensor_scalar(mi[:, 0:NB], psP[:, 64:64 + NB], float(P - 1), None, ALU.add)
                step(v.tensor_scalar(mcoli[0:NB, 0:1], psQ[0:NB, 0:1], float(P - 1), None, ALU.add))
                wait()
                v.tensor_scalar(mi[:, NB:2 * NB], mi[:, 0:NB], 7, None, ALU.logical_shift_right)
                step(v.tensor_scalar(mcoli[0:NB, 1:2], mcoli[0:NB, 0:1], 7, None, ALU.logical_shift_right))
                wait()
                step(v.tensor_copy(mrow[:, :], mi[:, NB:2 * NB]))
                v.tensor_copy(mcol[0:NB, 0:1], mcoli[0:NB, 1:2]).then_inc(s_mc, 1)
                wait()
                step(v.tensor_tensor_scan(mend[:, :], ones[:, 0:NB], mrow[:, :], 0.0, ALU.mult, ALU.add))
                wait()
                step(v.tensor_tensor(mrow[:, :], mend[:, :], mrow[:, :], ALU.subtract))
                wait()
                step(v.scalar_tensor_tensor(out=base[0:EP, :], in0=mrow[0:EP, :], scalar=float(P), in1=psP[0:EP, 0:NB],
                                            op0=ALU.mult, op1=ALU.add))
                wait()
                step(v.tensor_scalar(base[0:EP, :], base[0:EP, :], -1.0, None, ALU.add))
                v.wait_ge(s_ec, c + 1)
                step(v.tensor_copy(mcol[0:NB, 2:3], psQ[0:NB, 0:1]))
                wait()
                v.tensor_scalar(ge[0:NB, 0:tiles], iota_t[0:NB, 0:tiles], mcol[0:NB, 2:3], None, ALU.is_ge).then_inc(s_ge, 1)
                v.wait_ge(s_bk, c + 1)
                step(v.tensor_scalar(buck[0:1, ch0:ch0 + tiles], psQ[0:1, 0:tiles], float(NB - 1), float(AGW),
                                     ALU.min, ALU.mult))
                wait()
            elif name == "rank":
                def rank(i, groups=groups, ahead=ahead, t0=t0):
                    wait()
                    v.tensor_copy(b7[0:EP, :], iota_b[0:EP, ds(i * B7, B7)])
                    step(v.tensor_copy(n7[0:EP, :], base[0:EP, ds(i * B7, B7)]))
                    wait()
                    for j in range(B7):
                        ins = v.tensor_scalar(mask[0:EP, j * WMAX:j * WMAX + cols], blk[0:EP, c0:c0 + cols], b7[0:EP, j:j + 1],
                                              None, ALU.is_equal)
                    step(ins)
                    for j in range(B7 + 1):
                        wait()
                        if j:
                            q = (j - 1) % 2
                            m = mask[0:EP, (j - 1) * WMAX:(j - 1) * WMAX + cols]
                            v.sem_inc(s_past, 1)
                            step(v.copy_predicated(pos[0:EP, 0:cols], m.bitcast(U16), cum[0:EP, q * WMAX:q * WMAX + cols]))
                        if j < B7:
                            q = j % 2
                            step(v.tensor_tensor_scan(cum[0:EP, q * WMAX:q * WMAX + cols], onesw[0:EP, 0:cols],
                                                      mask[0:EP, j * WMAX:j * WMAX + cols], n7[0:EP, j:j + 1], ALU.mult, ALU.add))
                        if groups:
                            for s in range(2 * j, 2 * j + 2):
                                tile(i, s, t0, ahead)
                with v.Fori(0, its) as i:
                    step_count.loop(i, 2 + 2 * B7)
                    rank(i)
                step_count.end(its)
            elif name == "split":
                wait()
                step(v.tensor_copy(posi[0:EP, 0:cols], pos[0:EP, 0:cols]))
                wait()
                step(v.tensor_scalar(tli[0:EP, 0:cols], posi[0:EP, 0:cols], 7, None, ALU.logical_shift_right))
                wait()
                step(v.tensor_copy(tf[0:EP, 0:cols], tli[0:EP, 0:cols]))
                wait()
                step(v.tensor_scalar(tli[0:EP, 0:cols], posi[0:EP, 0:cols], P - 1, None, ALU.bitwise_and))
                wait()
                step(v.tensor_copy(pos[0:EP, 0:cols], tli[0:EP, 0:cols]))
                wait()
            elif name == "sort":
                def sort(i, groups=groups, ahead=ahead, t0=t0, k0=k0):
                    v.wait_ge(s_ht, i * CU + (k0 + GR))
                    v.tensor_copy(posh[0:EP, :], pos[0:EP, ds(i * CU + (k0 - c0), CU)])
                    if not groups:
                        v.tensor_copy(v1h[0:EP, :], v1[0:EP, ds(i * CU + k0, CU)])
                    v.tensor_copy(tfh[0:EP, :], tf[0:EP, ds(i * CU + (k0 - c0), CU)]).then_inc(s_posh, 1)
                    v.wait_ge(s_posh, i + (k0 // CU + 1))

                    def operands(j):
                        if j % CW == 0:
                            v.wait_ge(s_col, i * CU + (k0 + j + CW))
                        for n in range(j, j + CW):
                            q = n % KR
                            v.tensor_scalar(LH[0:EP, q * P:(q + 1) * P], iota_t[0:EP, 0:P],
                                            posh[0:EP, n:n + 1], None, ALU.is_equal).then_inc(s_lh, 1)
                        for n in range(j + 1, j + CW, 2) if not groups else ():
                            q = n % KR
                            v.tensor_scalar(LV[0:EP, 2 * q * P:(2 * q + 1) * P], iota_t[0:EP, 0:P],
                                            posh[0:EP, n:n + 1], v1h[0:EP, n:n + 1], ALU.is_equal, ALU.mult)
                        for n in range(j, j + CW):
                            q = n % KR
                            v.tensor_scalar(HT[0:EP, q * TMAX:q * TMAX + tiles], iota_t[0:EP, 0:tiles],
                                            tfh[0:EP, n:n + 1], None, ALU.is_equal).then_inc(s_ht, 1)

                    operands(0)
                    for j in range(CU):
                        if groups:
                            if j % CW == 0 and j + CW < CU:
                                operands(j + CW)
                            tile(i, j, t0, ahead)
                        elif j % CW == 0 and j:
                            operands(j)
                repeat(v, its, sort)
            elif name == "decode":
                v.wait_ge(s_sx, c + 1)
                a, b, d, e = (DI[:, n * TMAX:n * TMAX + tiles] for n in range(4))
                v.tensor_copy(a, psV[0][:, 0:tiles])
                step(v.tensor_copy(b, psV[1][:, 0:tiles]))
                wait()
                v.tensor_scalar(d, a, 3, None, ALU.logical_shift_left)
                step(v.tensor_scalar(e, b, 8, None, ALU.logical_shift_right))
                wait()
                step(v.tensor_tensor(idx[:, ch0:ch0 + tiles], d, e, ALU.bitwise_or))
                step(v.tensor_scalar(a, b, 255, None, ALU.bitwise_and))
                wait()
                v.tensor_copy(srcl[:, ch0:ch0 + tiles], a).then_inc(s_dec, 1)
                v.wait_ge(s_dec, c + 1)
                v.wait_ge(s_tile, ch0 + GR)
                for n in range(GR // QR):
                    fetch(0, n, ch0 // GR)
            elif name in ("heads", "tail"):
                nb = LD if name == "heads" else 1
                nh = nb * HEADS

                def heads(i, s):
                    w = slice(0, nb * D)
                    h3 = lambda ap: ap.rearrange("p (g d) -> p g d", d=HC)
                    wide = lambda ap: ap.unsqueeze(2).to_broadcast([P, nh, HC])
                    xb = X[:, ds((i + m0) * (LD * D), nb * D)] if name == "heads" else X[:, m0 * LD * D:m0 * LD * D + nb * D]
                    if s == 0:
                        step(v.tensor_reduce(hs[:, 0:nh], h3(xb), AX.X, ALU.add))
                    elif s == 1:
                        wait()
                        step(v.tensor_scalar(hm[:, 0:nh], hs[:, 0:nh], 1.0 / HC, None, ALU.mult))
                    elif s == 2:
                        wait()
                        v.tensor_tensor(h3(cen[:, w]), h3(xb), wide(hm[:, 0:nh]), ALU.subtract).then_inc(s_cen, 1)
                    elif s == 4:
                        v.wait_ge(s_sq, i + (m0 + 1))
                        v.tensor_reduce(hq[:, 0:nh], h3(sqr[:, w]), AX.X, ALU.add).then_inc(s_ss, 1)
                    elif s == 6:
                        v.wait_ge(s_hstd, i + (m0 + 1))
                        step(v.tensor_scalar(hs[:, 0:nh], hq[:, 0:nh], HEAD_EPS, None, ALU.add))
                    elif s == 7:
                        wait()
                        step(v.reciprocal(hr[:, 0:nh], hs[:, 0:nh]))
                    elif s == 8:
                        wait()
                        v.wait_ge(s_kg, i + (m0 + 1))
                        v.tensor_tensor(kn[:, 0:nb * 2 * KW].rearrange("p (k w) -> p k w", w=KW)[:, :, 0:P].rearrange(
                            "p k (g d) -> p k g d", d=HC), cen[:, w].rearrange("p (k g d) -> p k g d", d=HC, k=nb * 2),
                            hr[:, 0:nh].rearrange("p (k g) -> p k g", k=nb * 2).unsqueeze(3).to_broadcast(
                                [P, nb * 2, P // HC, HC]), ALU.mult).then_inc(s_kn, 1)

                def body(i, t0=t0, ahead=ahead):
                    for s in range(GR):
                        tile(i, s, t0, ahead)
                        if s < 10:
                            heads(i, s)
                if its > 1:
                    with v.Fori(0, its) as i:
                        step_count.loop(i, 4)
                        body(i)
                    step_count.end(its)
                else:
                    body(0)
                m0 += its
            elif name == "kv":
                v.wait_ge(s_par, 16 * 12)
                v.wait_ge(s_kg, NB // LD + 3)
                step(v.tensor_tensor(brow[:, :], brow[:, :], b2r[:, :], ALU.add))
                for h in range(2):
                    v.tensor_scalar(kvw[:, (4 + h) * P:(5 + h) * P], ident[:, :], psG[h][:, P:P + 1], None, ALU.mult).then_inc(s_dg, 1)
                v.wait_ge(s_se, 2)
                for h in range(2):
                    g, se, sd_ = psG[h][:, 0:P], psP[:, h * P:(h + 1) * P], psG[h][:, P:P + 1]
                    vwr, vbr = hrow[:, h * P:(h + 1) * P], hrow[:, D + h * P:D + (h + 1) * P]
                    kwc, kbc = hv[:, 2 * h:2 * h + 1], hv[:, 2 * h + 1:2 * h + 2]
                    t_ = [kvw[:, n * P:(n + 1) * P] for n in range(4)]
                    step(v.tensor_scalar(t_[0], se, kbc, None, ALU.mult))
                    step(v.tensor_scalar(mcol[:, 0:1], sd_, kwc, None, ALU.mult))
                    wait()
                    step(v.scalar_tensor_tensor(out=t_[1], in0=g, scalar=kwc, in1=t_[0], op0=ALU.mult, op1=ALU.add))
                    step(v.scalar_tensor_tensor(out=mcol[:, 1:2], in0=kbc, scalar=float(N), in1=mcol[:, 0:1],
                                                op0=ALU.mult, op1=ALU.add))
                    wait()
                    step(v.tensor_tensor(t_[2], t_[1], vwr, ALU.mult))
                    wait()
                    step(v.scalar_tensor_tensor(out=t_[3], in0=vbr, scalar=mcol[:, 1:2], in1=t_[2], op0=ALU.mult, op1=ALU.add))
                    wait()
                    for a in range(0, P, HC):
                        w = W1[a:a + HC, h * D + h * P + a:h * D + h * P + a + HC]
                        step(v.scalar_tensor_tensor(out=w, in0=t_[3][a:a + HC, a:a + HC], scalar=1.0 / N, in1=w,
                                                    op0=ALU.mult, op1=ALU.add))
                    wait()
                v.memset(mcol[:, :], 0.0).then_inc(s_kv, 1)
            elif name == "own":
                def body(i, t0=t0, ahead=ahead, b0=b0, nb=LD if its > 1 else 1):
                    for s in range(GR):
                        tile(i, s, t0, ahead)
                        if (s % 4 == 0 and 0 < s <= 4 * (nb - 1)) or s == (GR - 1 if nb == LD else 3):
                            j = -(-s // 4) - 1
                            b = i * LD + (b0 + j)
                            v.wait_ge(s_xp, b + 3)
                            v.tensor_tensor(X[:, ds(b * D, D)], X[:, ds(b * D, D)], psG[j % 2][:, 0:D], ALU.add).then_inc(s_xa, 1)
                repeat(v, its, body)
                b0 += its * LD
            t0 += its * GR * groups
            k0 += its * CU if name == "sort" else 0


def nodes(nc, ctx, kk, dram, x):
    def sb(name, shape, dt):
        return ctx.enter_context(nc.sbuf_tensor(name, shape, dt))

    def sem(name):
        return ctx.enter_context(nc.semaphore(name))

    X, AGG, ident, ones, eps, W2, brow, gw, gb = (kk[n] for n in (
        "X", "AGG", "ident", "ones", "eps", "W2", "brow", "gw", "gb"))
    bank = kk["psum"]
    psT, psM, psU, psL = bank[0:2], bank[2:4], bank[4:6], bank[6:8]
    LW = NQ * NX
    PT, PD = 64, 128
    rcn = sb("rcn", [P, NB], F32)
    xr = sb("xr", [P, 2 * NQ * D], F32)
    xlast = sb("xlast", [P, D], F32)
    mean = sb("mean", [P, 2 * D], F32)
    mt = sb("mt", [P, 2 * D], F32)
    tmp = sb("tmp", [P, 2 * D], F32)
    nst = sb("nst", [P, NQ * 6], F32)
    nmv = sb("nmv", [P, NQ * 2], F32)
    nsd = sb("nsd", [P, NQ], F32)
    nrs = sb("nrs", [P, NQ], F32)
    nmr = sb("nmr", [P, NQ], F32)
    X2 = sb("X2", [P, XR * NQ * D], F32)
    ut = sb("ut", [P, 2 * D], F32)
    less = sb("less", [P, P], F32)
    seg = sb("seg", [P, LW], F32)
    carry = sb("carry", [P, NX], F32)
    lg, r0, r1, r2, r3, r4 = (sb(f"route{n}", [P, LW], F32) for n in range(6))
    q = [sb(f"rnode{n}", [P, NQ], F32) for n in range(9)]
    sidx = sb("sidx", [P, XR * NQ], I32)

    s_xr = [sem("x_again_0"), sem("x_again_1")]
    s_rc, s_xb, s_mean, s_tr, s_mt, s_mm, s_xm, s_x1 = (sem(n) for n in (
        "count_reciprocals", "x_with_bias", "mean_ready", "mean_transposed", "mean_t_copied", "mean_products",
        "mean_products_added", "x1_ready"))
    s_v, s_nv, s_ns, s_nr, s_x2, s_u, s_ut, s_lg = (sem(n) for n in (
        "node_steps", "x1_variance", "x1_std", "x1_scale", "x1_normal", "x1n_transposed", "x1n_t_copied", "logits"))
    s_mx, s_ex, s_oh, s_pf, s_rt, s_sl = (sem(n) for n in (
        "logit_max", "logit_exp", "expert_onehot", "expert_prefix", "prefix_read", "slots_ready"))
    s_xl, s_zx = sem("last_x_again"), sem("last_x_zero")
    s_sc = [sem(f"rows_scattered_{n}") for n in range(XR)]
    block = ctx.enter_context(nc.Block())
    NT = NB // NQ
    NORM, GATE = NQ + 3, NQ + 4
    ROUTE = GATE + NQ + 1
    STEPS = (NT - 1) * NQ + ROUTE + NQ

    def blk(n, lag):
        return n - lag if 0 <= n - lag < NB else None

    def batch(n, lag):
        return (n - lag) // NQ if (n - lag) % NQ == 0 and 0 <= n - lag < NB else None

    @block.sync
    def _(sp):
        sp.wait_ge(s_zx, 1)
        sp.dma_start(xlast[0:LASTROWS, :], x[(NB - 1) * P:N, :]).then_inc(s_xl, 16)
        for t in range(NT):
            if t >= 2:
                sp.wait_ge(s_x1, (t - 1) * NQ)
            o = t % 2 * NQ * D
            nb = NQ if t < NT - 1 else NQ - 1
            sp.dma_start(xr[:, o:o + nb * D].rearrange("p (j d) -> p j d", d=D),
                         x[t * NQ * P:(t * NQ + nb) * P, :].rearrange("(j p) d -> p j d", p=P)).then_inc(s_xr[t % 2], 16)

    @block.scalar
    def _(act):
        def place(n):
            h = n % 2
            if n >= 2:
                act.wait_ge(s_tr, n - 1)
            act.activation(mean[:, h * D:(h + 1) * D], AGG[:, n * AGW:n * AGW + D], ACT.Copy,
                           scale=rcn[:, n:n + 1]).then_inc(s_mean, 1)
        act.wait_ge(s_rc, 1)
        place(0)
        for n in range(STEPS):
            t = batch(n, NORM)
            if t is not None:
                act.wait_ge(s_nv, t + 1)
                act.activation(nsd[:, :], nmv[:, 1:2 * NQ:2], ACT.Sqrt, bias=eps[:, :]).then_inc(s_ns, 1)
            if n + 1 < NB:
                place(n + 1)
            if n < NB:
                h = n % 2
                act.wait_ge(s_tr, n + 1)
                if n >= 2:
                    act.wait_ge(s_mm, n - 1)
                act.activation(mt[:, h * D:(h + 1) * D], psT[h][:, 0:D], ACT.Copy).then_inc(s_mt, 1)
            m = blk(n, GATE)
            if m is not None:
                g = m % 2
                act.wait_ge(s_u, m + 1)
                if m >= 2:
                    act.wait_ge(s_lg, m - 1)
                act.activation(ut[:, g * D:(g + 1) * D], psU[g][:, 0:D], ACT.Copy).then_inc(s_ut, 1)
            m = blk(n, NORM)
            if m is not None:
                if m % NQ == 0:
                    act.wait_ge(s_nr, m // NQ + 1)
                    if m // NQ >= XR:
                        act.wait_ge(s_sc[m // NQ % XR], m // (NQ * XR) * 16 * NQ)
                o = m % (XR * NQ) * D
                act.activation(X2[:, o:o + D], X[:, m * D:(m + 1) * D], ACT.Identity, bias=nmr[:, m % NQ:m % NQ + 1],
                               scale=nrs[:, m % NQ:m % NQ + 1]).then_inc(s_x2, 1)
            t = batch(n, ROUTE + 1)
            if t is not None:
                act.wait_ge(s_mx, t + 1)
                act.activation(r3[:, :], r3[:, :], ACT.Exp).then_inc(s_ex, 1)

    @block.tensor
    def _(pe):
        for n in range(STEPS):
            if n < NB:
                h = n % 2
                pe.wait_ge(s_mean, n + 1)
                if n >= 2:
                    pe.wait_ge(s_mt, n - 1)
                for k in range(2):
                    ins = pe.transpose(psT[h][:, k * P:(k + 1) * P], mean[:, h * D + k * P:h * D + (k + 1) * P], ident[:, :])
                ins.then_inc(s_tr, 1)
            m = blk(n, GATE)
            if m is not None:
                g = m % 2
                pe.wait_ge(s_x2, m + 1)
                if m >= 2:
                    pe.wait_ge(s_ut, m - 1)
                o = m % (XR * NQ) * D
                for k in range(2):
                    ins = pe.transpose(psU[g][:, k * P:(k + 1) * P], X2[:, o + k * P:o + (k + 1) * P], ident[:, :])
                ins.then_inc(s_u, 1)
            t = batch(n, ROUTE + 3)
            if t is not None:
                pe.wait_ge(s_oh, t + 1)
                pe.matmul(psL[t % 2][:, PT:PT + LW], ones[:, :], r1[:, :], start=True, stop=True)
                pe.matmul(psL[t % 2][:, PD:PD + LW], less[:, :], r1[:, :], start=True, stop=True).then_inc(s_pf, 1)
            m = blk(n, 1)
            if m is not None:
                h = m % 2
                pe.wait_ge(s_mt, m + 1)
                if m >= 2:
                    pe.wait_ge(s_xm, m - 1)
                for k in range(2):
                    ins = pe.matmul(psM[h][:, 0:D], mt[:, h * D + k * P:h * D + (k + 1) * P],
                                    W2[:, k * D:(k + 1) * D], start=(k == 0), stop=(k == 1))
                ins.then_inc(s_mm, 1)
            m = blk(n, GATE + 1)
            if m is not None:
                g, t, j = m % 2, m // NQ, m % NQ
                pe.wait_ge(s_ut, m + 1)
                if j == 0 and t >= 2:
                    pe.wait_ge(s_rt, t - 1)
                for k in range(2):
                    ins = pe.matmul(psL[t % 2][:, j * NX:(j + 1) * NX], ut[:, g * D + k * P:g * D + (k + 1) * P],
                                    gw[:, k * NX:(k + 1) * NX], start=(k == 0), stop=(k == 1))
                ins.then_inc(s_lg, 1)

    @block.vector
    def _(v):
        count = Tally(s_v)
        step = count.add

        def wait():
            v.wait_ge(s_v, count.value())
        v.memset(xlast[:, :], 0.0).then_inc(s_zx, 1)
        v.memset(seg[:, :], 1.0)
        v.memset(carry[:, :], 0.0)
        v.tensor_scalar(less[:, :], kk["upper"][:, :], -1.0, None, ALU.add)
        step(v.tensor_scalar(rcn[:, :], AGG[:, D:NB * AGW:AGW], 1.0, PARTS, ALU.max, ALU.mult))
        wait()
        step(v.memset(seg[:, 0:LW:NQ], 0.0))
        v.reciprocal(rcn[:, :], rcn[:, :]).then_inc(s_rc, 1)

        g3 = lambda ap: ap.rearrange("p (b e) -> p b e", e=NX)
        wide = lambda ap: ap.unsqueeze(2).to_broadcast([P, NQ, NX])
        io8 = kk["iota8"][:, :].unsqueeze(1).to_broadcast([P, NQ, NX])

        def route(t, s):
            mine = slice(t * NQ, (t + 1) * NQ)
            if s:
                wait()
            if s == 0:
                v.wait_ge(s_lg, t * NQ + NQ)
                step(v.tensor_tensor(g3(lg[:, :]), g3(psL[t % 2][:, 0:LW]), gb[:, :].unsqueeze(1).to_broadcast([P, NQ, NX]), ALU.add))
            elif s == 1:
                step(v.tensor_reduce(q[0][:, :], g3(lg[:, :]), AX.X, ALU.max))
            elif s == 2:
                v.tensor_tensor(g3(r3[:, :]), g3(lg[:, :]), wide(q[0][:, :]), ALU.subtract).then_inc(s_mx, 1)
            elif s == 3:
                step(v.tensor_tensor(g3(r0[:, :]), g3(lg[:, :]), wide(q[0][:, :]), ALU.is_equal))
            elif s == 4:
                step(v.tensor_tensor(g3(r0[:, :]), g3(r0[:, :]), io8, ALU.mult))
            elif s == 5:
                step(v.tensor_reduce(q[1][:, :], g3(r0[:, :]), AX.X, ALU.max))
            elif s == 6:
                v.tensor_tensor(g3(r1[:, :]), io8, wide(q[1][:, :]), ALU.is_equal).then_inc(s_oh, 1)
            elif s == 7:
                v.wait_ge(s_ex, t + 1)
                step(v.tensor_reduce(q[2][:, :], g3(r3[:, :]), AX.X, ALU.add))
            elif s == 8:
                step(v.reciprocal(q[3][:, :], q[2][:, :]))
            elif s == 9:
                v.wait_ge(s_pf, t + 1)
                step(v.tensor_copy(r2[:, :].rearrange("p (e b) -> p b e", b=NQ), g3(psL[t % 2][:, PT:PT + LW])))
            elif s == 10:
                step(v.tensor_tensor(r2[:, 0:LW:NQ], r2[:, 0:LW:NQ], carry[:, :], ALU.add))
            elif s == 11:
                step(v.tensor_tensor_scan(r4[:, :], seg[:, :], r2[:, :], 0.0, ALU.mult, ALU.add))
            elif s == 12:
                step(v.tensor_copy(carry[:, :], r4[:, NQ - 1:LW:NQ]))
            elif s == 13:
                v.tensor_tensor(g3(r0[:, :]), r4[:, :].rearrange("p (e b) -> p b e", b=NQ), g3(psL[t % 2][:, PD:PD + LW]),
                                ALU.add).then_inc(s_rt, 1)
            elif s == 14:
                v.wait_ge(s_rt, t + 1)
                step(v.tensor_tensor(r0[:, :], r0[:, :], r1[:, :], ALU.mult))
            elif s == 15:
                step(v.tensor_reduce(q[4][:, :], g3(r0[:, :]), AX.X, ALU.add))
            elif s == 16:
                step(v.tensor_scalar(q[5][:, :], q[4][:, :], float(CAP), None, ALU.is_lt))
                step(v.tensor_scalar(q[6][:, :], q[1][:, :], -float(CAPR), float(NX * CAPR), ALU.mult, ALU.add))
            elif s == 17:
                step(v.tensor_tensor(kk["kp"][:, mine], q[5][:, :], q[3][:, :], ALU.mult))
                step(v.tensor_tensor(q[7][:, :], q[4][:, :], q[6][:, :], ALU.add))
            elif s == 18:
                step(v.scalar_tensor_tensor(out=q[0][:, :], in0=q[7][:, :], scalar=-float(NX * CAPR), in1=q[5][:, :],
                                            op0=ALU.add, op1=ALU.mult))
                step(v.tensor_tensor(q[8][:, :], q[7][:, :], kk["dummy"][:, mine], ALU.subtract))
            elif s == 19:
                step(v.tensor_scalar(kk["gidx"][:, mine], q[0][:, :], float(NX * CAPR), None, ALU.add))
                step(v.tensor_tensor(q[8][:, :], q[8][:, :], q[5][:, :], ALU.mult))
            elif s == 20:
                v.tensor_tensor(sidx[:, t % XR * NQ:(t % XR + 1) * NQ], q[8][:, :], kk["dummy"][:, mine], ALU.add).then_inc(s_sl, 1)

        for n in range(STEPS):
            t = batch(n, NORM)
            if t is not None:
                v.wait_ge(s_ns, t + 1)
                step(v.reciprocal(nrs[:, :], nsd[:, :]))
                wait()
                v.scalar_tensor_tensor(out=nmr[:, :], in0=nmv[:, 0:2 * NQ:2], scalar=-1.0, in1=nrs[:, :],
                                       op0=ALU.mult, op1=ALU.mult).then_inc(s_nr, 1)
            m = blk(n, 2)
            if m is not None:
                h = m % 2
                v.wait_ge(s_xm, m + 1)
                if m % NQ == 0:
                    v.wait_ge(s_xb, m // NQ + 2)
                o = m % (2 * NQ) * D
                mine = xr[:, o:o + D] if m < NB - 1 else xlast[:, :]
                v.tensor_tensor(X[:, m * D:(m + 1) * D], tmp[:, h * D:(h + 1) * D], mine, ALU.add).then_inc(s_x1, 1)
            m = blk(n, 3)
            if m is not None:
                v.wait_ge(s_x1, m + 1)
                o = m % NQ * 6
                step(v.bn_stats(nst[:, o:o + 6], X[:, m * D:(m + 1) * D]))
            if n >= ROUTE and (n - ROUTE) // NQ < NT:
                for s in range(3):
                    route((n - ROUTE) // NQ, 3 * ((n - ROUTE) % NQ) + s)
            m = blk(n, 1)
            if m is not None:
                h = m % 2
                v.wait_ge(s_mm, m + 1)
                if m >= 2:
                    v.wait_ge(s_x1, m - 1)
                v.tensor_tensor(tmp[:, h * D:(h + 1) * D], psM[h][:, 0:D], X[:, m * D:(m + 1) * D], ALU.add).then_inc(s_xm, 1)
            if batch(n + 1, NORM) is not None:
                wait()
                for j in range(NQ):
                    ins = v.bn_aggr(nmv[:, 2 * j:2 * j + 2], nst[:, 6 * j:6 * j + 6])
                ins.then_inc(s_nv, 1)

    @block.gpsimd
    def _(pool):
        def bias(w, n):
            pool.tensor_tensor(w.rearrange("p (j d) -> p j d", d=D), w.rearrange("p (j d) -> p j d", d=D),
                               brow[:, :].unsqueeze(1).to_broadcast([P, n, D]), ALU.add).then_inc(s_xb, 1)

        def scatter(t):
            pool.wait_ge(s_sl, t + 1)
            for j in range(NQ):
                rows = LASTROWS if t * NQ + j == NB - 1 else P
                k = t % XR * NQ + j
                pool.indirect_dma_start(dram["buf"], bass.IndirectOffsetOnAxis(ap=sidx[0:rows, k:k + 1], axis=0),
                                        X2[0:rows, k * D:(k + 1) * D], None).then_inc(s_sc[t % XR], 16)
        pool.wait_ge(s_xl, 16)
        bias(xlast[:, :], 1)
        for t in range(NT + 3):
            if t < NT:
                nb = NQ if t < NT - 1 else NQ - 1
                pool.wait_ge(s_xr[t % 2], 16 * (t // 2 + 1))
                bias(xr[:, t % 2 * NQ * D:(t % 2 * NQ + nb) * D], nb)
            if t >= 3:
                scatter(t - 3)
        for n in range(XR):
            pool.wait_ge(s_sc[n], 16 * NQ * len(range(n, NT, XR)))


def experts(nc, ctx, kk, dram, f1, fb1, f2, fb2):
    def sb(name, shape, dt):
        return ctx.enter_context(nc.sbuf_tensor(name, shape, dt))

    def sem(name):
        return ctx.enter_context(nc.semaphore(name))

    ident, bank = kk["ident"], kk["psum"]
    buf, ybuf = dram["buf"], dram["ybuf"]
    w1 = sb("w1", [P, 2 * 2 * F], F32)
    w2 = sb("w2", [P, 2 * FT * D], F32)
    b2 = sb("b2", [P, 2 * D], F32)
    b1r = sb("b1r", [NX * FT, P], F32)
    b1c = sb("b1c", [P, NX * FT], F32)
    xb = sb("xb", [P, 2 * TQ * D], F32)
    xt = sb("xt", [P, 2 * HALF], F32)
    ht = sb("ht", [P, FT * HALF], F32)
    yb = sb("yb", [P, 2 * TQ * D], F32)
    nn = sb("nn", [P, TQ * D], U32)
    zr = sb("zr", [P, TQ * D], F32)
    s_w = [sem("weights_0"), sem("weights_1")]
    s_b = sem("first_biases")
    s_bt, s_bc = sem("first_biases_t"), sem("first_biases_copied")
    s_xb = [sem("rows_0"), sem("rows_1")]
    s_t, s_xt, s_h, s_r, s_y, s_ys, s_vs = (sem(n) for n in (
        "rows_transposed", "rows_t_copied", "hidden_product", "hidden_ready", "out_product", "out_copied", "expert_steps"))
    s_past = sem("past_a_wait_2")
    s_free = sem("out_slot_free")
    s_yd, s_zr = sem("out_sums"), sem("zeros_ready")
    s_st = [sem("out_stored_0"), sem("out_stored_1")]
    block = ctx.enter_context(nc.Block())
    psT, psH, psY = bank[0:2], bank[2:4], bank[4:6]

    def halves(eng, body, n=NX // 2):
        with eng.Fori(0, n) as i:
            for a in range(4):
                body(i, a)

    @block.sync
    def _(sp):
        sp.dma_start(b1r[:, :], fb1.rearrange("e (f p) -> (e f) p", p=P)).then_inc(s_b, 16)

        def weights(e, q):
            sp.dma_start(w1[:, q * 2 * F:(q + 1) * 2 * F].rearrange("p (k f) -> p k f", k=2),
                         f1[ds(e, 1), :, :].rearrange("a (k p) f -> p (a k) f", p=P)).then_inc(s_w[q], 16)
            sp.dma_start(w2[:, q * FT * D:(q + 1) * FT * D].rearrange("p (f d) -> p f d", f=FT),
                         f2[ds(e, 1), :, :].rearrange("a (f p) d -> p (a f) d", p=P)).then_inc(s_w[q], 16)
            sp.dma_start(b2[:, q * D:(q + 1) * D], fb2[ds(e, 1), :].partition_broadcast(P)).then_inc(s_w[q], 16)

        def load(i, a):
            if a % 2 == 0:
                sp.wait_ge(s_ys, i * 4 + (a + 2))
                weights(i * 2 + a // 2, a // 2)
            sp.wait_ge(s_t, i * 4 + (a + 1))
            sp.dma_start(xb[0:TM, a % 2 * TQ * D:(a % 2 + 1) * TQ * D],
                         buf[ds((i * 4 + a) * HALF, HALF), :].rearrange("(p m) d -> p (m d)", m=TQ)).then_inc(s_xb[a % 2], 16)
        halves(sp, load)

    @block.tensor
    def _(pe):
        pe.sem_inc(s_t, 2)
        pe.wait_ge(s_b, 16)
        pe.transpose(bank[6][:, 0:NX * FT], b1r[:, :], ident[0:NX * FT, 0:NX * FT]).then_inc(s_bt, 1)

        def half(i, a):
            n = i * 4 + a
            q, h = a // 2, a % 2
            pe.wait_ge(s_xb[h], (i * 2 + (q + 1)) * 16)
            pe.wait_ge(s_xt, n + 1)
            for m in range(TQ):
                for k in range(2):
                    ins = pe.transpose(psT[k][:, m * TM:(m + 1) * TM],
                                       xb[0:TM, h * TQ * D + m * D + k * P:h * TQ * D + m * D + (k + 1) * P],
                                       ident[0:TM, 0:TM])
            ins.then_inc(s_t, 1)
            if h == 0:
                pe.wait_ge(s_w[q], i * 48 + 48)
            pe.wait_ge(s_xt, n + 2)
            for f in range(FT):
                pe.wait_ge(s_r, n * FT + (f + 1))
                for k in range(2):
                    ins = pe.matmul(psH[f % 2][:, 0:HALF], w1[:, (q * 2 + k) * F + f * P:(q * 2 + k) * F + (f + 1) * P],
                                    xt[:, k * HALF:(k + 1) * HALF], start=(k == 0), stop=(k == 1))
                ins.then_inc(s_h, 1)
            for m in range(TQ):
                pe.wait_ge(s_y, n * TQ + (m + 1))
                for f in range(FT):
                    if m == 0:
                        pe.wait_ge(s_r, n * FT + (f + 3))
                    ins = pe.matmul(psY[m % 2][0:TM, 0:D], ht[:, f * HALF + m * TM:f * HALF + (m + 1) * TM],
                                    w2[:, (q * FT + f) * D:(q * FT + f + 1) * D], start=(f == 0), stop=(f == FT - 1))
                ins.then_inc(s_yd, 1)
        halves(pe, half)

    @block.scalar
    def _(act):
        act.sem_inc(s_xt, 1)
        act.sem_inc(s_r, 2)
        act.wait_ge(s_bt, 1)
        act.activation(b1c[:, :], bank[6][:, 0:NX * FT], ACT.Copy).then_inc(s_bc, 1)
        act.wait_ge(s_bc, 1)

        def half(i, a):
            n = i * 4 + a
            act.wait_ge(s_t, n + 3)
            act.wait_ge(s_h, n * FT + 1)
            for k in range(2):
                ins = act.activation(xt[:, k * HALF:(k + 1) * HALF], psT[k][:, 0:HALF], ACT.Copy)
            ins.then_inc(s_xt, 1)
            act.wait_ge(s_yd, n * TQ + 1)
            for f in range(FT):
                act.wait_ge(s_h, n * FT + (f + 2))
                act.sem_inc(s_past, 1)
                act.activation(ht[:, f * HALF:(f + 1) * HALF], psH[f % 2][:, 0:HALF], ACT.Relu,
                               bias=b1c[:, ds((i * 2 + a // 2) * FT + f, 1)]).then_inc(s_r, 1)
        halves(act, half)

    @block.vector
    def _(v):
        v.sem_inc(s_y, 2)
        v.sem_inc(s_ys, 4)
        v.sem_inc(s_h, 1)
        v.sem_inc(s_yd, 1)
        v.memset(zr[:, :], 0.0).then_inc(s_zr, 1)
        v.wait_ge(s_zr, 1)

        def half(i, a):
            n = i * 4 + a
            q, h = a // 2, a % 2
            y = yb[0:TM, h * TQ * D:(h + 1) * TQ * D]
            v.wait_ge(s_free, n + 1)
            for m in range(TQ):
                v.wait_ge(s_yd, n * TQ + (m + 2))
                v.tensor_tensor(y[:, m * D:(m + 1) * D], psY[m % 2][0:TM, 0:D], b2[0:TM, q * D:(q + 1) * D],
                                ALU.add).then_inc(s_y, 1)
            v.wait_ge(s_y, n * TQ + (TQ + 2))
            v.tensor_tensor(nn[0:TM, :], y, y, ALU.not_equal).then_inc(s_vs, 1)
            v.wait_ge(s_vs, n + 1)
            v.sem_inc(s_past, 1)
            v.copy_predicated(y, nn[0:TM, :], zr[0:TM, :]).then_inc(s_ys, 1)
        halves(v, half)

    @block.gpsimd
    def _(pool):
        pool.sem_inc(s_free, 2)

        def half(i, a):
            h = a % 2
            pool.wait_ge(s_ys, i * 4 + (a + 5))
            pool.dma_start(ybuf[ds((i * 4 + a) * HALF, HALF), :].rearrange("(p m) d -> p (m d)", m=TQ),
                           yb[0:TM, h * TQ * D:(h + 1) * TQ * D]).then_inc(s_st[h], 16)
            pool.wait_ge(s_st[h], (i * 2 + (a // 2 + 1)) * 16)
            pool.sem_inc(s_free, 1)
        halves(pool, half)


def outputs(nc, ctx, kk, dram, out):
    def sb(name, shape, dt):
        return ctx.enter_context(nc.sbuf_tensor(name, shape, dt))

    def sem(name):
        return ctx.enter_context(nc.semaphore(name))

    X, gidx, kp = kk["X"], kk["gidx"], kk["kp"]
    Y = sb("Y", [P, NB * D], F32)
    Z = sb("Z", [P, 4 * D], F32)
    lim = sb("lim", [P, 4 * D], F32)
    inf = sb("inf", [P, 4 * D], U32)
    R = 4
    s_y = [sem(f"row_gathered_{n}") for n in range(R)]
    s_z, s_c, s_i, s_o = (sem(n) for n in ("scaled", "clamped", "infinite_mask_and_set", "out_rows"))
    s_past = sem("past_a_wait_3")
    s_st = sem("out_stored")
    block = ctx.enter_context(nc.Block())

    def blocks(eng, body):
        with eng.Fori(0, NB // R) as i:
            for h in range(R):
                body(i * R + h, h, i * 16 + 16)
        body(NB - 1, 0, 16 * (NB // R + 1))

    @block.gpsimd
    def _(pool):
        for b in range(NB):
            if b >= R:
                pool.wait_ge(s_y[b % R], 16 * (b // R))
            pool.indirect_dma_start(Y[:, b * D:(b + 1) * D], None, dram["ybuf"],
                                    bass.IndirectOffsetOnAxis(ap=gidx[:, b:b + 1], axis=0)).then_inc(s_y[b % R], 16)

    @block.scalar
    def _(act):
        def body(b, h, k):
            act.wait_ge(s_y[h], k)
            act.wait_ge(s_o, b + 1)
            act.activation(Z[:, h * D:(h + 1) * D], Y[:, ds(b * D, D)], ACT.Copy, scale=kp[:, ds(b, 1)]).then_inc(s_z, 1)
        blocks(act, body)

    @block.vector
    def _(v):
        v.sem_inc(s_o, R)

        def body(b, h, k):
            w = slice(h * D, (h + 1) * D)
            y = Z[:, w]
            v.wait_ge(s_z, b + 1)
            v.wait_ge(s_o, b + 1)
            v.tensor_scalar(inf[:, w], y, 0.0, 0.0, ALU.mult, ALU.not_equal).then_inc(s_i, 1)
            v.tensor_scalar(lim[:, w], y, -10000.0, 10000.0, ALU.max, ALU.min).then_inc(s_c, 1)
            v.wait_ge(s_c, b + 1)
            v.sem_inc(s_past, 1)
            v.copy_predicated(y, inf[:, w], lim[:, w]).then_inc(s_i, 1)
            v.wait_ge(s_i, b * 2 + 2)
            v.tensor_tensor(X[:, ds(b * D, D)], X[:, ds(b * D, D)], y, ALU.add).then_inc(s_o, 1)
        blocks(v, body)

    @block.sync
    def _(sp):
        with sp.Fori(0, NB // R) as i:
            sp.wait_ge(s_o, i * R + 2 * R)
            sp.dma_start(out[ds(i * (R * P), R * P), :].rearrange("(j p) d -> p j d", p=P),
                         X[:, ds(i * (R * D), R * D)].rearrange("p (j d) -> p j d", j=R)).then_inc(s_st, 16)
        sp.wait_ge(s_o, NB + R)
        sp.dma_start(out[(NB - 1) * P:N, :], X[0:LASTROWS, (NB - 1) * D:NB * D]).then_inc(s_st, 16)
        sp.wait_ge(s_st, 16 * (NB // R + 1))


def kernel(x, src, dst, L0_gnn_W1, L0_gnn_b1, L0_gnn_W2, L0_gnn_b2, L0_mix_kln_weight, L0_mix_kln_bias,
           L0_mix_vln_weight, L0_mix_vln_bias, L0_ffn_gate_w, L0_ffn_gate_b, L0_ffn_w1, L0_ffn_b1, L0_ffn_w2,
           L0_ffn_b2):
    import numpy as np
    import concourse.bacc as bacc
    from concourse.bass_utils import run_bass_kernel_spmd

    arrays = {
        "x": x, "src": src, "dst": dst,
        "w1t": np.asarray(L0_gnn_W1).T, "w2t": np.asarray(L0_gnn_W2).T, "gb1": L0_gnn_b1, "gb2": L0_gnn_b2,
        "kw": L0_mix_kln_weight, "kb": L0_mix_kln_bias, "vw": L0_mix_vln_weight, "vb": L0_mix_vln_bias,
        "gate_w": L0_ffn_gate_w, "gate_b": L0_ffn_gate_b,
        "f1": L0_ffn_w1, "fb1": L0_ffn_b1, "f2": L0_ffn_w2, "fb2": L0_ffn_b2,
    }
    arrays = {name: np.ascontiguousarray(a) for name, a in arrays.items()}
    nc = bacc.Bacc("TRN2", target_bir_lowering=False, num_devices=1)
    args = {name: nc.dram_tensor(name, a.shape, mybir.dt.from_np(a.dtype), kind="ExternalInput").ap()
            for name, a in arrays.items()}
    out = nc.dram_tensor("out", (N, D), F32, kind="ExternalOutput").ap()
    build_program(nc, **args, out=out)
    r = run_bass_kernel_spmd(nc, [arrays], core_ids=[0])
    return r.results[0]["out"]
```

```python
from contextlib import ExitStack

import concourse.bass as bass
from concourse import mybir

ALU = mybir.AluOpType
ACT = mybir.ActivationFunctionType
AX = mybir.AxisListType
F32 = mybir.dt.float32
F16 = mybir.dt.float16
BF16 = mybir.dt.bfloat16
I32 = mybir.dt.int32
U32 = mybir.dt.uint32
U16 = mybir.dt.uint16
ds = bass.ds

P = 128
N, D = 6250, 256
NB = -(-N // P)
LASTROWS = N - (NB - 1) * P
LD = 4
HD = 3
E = 100000
EP = 125
EC = E // EP
HEADS, HC = 8, 32
NX, F = 8, 1024
FT = F // P
CAP = 977
TM, TQ = 123, 4
HALF = TM * TQ
CAPR = 2 * HALF
PARTS = 2048.0
QR = 4
GR = 16
SR = 8
KR = 8
CW = 2
AHEAD = 4
CU = 16
AGW = D + 1
XO, RW = AGW, AGW + D + 1
NOROW = 1 << 20
LN_EPS, HEAD_EPS = 1e-5, 1e-5


def chunk_plan():
    plan, c0, t0 = [], 0, 0
    for cols in (352, 448):
        tiles = (cols * EP + NB * (P - 1)) // P
        tiles = -(-tiles // GR) * GR
        plan.append((c0, cols, t0, tiles))
        c0 += cols
        t0 += tiles
    assert c0 == EC
    return plan


CHUNKS = chunk_plan()
VSHARE = 3
TILES = sum(c[3] for c in CHUNKS)
WMAX = max(c[1] for c in CHUNKS)
TMAX = max(c[3] for c in CHUNKS)
B7 = 7
NQ = 7
assert TMAX <= 2 * WMAX and HD <= LD and NB % HD == 1 and NB % NQ == 0 and NB // NQ % 2 == 1 and CAPR >= CAP and EP * EC == E and TMAX <= 512 and NB % B7 == 0


def phases():
    out, heads, late = [], NB // HD, NB // LD + 1
    for c, (_, cols, _, _) in enumerate(CHUNKS):
        left = CHUNKS[c - 1][3] // GR if c else 0
        sorts = cols // CU
        out += [(c, "count", NB // B7, 0, False), (c, "place", 1, 0, False),
                (c, "rank", NB // B7, min(left, 1), left > 0), (c, "split", 1, 0, False)]
        left -= min(left, NB // B7)
        early = max(0, heads + 1 - (CHUNKS[-1][3] // GR - late)) if c == len(CHUNKS) - 1 else 0
        with_sort = left - early
        assert with_sort <= sorts and early != 1
        if with_sort:
            out += [(c, "sort", with_sort - 1, 1, True), (c, "sort", 1, 1, early > 0)]
        if early > 0:
            out += [(c, "heads", early - 1, 1, True), (c, "heads", 1, 1, False)]
            heads -= early
        out += [(c, "sort", sorts - with_sort, 0, False), (c, "decode", 1, 0, False)]
    last = len(CHUNKS)
    rest = CHUNKS[-1][3] // GR - late - 1 - heads
    if rest:
        out += [(last, "rest", rest, 1, True)]
    return out + [(last, "heads", heads, 1, True), (last, "tail", 1, 1, True), (last, "kv", 1, 0, False),
                  (last, "own", late - 1, 1, True), (last, "own", 1, 1, False)]


PHASES = phases()


def xcols(b):
    return ds(b * RW + XO, D)


def xblocks(XA, b, nb):
    return XA[:, ds(b * RW, nb * RW)].rearrange("p (j w) -> p j w", w=RW)[:, :, XO:XO + D]


def load_weights(eng, w1, w2, b2, f1, f2, fb2, e, s_w):
    eng.dma_start(w1[:, :].rearrange("p (k f) -> p k f", k=2),
                  f1[ds(e, 1), :, :].rearrange("a (k p) f -> p (a k) f", p=P)).then_inc(s_w, 16)
    eng.dma_start(w2[:, :].rearrange("p (f d) -> p f d", f=FT),
                  f2[ds(e, 1), :, :].rearrange("a (f p) d -> p (a f) d", p=P)).then_inc(s_w, 16)
    eng.dma_start(b2[:, :], fb2[ds(e, 1), :].partition_broadcast(P)).then_inc(s_w, 16)


class Tally:

    def __init__(self, sem):
        self.sem, self.base, self.i, self.k, self.j = sem, 0, 0, 0, 0

    def loop(self, i, k):
        self.base, self.i, self.k, self.j = self.base + self.j, i, k, 0

    def end(self, n):
        assert self.j == self.k, (self.sem, self.j, self.k)
        self.base, self.i, self.k, self.j = self.base + n * self.k, 0, 0, 0

    def add(self, ins):
        ins.then_inc(self.sem, 1)
        self.j += 1

    def value(self, back=0):
        return self.i * self.k + (self.base + self.j - back)


def repeat(eng, n, body, first=0):
    if n == 1:
        body(first)
    elif n > 1:
        with eng.Fori(0, n) as i:
            body(i + first if first else i)


def build_program(nc, x, src, dst, w1t, w2t, gb1, gb2, kw, kb, vw, vb, gate_w, gate_b, f1, fb1, f2, fb2, out):
    dram = {
        "tab": nc.dram_tensor("xn_parts", (NB * P, 2 * D), F16, kind="Internal").ap(),
        "buf": nc.dram_tensor("expert_rows", (NX * CAPR, RW), F32, kind="Internal").ap(),
    }
    with ExitStack() as ctx:
        def sb(name, shape, dt):
            return ctx.enter_context(nc.sbuf_tensor(name, shape, dt))

        k = {
            "ident": sb("ident", [P, P], F32),
            "upper": sb("upper", [P, P], F32),
            "upinc": sb("upinc", [P, P], F32),
            "ones": sb("ones", [P, P], F32),
            "eps": sb("eps", [P, 1], F32),
            "W1": sb("W1", [P, 2 * D], F32),
            "W2": sb("W2", [P, 2 * D], F32),
            "brow": sb("brow", [P, D], F32),
            "gw": sb("gw", [P, 2 * NX], F32),
            "gb": sb("gb", [P, NX], F32),
            "iota8": sb("iota8", [P, NX], F32),
            "w1_0": sb("w1_0", [P, 2 * F], F32),
            "w2_0": sb("w2_0", [P, FT * D], F32),
            "b2_0": sb("b2_0", [P, D], F32),
            "s_w0": ctx.enter_context(nc.semaphore("weights_0")),
            "psum": [ctx.enter_context(nc.psum_tensor(f"bank{i}", [P, 512], F32)) for i in range(8)],
            "zst": ctx.enter_context(nc.semaphore("expert_rows_zeroed")),
        }
        with ExitStack() as c2:
            k["XA"] = c2.enter_context(nc.sbuf_tensor("XA", [P, NB * RW], F32))
            with ExitStack() as c:
                edges(nc, c, k, dram, x, src, dst, w1t, w2t, gb1, gb2, kw, kb, vw, vb, gate_w, gate_b)
            with ExitStack() as c:
                nodes(nc, c, k, dram, x, f1, f2, fb2, out)
        with ExitStack() as c:
            experts(nc, c, k, dram, f1, fb1, f2, fb2, out)


def edges(nc, ctx, kk, dram, x, src, dst, w1t, w2t, gb1, gb2, kw, kb, vw, vb, gate_w, gate_b):
    def sb(name, shape, dt):
        return ctx.enter_context(nc.sbuf_tensor(name, shape, dt))

    def sem(name):
        return ctx.enter_context(nc.semaphore(name))

    tab, buf = dram["tab"], dram["buf"]
    XA, ident, upper, upinc, ones, eps = (kk[n] for n in ("XA", "ident", "upper", "upinc", "ones", "eps"))
    W1, W2, brow, gw, gb = (kk[n] for n in ("W1", "W2", "brow", "gw", "gb"))
    bank = kk["psum"]
    psA, psV, psP, psG, psQ = bank[0:2], bank[2:4], bank[4], bank[5:7], bank[7]
    zst = kk["zst"]

    G = sb("G", [P, GR * 2 * D], F16)
    ones16 = sb("ones16", [P, 2], F16)
    zero16 = sb("zero16", [P, P], F16)
    zero32 = sb("zero32", [P, P], F32)
    iota_t = sb("iota_t", [P, TMAX], F16)
    iota_1 = sb("iota_1", [P, P], F16)
    iota_b = sb("iota_b", [P, NB], F32)
    lnst = sb("lnst", [P, 2 * LD * 6], F32)
    lnmv = sb("lnmv", [P, 2 * LD * 2], F32)
    lnsd = sb("lnsd", [P, 2 * LD], F32)
    lnrs = sb("lnrs", [P, 2 * LD], F32)
    lnmr = sb("lnmr", [P, 2 * LD], F32)
    TB = G[:, 0:2 * LD * 2 * D]
    b7 = sb("b7", [P, B7], F32)
    n7 = sb("n7", [P, B7], F32)
    mask = sb("mask", [P, B7 * WMAX], BF16)
    work = sb("work", [P, 8 * EC], BF16)
    srci = work[:, 0:2 * EC].bitcast(I32)
    dsti = work[:, 2 * EC:4 * EC].bitcast(I32)
    tmpi = work[:, 4 * EC:6 * EC].bitcast(I32)
    tmpj = work[:, 6 * EC:8 * EC].bitcast(I32)
    cen = work[:, 0:2 * LD * D].bitcast(F32)
    sqr = work[:, 2 * LD * D:4 * LD * D].bitcast(F32)
    KW = P + 1
    xs, xts = cen[:, 0:2 * D], cen[:, 2 * D:4 * D]
    kn = work[:, 4 * LD * D:4 * LD * D + 2 * LD * 2 * KW].bitcast(F32)
    blk = sb("blk", [P, EC], BF16)
    v1 = sb("v1", [P, EC], F32)
    v2 = sb("v2", [P, EC], F32)
    onesw = sb("onesw", [P, WMAX], BF16)
    cum = sb("cum", [P, 3 * WMAX], F32)
    pos = sb("pos", [P, WMAX], F32)
    tf = sb("tf", [P, WMAX], F32)
    iota_i = cum[:, 0:TMAX].bitcast(I32)
    posi = cum[:, 0:WMAX].bitcast(I32)
    tli = cum[:, WMAX:2 * WMAX].bitcast(I32)
    cnt = sb("cnt", [P, NB], F32)
    mi = sb("mi", [P, 2 * NB], I32)
    mrow = sb("mrow", [P, NB], F32)
    mend = sb("mend", [P, NB], F32)
    base = sb("base", [P, NB], F32)
    mcol = sb("mcol", [P, 4], F32)
    mcoli = sb("mcoli", [P, 4], I32)
    LH = sb("LH", [P, KR * P], F16)
    LV = sb("LV", [P, KR * 2 * P], F16)
    HT = sb("HT", [P, KR * TMAX], F16)
    ge = HT[:, 0:TMAX]
    DI = HT[:, :].bitcast(I32)
    idx = sb("idx", [P, TILES], I32)
    srcl = sb("srcl", [P, TILES], F32)
    buck = sb("buck", [1, TILES], I32)
    idxr = sb("idxr", [P, GR], I32)
    S = sb("S", [P, SR * P], F16)
    dist = sb("dist", [P, SR // 2 * P], F16)
    here = sb("here", [P, 4 * GR], F32)
    srch, posh, tfh, v1h = (here[:, n * GR:(n + 1) * GR] for n in range(4))
    hv = sb("hv", [P, 2 * 2], F32)
    hrow = kk["w2_0"][:, 0:2 * D]
    b2r = kk["w1_0"][:, 0:D]
    hs = sb("hs", [P, LD * HEADS], F32)
    hm = sb("hm", [P, LD * HEADS], F32)
    hq = sb("hq", [P, LD * HEADS], F32)
    hr = sb("hr", [P, LD * HEADS], F32)
    kvw = mask[:, 0:12 * P].bitcast(F32)

    s_par, s_edge, s_x, s_xl = sem("parameters_loaded"), sem("edges_loaded"), sem("x_loaded"), sem("x_last_loaded")
    s_pc, s_dc = sem("pool_constants"), sem("vector_constants")
    s_v = sem("vector_steps")
    s_pad = sem("x_padding_zero")
    s_nrm = sem("ln_scale")
    s_stat, s_sd, s_xn, s_hi, s_lo = sem("ln_statistics"), sem("ln_std"), sem("xn_ready"), sem("high_part"), sem("low_part")
    s_tb = [sem("parts_stored_0"), sem("parts_stored_1")]
    s_tbc = sem("parts_read")
    s_cnt, s_pre, s_mc, s_ec, s_ge, s_bk = (sem(n) for n in (
        "bucket_counts", "bucket_prefix", "tile_counts", "tile_ends", "tiles_past_ends", "tile_buckets"))
    s_lh, s_lv, s_ht, s_col, s_sx, s_dec = (sem(n) for n in (
        "lane_onehot", "lane_values", "tile_onehot", "columns_sorted", "sort_closed", "sort_read"))
    s_idx = sem("indices_ready")
    s_srch, s_posh = sem("sources_at_hand"), sem("places_at_hand")
    s_g = [sem(f"gathered_{i}") for i in range(GR)]
    s_dist = sem("source_distance")
    s_S, s_tile, s_ev = sem("source_onehot"), sem("tile_summed"), sem("tile_added")
    s_cen, s_sq, s_ss, s_hstd, s_kn, s_kg = (sem(n) for n in (
        "heads_centred", "heads_squared", "heads_variance", "heads_std", "heads_normal", "heads_multiplied"))
    s_zero, s_agg = sem("zeros_ready"), sem("sums_zero")
    s_kv = sem("key_values_in_w1")
    s_xs, s_xt, s_xtc, s_xp, s_xa = (sem(n) for n in (
        "xn_placed", "xn_transposed", "xn_t_copied", "xn_products", "xn_products_added"))
    s_dg, s_se = sem("heads_sums_diagonal"), sem("heads_sums_row")
    s_past = sem("past_a_wait")

    block = ctx.enter_context(nc.Block())
    PAR = 16 * 16

    @block.sync
    def _(sp):
        sp.dma_start(srci[0:EP, :], src.rearrange("(p t) -> p t", p=EP)).then_inc(s_edge, 16)
        sp.dma_start(dsti[0:EP, :], dst.rearrange("(p t) -> p t", p=EP)).then_inc(s_edge, 16)
        sp.wait_ge(s_pad, 1)
        sp.dma_start(XA[0:LASTROWS, xcols(NB - 1)], x[(NB - 1) * P:N, :]).then_inc(s_xl, 16)

        sp.sem_inc(s_x, 16)
        with sp.Fori(0, NB // (2 * LD)) as i:
            sp.wait_ge(s_x, i * 16 + 16)
            sp.dma_start(xblocks(XA, i * (2 * LD), 2 * LD),
                         x[ds(i * (2 * LD * P), 2 * LD * P), :].rearrange("(j p) d -> p j d", p=P)).then_inc(s_x, 16)
        sp.wait_ge(s_zero, 1)
        flat, zeros = buf.rearrange("r w -> (r w)").rearrange("(p n) -> p n", p=P), G[:, :].bitcast(F32)
        per, width = NX * CAPR * RW // P, GR * D
        for o in range(0, per, width):
            sp.dma_start(flat[:, o:min(o + width, per)], zeros[:, 0:min(width, per - o)]).then_inc(zst, 16)

    @block.gpsimd
    def _(pool):
        pool.iota(iota_i[:, :], [[1, TMAX]], base=0, channel_multiplier=0).then_inc(s_pc, 1)
        pool.memset(ones[:, :], 1.0).then_inc(s_pc, 1)
        pool.memset(ident[:, :], 0.0).then_inc(s_pc, 1)
        pool.wait_ge(s_pc, 3)
        pool.affine_select(out=ident[:, :], in_=ident[:, :], compare_op=ALU.not_equal, fill=1.0, base=0,
                           pattern=[[-1, P]], channel_multiplier=1).then_inc(s_pc, 1)
        pool.affine_select(out=upper[:, :], in_=ones[:, :], compare_op=ALU.is_gt, fill=0.0, base=0,
                           pattern=[[1, P]], channel_multiplier=-1).then_inc(s_pc, 1)
        pool.affine_select(out=upinc[:, :], in_=ones[:, :], compare_op=ALU.is_ge, fill=0.0, base=0,
                           pattern=[[1, P]], channel_multiplier=-1).then_inc(s_pc, 1)
        pool.iota(mi[:, 0:NB], [[P, NB]], base=1, channel_multiplier=1).then_inc(s_pc, 1)
        pool.memset(XA[:, :].rearrange("p (b w) -> p b w", w=RW)[:, :, 0:AGW], 0.0).then_inc(s_agg, 1)

        def store(h, nb, rows, low):
            pool.wait_ge(s_lo, low)
            o = h * LD * 2 * D
            pool.dma_start(tab[rows, :].rearrange("(j p) d -> p j d", p=P),
                           TB[:, o:o + nb * 2 * D].rearrange("p (j d) -> p j d", j=nb)).then_inc(s_tb[h], 16)

        with pool.Fori(0, NB // (2 * LD)) as i:
            for h in range(2):
                store(h, LD, ds((i * 2 + h) * (LD * P), LD * P), i * 2 + (h + 1))
        n = NB // (2 * LD)
        store(0, 1, slice((NB - 1) * P, NB * P), 2 * n + 1)
        pool.wait_ge(s_tb[0], 16 * (n + 1))
        pool.wait_ge(s_tb[1], 16 * n)
        pool.memset(G[:, :].bitcast(F32), 0.0).then_inc(s_zero, 1)
        pool.wait_ge(zst, 16 * -(-(NX * CAPR * RW // P) // (GR * D)))

        g0 = 0
        for c, step, its, groups, _ in PHASES:
            if not groups:
                continue

            def gather(i, g0=g0):
                for s in range(GR):
                    if s % QR == 0:
                        pool.wait_ge(s_idx, i * (GR // QR) + (GR // QR * g0 + s // QR + 1))
                        pool.wait_ge(s_tile, i * GR + (GR * g0 + s + QR))
                        pool.sem_inc(s_past, 1)
                    pool.indirect_dma_start(G[:, s * 2 * D:(s + 1) * 2 * D], None, tab,
                                            bass.IndirectOffsetOnAxis(ap=idxr[:, s:s + 1], axis=0)).then_inc(s_g[s], 16)
            repeat(pool, its, gather)
            g0 += its

    @block.scalar
    def _(act):
        for a, b in ((W1, w1t), (W2, w2t)):
            act.dma_start(a[:, :].rearrange("p (k o) -> p k o", k=2), b.rearrange("(k p) o -> p k o", p=P)).then_inc(s_par, 16)
        act.dma_start(brow[:, :], gb1.rearrange("(a n) -> a n", a=1).partition_broadcast(P)).then_inc(s_par, 16)
        act.dma_start(b2r[:, :], gb2.rearrange("(a n) -> a n", a=1).partition_broadcast(P)).then_inc(s_par, 16)
        act.dma_start(gw[:, :].rearrange("p (k o) -> p k o", k=2), gate_w.rearrange("(k p) o -> p k o", p=P)).then_inc(s_par, 16)
        act.dma_start(gb[:, :], gate_b.rearrange("(a n) -> a n", a=1).partition_broadcast(P)).then_inc(s_par, 16)
        for n, col in enumerate((kw, kb)):
            flat = col.rearrange("h a c -> (h a c)").rearrange("(k p a) -> k p a", k=2, a=1)
            for h in range(2):
                act.dma_start(hv[:, 2 * h + n:2 * h + n + 1], flat[h]).then_inc(s_par, 16)
        for n, row in enumerate((vw, vb)):
            act.dma_start(hrow[:, n * D:(n + 1) * D],
                          row.rearrange("h a c -> a (h c)").partition_broadcast(P)).then_inc(s_par, 16)
        act.wait_ge(s_dc, 1)

        def std(h, nb, k):
            act.wait_ge(s_stat, k)
            act.activation(lnsd[:, h * LD:h * LD + nb], lnmv[:, 2 * h * LD + 1:2 * (h * LD + nb):2], ACT.Sqrt,
                           bias=eps[:, :]).then_inc(s_sd, 1)

        def normal(h, nb, at, k, last):
            act.wait_ge(s_nrm, k)
            act.sem_inc(s_past, 1)
            for j in range(nb):
                q = h * LD + j
                ins = act.activation(XA[:, at(j)], XA[:, at(j)], ACT.Identity, bias=lnmr[:, q:q + 1], scale=lnrs[:, q:q + 1])
            ins.then_inc(s_xn, 1)
            act.wait_ge(s_xn, k)
            if last is not None:
                act.wait_ge(s_tb[h], last)
            act.sem_inc(s_past, 1)
            o = h * LD * 2 * D
            act.activation(TB[:, o:o + nb * 2 * D].rearrange("p (j d) -> p j d", j=nb)[:, :, 0:D],
                           xblocks(XA, at(None), nb), ACT.Copy, scale=PARTS).then_inc(s_hi, 1)

        n = NB // (2 * LD)

        def pair(i, first):
            for h in range(2):
                std(h, LD, i * 2 + (h + 1))
            for h in range(2):
                b = (i * 2 + h) * LD
                normal(h, LD, lambda j: b if j is None else xcols(b + j), i * 2 + (h + 1),
                       None if first else i * 16)
        pair(0, True)
        with act.Fori(1, n) as i:
            pair(i, False)
        std(0, 1, 2 * n + 1)
        normal(0, 1, lambda j: NB - 1 if j is None else xcols(NB - 1), 2 * n + 1, 16 * n)

        act.wait_ge(s_pc, 7)
        k0, m0, b0, t0, made = 0, 0, 0, 0, 0
        for c, step, its, groups, _ in PHASES:
            if step == "rank" and groups:
                def onehots(i, t0=t0, made=made):
                    act.wait_ge(s_srch, i + (t0 // GR + 1))
                    for n, s in enumerate(range(0, GR, SR // 2)):
                        t = i * GR + (t0 + s)
                        act.wait_ge(s_S, t)
                        for j in range(SR // 2):
                            ins = act.activation(dist[:, j * P:(j + 1) * P], iota_1[:, :], ACT.Square,
                                                 bias=srch[:, s + j:s + j + 1])
                        ins.then_inc(s_dist, 1)
                        act.wait_ge(s_dist, i * (GR * 2 // SR) + (made + n + 1))
                        act.wait_ge(s_tile, t + (GR - SR // 2))
                        act.activation(S[:, s % SR * P:(s % SR + SR // 2) * P], dist[:, :], ACT.Relu, bias=ones[:, 0:1],
                                       scale=-1.0).then_inc(s_S, SR // 2)
                repeat(act, its, onehots)
                made += its * (GR * 2 // SR)
            t0 += its * GR * groups
            if step == "sort":
                c0 = CHUNKS[c][0]

                def values(i, k0=k0, groups=groups, share=VSHARE):
                    for j in range(CU):
                        q = j % KR
                        col = i * CU + (k0 + j)
                        if j % CW == 0:
                            act.wait_ge(s_lh, col + CW)
                        for n, v in enumerate((v1, v2)):
                            if n == 0 and not groups and j % share == share - 1:
                                continue
                            ins = act.activation(LV[0:EP, (2 * q + n) * P:(2 * q + n + 1) * P], LH[0:EP, q * P:(q + 1) * P],
                                                 ACT.Copy, scale=v[0:EP, ds(col, 1)])
                        ins.then_inc(s_lv, 1)
                repeat(act, its, values)
                k0 += its * CU
            elif step in ("heads", "tail"):
                nb = HD if step == "heads" else 1

                def heads(i, m0=m0, nb=nb):
                    act.wait_ge(s_cen, i + (m0 + 1))
                    act.activation(sqr[:, 0:nb * D], cen[:, 0:nb * D], ACT.Square).then_inc(s_sq, 1)
                    act.wait_ge(s_ss, i + (m0 + 1))
                    act.activation(hq[:, 0:nb * HEADS], hq[:, 0:nb * HEADS], ACT.Sqrt, scale=1.0 / (HC - 1)).then_inc(s_hstd, 1)
                repeat(act, its, heads)
                m0 += its
            elif step == "kv":
                act.wait_ge(s_kv, 1)
            elif step == "own":
                def own(i, b0=b0, nb=LD if its > 1 else 1):
                    for j in range(nb):
                        h, b = j % 2, i * LD + (b0 + j)
                        act.wait_ge(s_xt, b + 1)
                        act.activation(xs[:, h * D:(h + 1) * D], XA[:, xcols(b)], ACT.Copy).then_inc(s_xs, 1)
                        act.wait_ge(s_xt, b + 3)
                        act.wait_ge(s_xp, b + 1)
                        act.activation(xts[:, h * D:(h + 1) * D], psV[h][:, 0:D], ACT.Copy).then_inc(s_xtc, 1)
                repeat(act, its, own)
                b0 += its * LD

    @block.tensor
    def _(pe):
        pe.wait_ge(s_pc, 7)
        pe.wait_ge(s_dc, 2)
        pe.sem_inc(s_col, KR)
        pe.sem_inc(s_tile, GR)
        pe.sem_inc(s_kg, 1)
        pe.sem_inc(s_xt, 2)
        pe.sem_inc(s_xp, 2)
        t0, k0, m0, b0 = 0, 0, 0, 0
        for c, step, its, groups, _ in PHASES:
            if step == "place":
                _, cols, ch0, tiles = CHUNKS[c]
                pe.wait_ge(s_cnt, c + 1)
                pe.matmul(psP[:, 0:NB], upper[0:EP, :], cnt[0:EP, :], start=True, stop=True)
                pe.matmul(psP[:, 64:64 + NB], ones[0:EP, :], cnt[0:EP, :], start=True, stop=True)
                pe.matmul(psQ[0:NB, 0:1], cnt[0:EP, :], ones[0:EP, 0:1], start=True, stop=True).then_inc(s_pre, 1)
                pe.wait_ge(s_mc, c + 1)
                pe.matmul(psQ[0:NB, 0:1], upinc[0:NB, 0:NB], mcol[0:NB, 0:1], start=True, stop=True).then_inc(s_ec, 1)
                pe.wait_ge(s_ge, c + 1)
                pe.matmul(psQ[0:1, 0:tiles], ones16[0:NB, 0:1], ge[0:NB, 0:tiles], start=True, stop=True).then_inc(s_bk, 1)
                if c:
                    pe.wait_ge(s_dec, c)
                for n in range(2):
                    pe.matmul(psV[n][:, 0:tiles], zero16[0:EP, :], iota_t[0:EP, 0:tiles], start=True, stop=False,
                              skip_group_check=True)

            def tiles_of(i, s, t0=t0):
                t = i * GR + (t0 + s)
                q = s % SR
                pe.wait_ge(s_g[s], (i + (t0 // GR + 1)) * 16)
                pe.wait_ge(s_S, t + 1)
                pe.wait_ge(s_ev, t + 1)
                lhs = S[:, q * P:(q + 1) * P]
                o = s * 2 * D
                pe.matmul(psA[s % 2][:, 0:D], lhs, G[:, o:o + D], start=True, stop=False)
                pe.matmul(psA[s % 2][:, 0:D], lhs, G[:, o + D:o + 2 * D], start=False, stop=True)
                pe.matmul(psA[s % 2][:, D:D + 1], lhs, ones16[:, 0:1], start=True, stop=True).then_inc(s_tile, 1)

            def column(i, j, k0=k0, tiles=CHUNKS[min(c, len(CHUNKS) - 1)][3]):
                q = j % KR
                col = i * CU + (k0 + j)
                if j % CW == 0:
                    pe.wait_ge(s_lv, col + CW)
                    pe.wait_ge(s_ht, col + (CW + GR))
                for n in range(2):
                    ins = pe.matmul(psV[n][:, 0:tiles], LV[0:EP, (2 * q + n) * P:(2 * q + n + 1) * P],
                                    HT[0:EP, q * TMAX:q * TMAX + tiles], start=False, stop=False, skip_group_check=True)
                ins.then_inc(s_col, 1)

            def products(pieces):
                for piece in pieces:
                    for j, h in ((piece // 2, piece % 2),):
                        o = (j * 2 + h) * KW
                        ins = pe.matmul(psG[h][:, 0:KW], kn[:, o:o + P], kn[:, o:o + KW], start=False, stop=False,
                                        skip_group_check=True)
                return ins

            if step == "heads" and m0 == 0:
                pe.wait_ge(s_par, 16 * 12)
                for h in range(2):
                    pe.matmul(psG[h][:, 0:KW], zero32[:, :], W1[:, 0:KW], start=True, stop=False,
                              skip_group_check=True)

            def own(i, s, b0=b0):
                h, b = s // 4 % 2, i * LD + (b0 + s // 4)
                if s % 4 == 0:
                    pe.wait_ge(s_xs, b + 1)
                    pe.wait_ge(s_xtc, b + 1)
                    for n in range(2):
                        ins = pe.transpose(psV[h][:, n * P:(n + 1) * P], xs[:, h * D + n * P:h * D + (n + 1) * P], ident[:, :])
                    ins.then_inc(s_xt, 1)
                elif s % 4 == 2:
                    pe.wait_ge(s_xtc, b + 3)
                    pe.wait_ge(s_xa, b + 1)
                    for n in range(2):
                        ins = pe.matmul(psG[h][:, 0:D], xts[:, h * D + n * P:h * D + (n + 1) * P],
                                        W1[:, n * D:(n + 1) * D], start=(n == 0), stop=(n == 1))
                    ins.then_inc(s_xp, 1)

            def body(i, step=step, groups=groups, its=its):
                for s in range(GR if groups or step == "sort" else 0):
                    if groups:
                        tiles_of(i, s)
                    if step == "own" and s < 4 * (LD if its > 1 else 1):
                        own(i, s)
                    if step == "sort":
                        column(i, s)
                    if step in ("heads", "tail") and s >= 10:
                        pieces = (1 if step == "tail" else HD) * 2
                        per = -(-pieces // 6)
                        if s == 10:
                            pe.wait_ge(s_kn, i + (m0 + 1))
                        mine = range(min((s - 10) * per, pieces), min((s - 9) * per, pieces))
                        if mine:
                            ins = products(mine)
                            if mine[-1] == pieces - 1:
                                ins.then_inc(s_kg, 1)

            if step == "kv":
                for h in range(2):
                    ins = pe.matmul(psG[h][:, 0:KW], zero32[:, :], W1[:, 0:KW], start=False, stop=True,
                                    skip_group_check=True)
                ins.then_inc(s_kg, 1)
                for h in range(2):
                    pe.wait_ge(s_dg, h + 1)
                    pe.matmul(psP[:, h * P:(h + 1) * P], ones[:, :], kvw[:, (4 + h) * P:(5 + h) * P], start=True,
                              stop=True).then_inc(s_se, 1)
                pe.wait_ge(s_kv, 1)
            if groups or step == "sort":
                repeat(pe, its, body)
                b0 += its * LD if step == "own" else 0
                t0 += its * GR * groups
                k0 += its * CU if step == "sort" else 0
                m0 += its if step in ("heads", "tail") else 0
            if step == "decode":
                for n in range(2):
                    ins = pe.matmul(psV[n][:, 0:CHUNKS[c][3]], zero16[0:EP, :], iota_t[0:EP, 0:CHUNKS[c][3]],
                                    start=False, stop=True, skip_group_check=True)
                ins.then_inc(s_sx, 1)

    @block.vector
    def _(v):
        step_count = Tally(s_v)
        step = step_count.add

        def wait(back=0):
            v.wait_ge(s_v, step_count.value(back))

        v.memset(eps[:, :], LN_EPS).then_inc(s_dc, 1)
        v.memset(XA[:, xcols(NB - 1)], 0.0).then_inc(s_pad, 1)
        v.memset(zero16[:, :], 0.0)
        v.memset(zero32[:, :], 0.0)
        v.memset(ones16[:, :], 1.0)
        v.memset(onesw[:, :], 1.0)
        v.memset(pos[:, :], 0.0)
        v.wait_ge(s_pc, 7)
        v.tensor_copy(iota_t[:, :], iota_i[:, :])
        v.tensor_scalar(iota_1[:, :], iota_i[:, 0:P], 1.0, None, ALU.add)
        v.tensor_copy(iota_b[:, :], iota_i[:, 0:NB])
        v.tensor_copy(XA[:, RW - 1:NB * RW:RW], mi[:, 0:NB])
        v.tensor_scalar(kk["iota8"][:, :], iota_i[:, 0:NX], -1.0, float(NX), ALU.mult, ALU.add)
        v.memset(LH[:, :], 0.0).then_inc(s_dc, 1)
        v.sem_inc(s_ht, GR)
        v.sem_inc(s_ev, 2)

        v.wait_ge(s_edge, 32)
        step(v.tensor_scalar(tmpi[0:EP, :], srci[0:EP, :], 7, None, ALU.logical_shift_right))
        step(v.tensor_scalar(tmpj[0:EP, :], dsti[0:EP, :], 3, None, ALU.logical_shift_right))
        wait()
        v.tensor_copy(blk[0:EP, :], tmpi[0:EP, :])
        step(v.tensor_copy(v1[0:EP, :], tmpj[0:EP, :]))
        wait()
        v.tensor_scalar(tmpi[0:EP, :], srci[0:EP, :], P - 1, None, ALU.bitwise_and)
        step(v.tensor_scalar(tmpj[0:EP, :], dsti[0:EP, :], 7, None, ALU.bitwise_and))
        wait()
        step(v.tensor_scalar(v2[0:EP, :], tmpj[0:EP, :], 256.0, 1.0, ALU.mult, ALU.add))
        wait()
        step(v.tensor_tensor(v2[0:EP, :], v2[0:EP, :], tmpi[0:EP, :], ALU.add))
        wait()

        def stats(h, nb, at):
            for j in range(nb):
                q = h * LD + j
                step(v.bn_stats(lnst[:, 6 * q:6 * q + 6], XA[:, at(j)]))
            wait()
            v.sem_inc(s_past, 1)
            for j in range(nb):
                q = h * LD + j
                ins = v.bn_aggr(lnmv[:, 2 * q:2 * q + 2], lnst[:, 6 * q:6 * q + 6])
            ins.then_inc(s_stat, 1)

        def scale(h, nb, k):
            v.wait_ge(s_sd, k)
            step(v.reciprocal(lnrs[:, h * LD:h * LD + nb], lnsd[:, h * LD:h * LD + nb]))
            wait()
            v.scalar_tensor_tensor(out=lnmr[:, h * LD:h * LD + nb], in0=lnmv[:, 2 * h * LD:2 * (h * LD + nb):2],
                                   scalar=-1.0, in1=lnrs[:, h * LD:h * LD + nb], op0=ALU.mult, op1=ALU.mult).then_inc(s_nrm, 1)

        def low(h, nb, at, k):
            v.wait_ge(s_hi, k)
            o = h * LD * 2 * D
            tb = TB[:, o:o + nb * 2 * D].rearrange("p (j d) -> p j d", j=nb)
            v.scalar_tensor_tensor(out=tb[:, :, D:2 * D], in0=xblocks(XA, at, nb),
                                   scalar=PARTS, in1=tb[:, :, 0:D], op0=ALU.mult, op1=ALU.subtract).then_inc(s_lo, 1)

        n = NB // (2 * LD)

        def pair(i, back):
            v.wait_ge(s_x, i * 16 + 32)
            for h in range(2):
                stats(h, LD, lambda j: xcols(i * (2 * LD) + (h * LD + j)))
            if back:
                for h in range(2):
                    low(h, LD, i * (2 * LD) + (h - 2) * LD, i * 2 + (h - 1))
            for h in range(2):
                scale(h, LD, i * 2 + (h + 1))

        def last():
            v.wait_ge(s_xl, 16)
            stats(0, 1, lambda j: xcols(NB - 1))
            scale(0, 1, 2 * n + 1)
            for h in range(2):
                low(h, LD, (2 * n - 2 + h) * LD, 2 * n - 1 + h)
            low(0, 1, NB - 1, 2 * n + 1)

        pair(0, False)

        def source_onehot(i, s, t0):
            q = s % SR
            v.tensor_scalar(S[:, q * P:(q + 1) * P], iota_1[:, :], srch[:, s:s + 1], None, ALU.is_equal).then_inc(s_S, 1)

        offsets = []

        def add_tile(i, s, t0):
            t = i * GR + (t0 + s)
            v.wait_ge(s_tile, t + (GR + 1))
            v.wait_ge(s_ev, t + 2)
            o = offsets[s]
            v.tensor_tensor(XA[:, ds(o, AGW)], XA[:, ds(o, AGW)], psA[s % 2][:, 0:AGW], ALU.add).then_inc(s_ev, 1)

        def fetch(i, k, g0):
            v.tensor_copy(idxr[:, QR * k:QR * k + QR], idx[:, ds(i * GR + (g0 * GR + QR * k), QR)]).then_inc(s_idx, 1)

        def sources(i, t0, scale=1.0):
            v.tensor_scalar(srch, srcl[:, ds(i * GR + t0, GR)], scale, None, ALU.mult).then_inc(s_srch, 1)

        def tile(i, s, t0, ahead, onehots=True):
            if s == 0:
                if onehots:
                    sources(i, t0)
                offsets[:] = nc.values_load_multi_w_load_instructions(
                    buck[0:1, ds(i * GR + t0, GR)], engines=[mybir.EngineType.DVE], min_val=0, max_val=(NB - 1) * RW,
                    skip_runtime_bounds_check_because="the place step clamps the tiles' blocks to NB - 1")[1]
                if onehots:
                    v.wait_ge(s_srch, i + (t0 // GR + 1))
                    source_onehot(i, 0, t0)
                    source_onehot(i, 1, t0)
            if onehots and s + 2 < GR:
                source_onehot(i, s + 2, t0)
            add_tile(i, s, t0)
            if ahead and s % QR == QR - 1:
                fetch(i, s // QR, t0 // GR + 1)

        v.sem_inc(s_xtc, 2)
        v.sem_inc(s_xa, 2)
        t0, k0, m0, b0 = 0, 0, 0, 0
        v.memset(kn[:, P:LD * 2 * KW:KW], 1.0)
        for c, name, its, groups, ahead in PHASES:
            if c < len(CHUNKS):
                c0, cols, ch0, tiles = CHUNKS[c]
            if name == "count":
                if c == 1:
                    v.wait_ge(s_agg, 1)

                def count(i):
                    step(v.tensor_copy(b7[0:EP, :], iota_b[0:EP, ds(i * B7, B7)]))
                    wait()
                    for j in range(B7):
                        o = j * WMAX
                        ins = v.tensor_scalar(mask[0:EP, o:o + cols], blk[0:EP, c0:c0 + cols], b7[0:EP, j:j + 1], 0.0,
                                              ALU.is_equal, ALU.add, accum_out=n7[0:EP, j:j + 1])
                    step(ins)
                    wait()
                    step(v.tensor_copy(cnt[0:EP, ds(i * B7, B7)], n7[0:EP, :]))
                with v.Fori(0, its) as i:
                    step_count.loop(i, 3)
                    count(i)
                step_count.end(its)
                v.wait_ge(s_v, step_count.value())
                step(v.memset(mcol[:, :], 0.0))
                wait()
                v.memset(mcoli[:, :], 0).then_inc(s_cnt, 1)
            elif name == "place":
                v.wait_ge(s_pre, c + 1)
                v.tensor_scalar(mi[:, 0:NB], psP[:, 64:64 + NB], float(P - 1), None, ALU.add)
                step(v.tensor_scalar(mcoli[0:NB, 0:1], psQ[0:NB, 0:1], float(P - 1), None, ALU.add))
                wait()
                v.tensor_scalar(mi[:, NB:2 * NB], mi[:, 0:NB], 7, None, ALU.logical_shift_right)
                step(v.tensor_scalar(mcoli[0:NB, 1:2], mcoli[0:NB, 0:1], 7, None, ALU.logical_shift_right))
                wait()
                step(v.tensor_copy(mrow[:, :], mi[:, NB:2 * NB]))
                v.tensor_copy(mcol[0:NB, 0:1], mcoli[0:NB, 1:2]).then_inc(s_mc, 1)
                wait()
                step(v.tensor_tensor_scan(mend[:, :], ones[:, 0:NB], mrow[:, :], 0.0, ALU.mult, ALU.add))
                wait()
                step(v.tensor_tensor(mrow[:, :], mend[:, :], mrow[:, :], ALU.subtract))
                wait()
                step(v.scalar_tensor_tensor(out=base[0:EP, :], in0=mrow[0:EP, :], scalar=float(P), in1=psP[0:EP, 0:NB],
                                            op0=ALU.mult, op1=ALU.add))
                wait()
                step(v.tensor_scalar(base[0:EP, :], base[0:EP, :], -1.0, None, ALU.add))
                v.wait_ge(s_ec, c + 1)
                step(v.tensor_copy(mcol[0:NB, 2:3], psQ[0:NB, 0:1]))
                wait()
                v.tensor_scalar(ge[0:NB, 0:tiles], iota_t[0:NB, 0:tiles], mcol[0:NB, 2:3], None, ALU.is_ge).then_inc(s_ge, 1)
                v.wait_ge(s_bk, c + 1)
                step(v.tensor_scalar(buck[0:1, ch0:ch0 + tiles], psQ[0:1, 0:tiles], float(NB - 1), float(RW),
                                     ALU.min, ALU.mult))
                wait()
            elif name == "rank":
                def rank(i, groups=groups, ahead=ahead, t0=t0):
                    if groups:
                        sources(i, t0, -1.0)
                    wait()
                    v.tensor_copy(b7[0:EP, :], iota_b[0:EP, ds(i * B7, B7)])
                    step(v.tensor_copy(n7[0:EP, :], base[0:EP, ds(i * B7, B7)]))
                    wait()
                    for j in range(B7):
                        ins = v.tensor_scalar(mask[0:EP, j * WMAX:j * WMAX + cols], blk[0:EP, c0:c0 + cols], b7[0:EP, j:j + 1],
                                              None, ALU.is_equal)
                    step(ins)
                    wait()
                    for j in range(B7 + 1):
                        if j < B7:
                            q = j % 3
                            step(v.tensor_tensor_scan(cum[0:EP, q * WMAX:q * WMAX + cols], onesw[0:EP, 0:cols],
                                                      mask[0:EP, j * WMAX:j * WMAX + cols], n7[0:EP, j:j + 1], ALU.mult, ALU.add))
                        if j:
                            q = (j - 1) % 3
                            m = mask[0:EP, (j - 1) * WMAX:(j - 1) * WMAX + cols]
                            wait(1 if j < B7 else 0)
                            v.sem_inc(s_past, 1)
                            step(v.copy_predicated(pos[0:EP, 0:cols], m.bitcast(U16), cum[0:EP, q * WMAX:q * WMAX + cols]))
                        if groups:
                            for s in range(2 * j, 2 * j + 2):
                                tile(i, s, t0, ahead, False)
                first = 0
                if c == 0:
                    first = n - 1
                    with v.Fori(0, first) as i:
                        step_count.loop(i, 2 + 2 * B7 + 2 * LD + 2)
                        rank(i)
                        pair(i + 1, True)
                    step_count.end(first)
                    last()
                with v.Fori(0, its - first) as i:
                    step_count.loop(i, 2 + 2 * B7)
                    rank(i + first)
                step_count.end(its - first)
            elif name == "split":
                wait()
                step(v.tensor_copy(posi[0:EP, 0:cols], pos[0:EP, 0:cols]))
                wait()
                step(v.tensor_scalar(tli[0:EP, 0:cols], posi[0:EP, 0:cols], 7, None, ALU.logical_shift_right))
                wait()
                step(v.tensor_copy(tf[0:EP, 0:cols], tli[0:EP, 0:cols]))
                wait()
                step(v.tensor_scalar(tli[0:EP, 0:cols], posi[0:EP, 0:cols], P - 1, None, ALU.bitwise_and))
                wait()
                step(v.tensor_copy(pos[0:EP, 0:cols], tli[0:EP, 0:cols]))
                wait()
            elif name == "sort":
                def sort(i, share=VSHARE, groups=groups, ahead=ahead, t0=t0, k0=k0):
                    v.wait_ge(s_ht, i * CU + (k0 + GR))
                    v.tensor_copy(posh[0:EP, :], pos[0:EP, ds(i * CU + (k0 - c0), CU)])
                    if not groups:
                        v.tensor_copy(v1h[0:EP, :], v1[0:EP, ds(i * CU + k0, CU)])
                    v.tensor_copy(tfh[0:EP, :], tf[0:EP, ds(i * CU + (k0 - c0), CU)]).then_inc(s_posh, 1)
                    v.wait_ge(s_posh, i + (k0 // CU + 1))

                    def operands(j):
                        if j % CW == 0:
                            v.wait_ge(s_col, i * CU + (k0 + j + CW))
                        for n in range(j, j + CW):
                            q = n % KR
                            v.tensor_scalar(LH[0:EP, q * P:(q + 1) * P], iota_t[0:EP, 0:P],
                                            posh[0:EP, n:n + 1], None, ALU.is_equal).then_inc(s_lh, 1)
                        for n in range(j, j + CW) if not groups else ():
                            if n % share != share - 1:
                                continue
                            q = n % KR
                            v.tensor_scalar(LV[0:EP, 2 * q * P:(2 * q + 1) * P], iota_t[0:EP, 0:P],
                                            posh[0:EP, n:n + 1], v1h[0:EP, n:n + 1], ALU.is_equal, ALU.mult)
                        for n in range(j, j + CW):
                            q = n % KR
                            v.tensor_scalar(HT[0:EP, q * TMAX:q * TMAX + tiles], iota_t[0:EP, 0:tiles],
                                            tfh[0:EP, n:n + 1], None, ALU.is_equal).then_inc(s_ht, 1)

                    for j in range(0, AHEAD if groups else CW, CW):
                        operands(j)
                    for j in range(CU):
                        if groups:
                            if j % CW == 0 and j + AHEAD < CU:
                                operands(j + AHEAD)
                            tile(i, j, t0, ahead)
                        elif j % CW == 0 and j:
                            operands(j)
                repeat(v, its, sort)
            elif name == "decode":
                v.wait_ge(s_sx, c + 1)
                a, b, d, e = (DI[:, n * TMAX:n * TMAX + tiles] for n in range(4))
                v.tensor_copy(a, psV[0][:, 0:tiles])
                step(v.tensor_copy(b, psV[1][:, 0:tiles]))
                wait()
                v.tensor_scalar(d, a, 3, None, ALU.logical_shift_left)
                step(v.tensor_scalar(e, b, 8, None, ALU.logical_shift_right))
                wait()
                step(v.tensor_tensor(idx[:, ch0:ch0 + tiles], d, e, ALU.bitwise_or))
                step(v.tensor_scalar(a, b, 255, None, ALU.bitwise_and))
                wait()
                v.tensor_copy(srcl[:, ch0:ch0 + tiles], a).then_inc(s_dec, 1)
                v.wait_ge(s_dec, c + 1)
                v.wait_ge(s_tile, ch0 + GR)
                for n in range(GR // QR):
                    fetch(0, n, ch0 // GR)
            elif name in ("heads", "tail"):
                nb = HD if name == "heads" else 1
                nh = nb * HEADS

                def heads(i, s):
                    w = slice(0, nb * D)
                    h3 = lambda ap: ap.rearrange("p (g d) -> p g d", d=HC)
                    h4 = lambda ap: ap.rearrange("p j (g d) -> p j g d", d=HC)
                    by4 = lambda ap: ap.rearrange("p (j g) -> p j g", g=HEADS)
                    wide = lambda ap: ap.unsqueeze(2).to_broadcast([P, nh, HC])
                    xb = h4(xblocks(XA, (i + m0) * HD, nb))
                    if s == 0:
                        step(v.tensor_reduce(by4(hs[:, 0:nh]), xb, AX.X, ALU.add))
                    elif s == 1:
                        wait()
                        step(v.tensor_scalar(hm[:, 0:nh], hs[:, 0:nh], 1.0 / HC, None, ALU.mult))
                    elif s == 2:
                        wait()
                        v.tensor_tensor(cen[:, w].rearrange("p (j g d) -> p j g d", j=nb, d=HC), xb,
                                        by4(hm[:, 0:nh]).unsqueeze(3).to_broadcast([P, nb, HEADS, HC]),
                                        ALU.subtract).then_inc(s_cen, 1)
                    elif s == 4:
                        v.wait_ge(s_sq, i + (m0 + 1))
                        v.tensor_reduce(hq[:, 0:nh], h3(sqr[:, w]), AX.X, ALU.add).then_inc(s_ss, 1)
                    elif s == 6:
                        v.wait_ge(s_hstd, i + (m0 + 1))
                        step(v.tensor_scalar(hs[:, 0:nh], hq[:, 0:nh], HEAD_EPS, None, ALU.add))
                    elif s == 7:
                        wait()
                        step(v.reciprocal(hr[:, 0:nh], hs[:, 0:nh]))
                    elif s == 8:
                        wait()
                        v.wait_ge(s_kg, i + (m0 + 1))
                        v.tensor_tensor(kn[:, 0:nb * 2 * KW].rearrange("p (k w) -> p k w", w=KW)[:, :, 0:P].rearrange(
                            "p k (g d) -> p k g d", d=HC), cen[:, w].rearrange("p (k g d) -> p k g d", d=HC, k=nb * 2),
                            hr[:, 0:nh].rearrange("p (k g) -> p k g", k=nb * 2).unsqueeze(3).to_broadcast(
                                [P, nb * 2, P // HC, HC]), ALU.mult).then_inc(s_kn, 1)

                def body(i, t0=t0, ahead=ahead):
                    for s in range(GR):
                        tile(i, s, t0, ahead)
                        if s < 10:
                            heads(i, s)
                if its > 1:
                    with v.Fori(0, its) as i:
                        step_count.loop(i, 4)
                        body(i)
                    step_count.end(its)
                else:
                    body(0)
                m0 += its
            elif name == "rest":
                def body(i, t0=t0, ahead=ahead):
                    for s in range(GR):
                        tile(i, s, t0, ahead)
                repeat(v, its, body)
            elif name == "kv":
                v.wait_ge(s_par, 16 * 12)
                v.wait_ge(s_kg, NB // HD + 3)
                step(v.tensor_tensor(brow[:, :], brow[:, :], b2r[:, :], ALU.add))
                for h in range(2):
                    v.tensor_scalar(kvw[:, (4 + h) * P:(5 + h) * P], ident[:, :], psG[h][:, P:P + 1], None, ALU.mult).then_inc(s_dg, 1)
                v.wait_ge(s_se, 2)
                for h in range(2):
                    g, se, sd_ = psG[h][:, 0:P], psP[:, h * P:(h + 1) * P], psG[h][:, P:P + 1]
                    vwr, vbr = hrow[:, h * P:(h + 1) * P], hrow[:, D + h * P:D + (h + 1) * P]
                    kwc, kbc = hv[:, 2 * h:2 * h + 1], hv[:, 2 * h + 1:2 * h + 2]
                    t_ = [kvw[:, n * P:(n + 1) * P] for n in range(4)]
                    step(v.tensor_scalar(t_[0], se, kbc, None, ALU.mult))
                    step(v.tensor_scalar(mcol[:, 0:1], sd_, kwc, None, ALU.mult))
                    wait()
                    step(v.scalar_tensor_tensor(out=t_[1], in0=g, scalar=kwc, in1=t_[0], op0=ALU.mult, op1=ALU.add))
                    step(v.scalar_tensor_tensor(out=mcol[:, 1:2], in0=kbc, scalar=float(N), in1=mcol[:, 0:1],
                                                op0=ALU.mult, op1=ALU.add))
                    wait()
                    step(v.tensor_tensor(t_[2], t_[1], vwr, ALU.mult))
                    wait()
                    step(v.scalar_tensor_tensor(out=t_[3], in0=vbr, scalar=mcol[:, 1:2], in1=t_[2], op0=ALU.mult, op1=ALU.add))
                    wait()
                    for a in range(0, P, HC):
                        w = W1[a:a + HC, h * D + h * P + a:h * D + h * P + a + HC]
                        step(v.scalar_tensor_tensor(out=w, in0=t_[3][a:a + HC, a:a + HC], scalar=1.0 / N, in1=w,
                                                    op0=ALU.mult, op1=ALU.add))
                    wait()
                v.memset(mcol[:, :], 0.0).then_inc(s_kv, 1)
            elif name == "own":
                def body(i, t0=t0, ahead=ahead, b0=b0, nb=LD if its > 1 else 1):
                    for s in range(GR):
                        tile(i, s, t0, ahead)
                        if (s % 4 == 0 and 0 < s <= 4 * (nb - 1)) or s == (GR - 1 if nb == LD else 3):
                            j = -(-s // 4) - 1
                            b = i * LD + (b0 + j)
                            v.wait_ge(s_xp, b + 3)
                            v.tensor_tensor(XA[:, xcols(b)], XA[:, xcols(b)], psG[j % 2][:, 0:D], ALU.add).then_inc(s_xa, 1)
                repeat(v, its, body)
                b0 += its * LD
            t0 += its * GR * groups
            k0 += its * CU if name == "sort" else 0


def nodes(nc, ctx, kk, dram, x, f1, f2, fb2, out):
    def sb(name, shape, dt):
        return ctx.enter_context(nc.sbuf_tensor(name, shape, dt))

    def sem(name):
        return ctx.enter_context(nc.semaphore(name))

    XA, ident, ones, eps, W2, brow, gw, gb = (kk[n] for n in (
        "XA", "ident", "ones", "eps", "W2", "brow", "gw", "gb"))
    bank = kk["psum"]
    psT, psM, psU, psL = bank[0:2], bank[2:4], bank[4:6], bank[6:8]
    LW = NQ * NX
    PT, PD = 64, 128
    rcn = sb("rcn", [P, NB], F32)
    xr = sb("xr", [P, 2 * NQ * D], F32)
    xlast = sb("xlast", [P, D], F32)
    mean = sb("mean", [P, 2 * D], F32)
    mt = sb("mt", [P, 2 * D], F32)
    tmp = sb("tmp", [P, 2 * D], F32)
    nst = sb("nst", [P, NQ * 6], F32)
    nmv = sb("nmv", [P, NQ * 2], F32)
    nsd = sb("nsd", [P, NQ], F32)
    nrs = sb("nrs", [P, NQ], F32)
    nmr = sb("nmr", [P, NQ], F32)
    ut = sb("ut", [P, 2 * D], F32)
    less = sb("less", [P, P], F32)
    seg = sb("seg", [P, LW], F32)
    carry = sb("carry", [P, NX], F32)
    lg, r0, r1, r2, r3, r4 = (sb(f"route{n}", [P, LW], F32) for n in range(6))
    q = [sb(f"rnode{n}", [P, NQ], F32) for n in range(9)]
    sidx = sb("sidx", [P, NB], I32)

    s_xr = [sem("x_again_0"), sem("x_again_1")]
    s_rc, s_xb, s_mean, s_tr, s_mt, s_mm, s_xm, s_x1 = (sem(n) for n in (
        "count_reciprocals", "x_with_bias", "mean_ready", "mean_transposed", "mean_t_copied", "mean_products",
        "mean_products_added", "x1_ready"))
    s_v, s_nv, s_ns, s_nr, s_x2, s_u, s_ut, s_lg = (sem(n) for n in (
        "node_steps", "x1_variance", "x1_std", "x1_scale", "x1_normal", "x1n_transposed", "x1n_t_copied", "logits"))
    s_mx, s_ex, s_oh, s_pf, s_rt, s_sl = (sem(n) for n in (
        "logit_max", "logit_exp", "expert_onehot", "expert_prefix", "prefix_read", "slots_ready"))
    s_xl, s_zx = sem("last_x_again"), sem("last_x_zero")
    s_sc, s_xo = sem("rows_scattered"), sem("x1_stored")
    block = ctx.enter_context(nc.Block())
    NT = NB // NQ
    NORM, GATE = NQ + 3, NQ + 4
    ROUTE = GATE + NQ + 1
    STEPS = (NT - 1) * NQ + ROUTE + NQ

    def blk(n, lag):
        return n - lag if 0 <= n - lag < NB else None

    def batch(n, lag):
        return (n - lag) // NQ if (n - lag) % NQ == 0 and 0 <= n - lag < NB else None

    @block.sync
    def _(sp):
        def store(t, nb):
            sp.dma_start(out[t * NQ * P:(t * NQ + nb) * P, :].rearrange("(j p) d -> p j d", p=P),
                         xblocks(XA, t * NQ, nb)).then_inc(s_xo, 16)
        sp.wait_ge(s_zx, 1)
        sp.dma_start(xlast[0:LASTROWS, :], x[(NB - 1) * P:N, :]).then_inc(s_xl, 16)
        for t in range(NT):
            if t >= 2:
                sp.wait_ge(s_x1, (t - 1) * NQ)
            o = t % 2 * NQ * D
            nb = NQ if t < NT - 1 else NQ - 1
            sp.dma_start(xr[:, o:o + nb * D].rearrange("p (j d) -> p j d", d=D),
                         x[t * NQ * P:(t * NQ + nb) * P, :].rearrange("(j p) d -> p j d", p=P)).then_inc(s_xr[t % 2], 16)
            if t == 1:
                load_weights(sp, kk["w1_0"], kk["w2_0"], kk["b2_0"], f1, f2, fb2, 0, kk["s_w0"])
            if t >= 2:
                store(t - 2, NQ)
        sp.wait_ge(s_x1, (NT - 1) * NQ)
        store(NT - 2, NQ)
        sp.wait_ge(s_x1, NB)
        store(NT - 1, NQ - 1)
        sp.dma_start(out[(NB - 1) * P:N, :], XA[0:LASTROWS, xcols(NB - 1)]).then_inc(s_xo, 16)
        sp.wait_ge(s_xo, 16 * (NT + 1))

    @block.scalar
    def _(act):
        def place(n):
            h = n % 2
            if n >= 2:
                act.wait_ge(s_tr, n - 1)
            act.activation(mean[:, h * D:(h + 1) * D], XA[:, n * RW:n * RW + D], ACT.Copy,
                           scale=rcn[:, n:n + 1]).then_inc(s_mean, 1)
        act.wait_ge(s_rc, 1)
        place(0)
        for n in range(STEPS):
            t = batch(n, NORM)
            if t is not None:
                act.wait_ge(s_nv, t + 1)
                act.activation(nsd[:, :], nmv[:, 1:2 * NQ:2], ACT.Sqrt, bias=eps[:, :]).then_inc(s_ns, 1)
            if n + 1 < NB:
                place(n + 1)
            if n < NB:
                h = n % 2
                act.wait_ge(s_tr, n + 1)
                if n >= 2:
                    act.wait_ge(s_mm, n - 1)
                act.activation(mt[:, h * D:(h + 1) * D], psT[h][:, 0:D], ACT.Copy).then_inc(s_mt, 1)
            m = blk(n, GATE)
            if m is not None:
                g = m % 2
                act.wait_ge(s_u, m + 1)
                if m >= 2:
                    act.wait_ge(s_lg, m - 1)
                act.activation(ut[:, g * D:(g + 1) * D], psU[g][:, 0:D], ACT.Copy).then_inc(s_ut, 1)
            m = blk(n, NORM)
            if m is not None:
                if m % NQ == 0:
                    act.wait_ge(s_nr, m // NQ + 1)
                act.activation(XA[:, m * RW:m * RW + D], XA[:, xcols(m)], ACT.Identity, bias=nmr[:, m % NQ:m % NQ + 1],
                               scale=nrs[:, m % NQ:m % NQ + 1]).then_inc(s_x2, 1)
            t = batch(n, ROUTE + 1)
            if t is not None:
                act.wait_ge(s_mx, t + 1)
                act.activation(r3[:, :], r3[:, :], ACT.Exp).then_inc(s_ex, 1)

    @block.tensor
    def _(pe):
        for n in range(STEPS):
            if n < NB:
                h = n % 2
                pe.wait_ge(s_mean, n + 1)
                if n >= 2:
                    pe.wait_ge(s_mt, n - 1)
                for k in range(2):
                    ins = pe.transpose(psT[h][:, k * P:(k + 1) * P], mean[:, h * D + k * P:h * D + (k + 1) * P], ident[:, :])
                ins.then_inc(s_tr, 1)
            m = blk(n, GATE)
            if m is not None:
                g = m % 2
                pe.wait_ge(s_x2, m + 1)
                if m >= 2:
                    pe.wait_ge(s_ut, m - 1)
                o = m * RW
                for k in range(2):
                    ins = pe.transpose(psU[g][:, k * P:(k + 1) * P], XA[:, o + k * P:o + (k + 1) * P], ident[:, :])
                ins.then_inc(s_u, 1)
            t = batch(n, ROUTE + 3)
            if t is not None:
                pe.wait_ge(s_oh, t + 1)
                pe.matmul(psL[t % 2][:, PT:PT + LW], ones[:, :], r1[:, :], start=True, stop=True)
                pe.matmul(psL[t % 2][:, PD:PD + LW], less[:, :], r1[:, :], start=True, stop=True).then_inc(s_pf, 1)
            m = blk(n, 1)
            if m is not None:
                h = m % 2
                pe.wait_ge(s_mt, m + 1)
                if m >= 2:
                    pe.wait_ge(s_xm, m - 1)
                for k in range(2):
                    ins = pe.matmul(psM[h][:, 0:D], mt[:, h * D + k * P:h * D + (k + 1) * P],
                                    W2[:, k * D:(k + 1) * D], start=(k == 0), stop=(k == 1))
                ins.then_inc(s_mm, 1)
            m = blk(n, GATE + 1)
            if m is not None:
                g, t, j = m % 2, m // NQ, m % NQ
                pe.wait_ge(s_ut, m + 1)
                if j == 0 and t >= 2:
                    pe.wait_ge(s_rt, t - 1)
                for k in range(2):
                    ins = pe.matmul(psL[t % 2][:, j * NX:(j + 1) * NX], ut[:, g * D + k * P:g * D + (k + 1) * P],
                                    gw[:, k * NX:(k + 1) * NX], start=(k == 0), stop=(k == 1))
                ins.then_inc(s_lg, 1)

    @block.vector
    def _(v):
        count = Tally(s_v)
        step = count.add

        def wait():
            v.wait_ge(s_v, count.value())
        v.memset(xlast[:, :], 0.0).then_inc(s_zx, 1)
        v.memset(seg[:, :], 1.0)
        v.memset(carry[:, :], 0.0)
        v.tensor_scalar(less[:, :], kk["upper"][:, :], -1.0, None, ALU.add)
        step(v.tensor_scalar(rcn[:, :], XA[:, D:NB * RW:RW], 1.0, PARTS, ALU.max, ALU.mult))
        wait()
        step(v.memset(seg[:, 0:LW:NQ], 0.0))
        v.reciprocal(rcn[:, :], rcn[:, :]).then_inc(s_rc, 1)

        g3 = lambda ap: ap.rearrange("p (b e) -> p b e", e=NX)
        wide = lambda ap: ap.unsqueeze(2).to_broadcast([P, NQ, NX])
        io8 = kk["iota8"][:, :].unsqueeze(1).to_broadcast([P, NQ, NX])

        def route(t, s):
            mine = slice(t * NQ, (t + 1) * NQ)
            if 0 < s < 20:
                wait()
            if s == 0:
                v.wait_ge(s_lg, t * NQ + NQ)
                step(v.tensor_tensor(g3(lg[:, :]), g3(psL[t % 2][:, 0:LW]), gb[:, :].unsqueeze(1).to_broadcast([P, NQ, NX]), ALU.add))
            elif s == 1:
                step(v.tensor_reduce(q[0][:, :], g3(lg[:, :]), AX.X, ALU.max))
            elif s == 2:
                v.tensor_tensor(g3(r3[:, :]), g3(lg[:, :]), wide(q[0][:, :]), ALU.subtract).then_inc(s_mx, 1)
            elif s == 3:
                step(v.tensor_tensor(g3(r0[:, :]), g3(lg[:, :]), wide(q[0][:, :]), ALU.is_equal))
            elif s == 4:
                step(v.tensor_tensor(g3(r0[:, :]), g3(r0[:, :]), io8, ALU.mult))
            elif s == 5:
                step(v.tensor_reduce(q[1][:, :], g3(r0[:, :]), AX.X, ALU.max))
            elif s == 6:
                v.tensor_tensor(g3(r1[:, :]), io8, wide(q[1][:, :]), ALU.is_equal).then_inc(s_oh, 1)
            elif s == 7:
                v.wait_ge(s_ex, t + 1)
                step(v.tensor_reduce(q[2][:, :], g3(r3[:, :]), AX.X, ALU.add))
            elif s == 8:
                step(v.reciprocal(XA[:, t * NQ * RW + D:(t + 1) * NQ * RW:RW], q[2][:, :]))
            elif s == 9:
                v.wait_ge(s_pf, t + 1)
                step(v.tensor_copy(r2[:, :].rearrange("p (e b) -> p b e", b=NQ), g3(psL[t % 2][:, PT:PT + LW])))
            elif s == 10:
                step(v.tensor_tensor(r2[:, 0:LW:NQ], r2[:, 0:LW:NQ], carry[:, :], ALU.add))
            elif s == 11:
                step(v.tensor_tensor_scan(r4[:, :], seg[:, :], r2[:, :], 0.0, ALU.mult, ALU.add))
            elif s == 12:
                step(v.tensor_copy(carry[:, :], r4[:, NQ - 1:LW:NQ]))
            elif s == 13:
                v.tensor_tensor(g3(r0[:, :]), r4[:, :].rearrange("p (e b) -> p b e", b=NQ), g3(psL[t % 2][:, PD:PD + LW]),
                                ALU.add).then_inc(s_rt, 1)
            elif s == 14:
                v.wait_ge(s_rt, t + 1)
                step(v.tensor_tensor(r0[:, :], r0[:, :], r1[:, :], ALU.mult))
            elif s == 15:
                step(v.tensor_reduce(q[4][:, :], g3(r0[:, :]), AX.X, ALU.add))
            elif s == 16:
                step(v.tensor_scalar(q[5][:, :], q[4][:, :], float(CAP), None, ALU.is_lt))
                step(v.tensor_scalar(q[6][:, :], q[1][:, :], -float(CAPR), float(NX * CAPR), ALU.mult, ALU.add))
            elif s == 17:
                step(v.tensor_tensor(q[7][:, :], q[4][:, :], q[6][:, :], ALU.add))
            elif s == 18:
                step(v.scalar_tensor_tensor(out=q[0][:, :], in0=q[7][:, :], scalar=-float(NX * CAPR), in1=q[5][:, :],
                                            op0=ALU.add, op1=ALU.mult))
            elif s == 19:
                v.tensor_scalar(sidx[:, mine], q[0][:, :], float(NX * CAPR), None, ALU.add).then_inc(s_sl, 1)

        for n in range(STEPS):
            t = batch(n, NORM)
            if t is not None:
                v.wait_ge(s_ns, t + 1)
                step(v.reciprocal(nrs[:, :], nsd[:, :]))
                wait()
                v.scalar_tensor_tensor(out=nmr[:, :], in0=nmv[:, 0:2 * NQ:2], scalar=-1.0, in1=nrs[:, :],
                                       op0=ALU.mult, op1=ALU.mult).then_inc(s_nr, 1)
            m = blk(n, 2)
            if m is not None:
                h = m % 2
                v.wait_ge(s_xm, m + 1)
                if m % NQ == 0:
                    v.wait_ge(s_xb, m // NQ + 2)
                o = m % (2 * NQ) * D
                mine = xr[:, o:o + D] if m < NB - 1 else xlast[:, :]
                v.tensor_tensor(XA[:, xcols(m)], tmp[:, h * D:(h + 1) * D], mine, ALU.add).then_inc(s_x1, 1)
            m = blk(n, 3)
            if m is not None:
                v.wait_ge(s_x1, m + 1)
                o = m % NQ * 6
                step(v.bn_stats(nst[:, o:o + 6], XA[:, xcols(m)]))
            if n >= ROUTE and (n - ROUTE) // NQ < NT:
                for s in range(3):
                    route((n - ROUTE) // NQ, 3 * ((n - ROUTE) % NQ) + s)
            m = blk(n, 1)
            if m is not None:
                h = m % 2
                v.wait_ge(s_mm, m + 1)
                if m >= 2:
                    v.wait_ge(s_x1, m - 1)
                v.tensor_tensor(tmp[:, h * D:(h + 1) * D], psM[h][:, 0:D], XA[:, xcols(m)], ALU.add).then_inc(s_xm, 1)
            if batch(n + 1, NORM) is not None:
                wait()
                for j in range(NQ):
                    ins = v.bn_aggr(nmv[:, 2 * j:2 * j + 2], nst[:, 6 * j:6 * j + 6])
                ins.then_inc(s_nv, 1)

    @block.gpsimd
    def _(pool):
        def bias(w, n):
            pool.tensor_tensor(w.rearrange("p (j d) -> p j d", d=D), w.rearrange("p (j d) -> p j d", d=D),
                               brow[:, :].unsqueeze(1).to_broadcast([P, n, D]), ALU.add).then_inc(s_xb, 1)

        def scatter(t):
            pool.wait_ge(s_sl, t + 1)
            for j in range(NQ):
                rows = LASTROWS if t * NQ + j == NB - 1 else P
                b = t * NQ + j
                pool.indirect_dma_start(dram["buf"], bass.IndirectOffsetOnAxis(ap=sidx[0:rows, b:b + 1], axis=0),
                                        XA[0:rows, b * RW:(b + 1) * RW], None, bounds_check=NX * CAPR - 1,
                                        oob_is_err=False).then_inc(s_sc, 16)
        pool.wait_ge(s_xl, 16)
        bias(xlast[:, :], 1)
        for t in range(NT + 3):
            if t < NT:
                nb = NQ if t < NT - 1 else NQ - 1
                pool.wait_ge(s_xr[t % 2], 16 * (t // 2 + 1))
                bias(xr[:, t % 2 * NQ * D:(t % 2 * NQ + nb) * D], nb)
            if t >= 3:
                scatter(t - 3)
        pool.wait_ge(s_sc, 16 * NB)


def experts(nc, ctx, kk, dram, f1, fb1, f2, fb2, out):
    def sb(name, shape, dt):
        return ctx.enter_context(nc.sbuf_tensor(name, shape, dt))

    def sem(name):
        return ctx.enter_context(nc.semaphore(name))

    ident, bank, buf = kk["ident"], kk["psum"], dram["buf"]
    w1 = [kk["w1_0"], sb("w1_1", [P, 2 * F], F32)]
    w2 = [kk["w2_0"], sb("w2_1", [P, FT * D], F32)]
    b2 = [kk["b2_0"], sb("b2_1", [P, D], F32)]
    b1r = sb("b1r", [NX * FT, P], F32)
    b1c = sb("b1c", [P, NX * FT], F32)
    xb = sb("xb", [P, 2 * TQ * RW], F32)
    xt = sb("xt", [P, 2 * 2 * HALF], F32)
    ht = sb("ht", [P, FT * HALF], F32)
    y = sb("y", [P, TQ * D], F32)
    z = sb("z", [P, TQ * D], F32)
    lim = sb("lim", [P, TQ * D], F32)
    odd = sb("odd", [P, TQ * D], U32)
    zr = sb("zr", [P, TQ * D], F32)
    ob = sb("ob", [P, 2 * TQ * D], F32)
    none = sb("none", [P, TQ], F32)
    tok = sb("tok", [P, 2 * TQ], I32)
    s_w = [kk["s_w0"], sem("weights_1")]
    s_b = sem("first_biases")
    s_bt, s_bc = sem("first_biases_t"), sem("first_biases_copied")
    s_xb = [sem("rows_0"), sem("rows_1")]
    s_t, s_xt, s_h, s_r, s_yd, s_y, s_v, s_fin = (sem(n) for n in (
        "rows_transposed", "rows_t_copied", "hidden_product", "hidden_ready", "out_sums", "out_sums_read",
        "expert_steps", "rows_finished"))
    s_past = sem("past_a_wait_2")
    s_free = sem("finished_slot_free")
    s_st = [sem("out_scattered_0"), sem("out_scattered_1")]
    block = ctx.enter_context(nc.Block())
    psT, psH, psY = bank[0:2], bank[2:4], bank[4:6]

    def halves(eng, body):
        n = NX // 2
        with eng.Fori(0, n - 1) as i:
            for a in range(4):
                body(i, a, False)
        for a in range(4):
            body(n - 1, a, a == 3)

    @block.sync
    def _(sp):
        sp.dma_start(b1r[:, :], fb1.rearrange("e (f p) -> (e f) p", p=P)).then_inc(s_b, 16)

        def load(i, a, last):
            sp.wait_ge(s_fin, i * 4 + (a + 1))
            sp.dma_start(xb[0:TM, a % 2 * TQ * RW:(a % 2 + 1) * TQ * RW],
                         buf[ds((i * 4 + a) * HALF, HALF), :].rearrange("(p m) d -> p (m d)", m=TQ)).then_inc(s_xb[a % 2], 16)
            if a % 2 and not last:
                e, q = i * 2 + (a // 2 + 1), 1 - a // 2
                load_weights(sp, w1[q], w2[q], b2[q], f1, f2, fb2, e, s_w[q])
        halves(sp, load)

    @block.tensor
    def _(pe):
        pe.wait_ge(s_b, 16)
        pe.transpose(bank[6][:, 0:NX * FT], b1r[:, :], ident[0:NX * FT, 0:NX * FT]).then_inc(s_bt, 1)

        def transposes(i, a):
            h = a % 2
            pe.wait_ge(s_xb[h], (i * 2 + (a // 2 + 1)) * 16)
            for m in range(TQ):
                for k in range(2):
                    o = (h * TQ + m) * RW + k * P
                    ins = pe.transpose(psT[k][:, m * TM:(m + 1) * TM], xb[0:TM, o:o + P], ident[0:TM, 0:TM])
            ins.then_inc(s_t, 1)

        def half(i, a, last):
            n = i * 4 + a
            q, h = a // 2, a % 2
            if h == 0:
                pe.wait_ge(s_w[q], i * 48 + 48)
            pe.wait_ge(s_xt, n + 1)
            for f in range(FT):
                pe.wait_ge(s_r, n * FT + (f + 1))
                for k in range(2):
                    o = (h * 2 + k) * HALF
                    ins = pe.matmul(psH[f % 2][:, 0:HALF], w1[q][:, k * F + f * P:k * F + (f + 1) * P],
                                    xt[:, o:o + HALF], start=(k == 0), stop=(k == 1))
                ins.then_inc(s_h, 1)
            if not last:
                transposes(i, a + 1)
            for m in range(TQ):
                pe.wait_ge(s_y, n * TQ + (m + 1))
                for f in range(FT):
                    if m == 0:
                        pe.wait_ge(s_r, n * FT + (f + 3))
                    ins = pe.matmul(psY[m % 2][0:TM, 0:D], ht[:, f * HALF + m * TM:f * HALF + (m + 1) * TM],
                                    w2[q][:, f * D:(f + 1) * D], start=(f == 0), stop=(f == FT - 1))
                ins.then_inc(s_yd, 1)
        transposes(0, 0)
        halves(pe, half)

    @block.scalar
    def _(act):
        act.sem_inc(s_r, 2)
        act.wait_ge(s_bt, 1)
        act.activation(b1c[:, :], bank[6][:, 0:NX * FT], ACT.Copy).then_inc(s_bc, 1)
        act.wait_ge(s_bc, 1)

        def rows_t(n, h):
            act.wait_ge(s_t, n + 1)
            for k in range(2):
                ins = act.activation(xt[:, (h * 2 + k) * HALF:(h * 2 + k + 1) * HALF], psT[k][:, 0:HALF], ACT.Copy)
            ins.then_inc(s_xt, 1)

        def half(i, a, last):
            n = i * 4 + a
            act.wait_ge(s_yd, n * TQ + 1)
            for f in range(FT):
                act.wait_ge(s_h, n * FT + (f + 1))
                act.sem_inc(s_past, 1)
                act.activation(ht[:, f * HALF:(f + 1) * HALF], psH[f % 2][:, 0:HALF], ACT.Relu,
                               bias=b1c[:, ds((i * 2 + a // 2) * FT + f, 1)]).then_inc(s_r, 1)
            if not last:
                rows_t(i * 4 + (a + 1), 1 - a % 2)
        rows_t(0, 0)
        halves(act, half)

    @block.vector
    def _(v):
        count = Tally(s_v)

        def step(ins):
            count.add(ins)
            v.wait_ge(s_v, count.value())
            v.sem_inc(s_past, 1)
        v.sem_inc(s_y, 2)
        v.sem_inc(s_fin, 2)
        v.sem_inc(s_yd, 1)
        step(v.memset(zr[:, :], 0.0))

        def half(i, a):
            n = i * 4 + a
            q, h = a // 2, a % 2
            rows = xb[0:TM, h * TQ * RW:(h + 1) * TQ * RW].rearrange("p (m w) -> p m w", w=RW)
            for m in range(TQ):
                v.wait_ge(s_yd, n * TQ + (m + 2))
                v.tensor_tensor(y[0:TM, m * D:(m + 1) * D], psY[m % 2][0:TM, 0:D], b2[q][0:TM, :], ALU.add).then_inc(s_y, 1)
            v.wait_ge(s_y, n * TQ + (TQ + 2))
            for m in range(TQ):
                o = (h * TQ + m) * RW + D
                ins = v.tensor_scalar(z[0:TM, m * D:(m + 1) * D], y[0:TM, m * D:(m + 1) * D], xb[0:TM, o:o + 1], None, ALU.mult)
            step(ins)
            zz = z[0:TM, :]
            step(v.tensor_tensor(odd[0:TM, :], zz, zz, ALU.not_equal))
            step(v.copy_predicated(zz, odd[0:TM, :], zr[0:TM, :]))
            v.tensor_scalar(odd[0:TM, :], zz, 0.0, 0.0, ALU.mult, ALU.not_equal)
            step(v.tensor_scalar(lim[0:TM, :], zz, -10000.0, 10000.0, ALU.max, ALU.min))
            step(v.copy_predicated(zz, odd[0:TM, :], lim[0:TM, :]))
            v.wait_ge(s_free, n + 1)
            o3 = ob[0:TM, h * TQ * D:(h + 1) * TQ * D].rearrange("p (m d) -> p m d", d=D)
            v.tensor_tensor(o3, z[0:TM, :].rearrange("p (m d) -> p m d", d=D), rows[:, :, XO:XO + D], ALU.add)
            t1 = xb[0:TM, h * TQ * RW + RW - 1:(h + 1) * TQ * RW:RW]
            step(v.tensor_scalar(none[0:TM, :], t1, 0.0, float(NOROW), ALU.is_equal, ALU.mult))
            v.scalar_tensor_tensor(out=tok[0:TM, h * TQ:(h + 1) * TQ], in0=t1, scalar=-1.0, in1=none[0:TM, :],
                                   op0=ALU.add, op1=ALU.add).then_inc(s_fin, 1)
        with v.Fori(0, NX // 2) as i:
            count.loop(i, 4 * 6)
            for a in range(4):
                half(i, a)
        count.end(NX // 2)

    @block.gpsimd
    def _(pool):
        pool.sem_inc(s_free, 2)

        def half(i, a, last):
            h = a % 2
            pool.wait_ge(s_fin, i * 4 + (a + 3))
            pool.sem_inc(s_past, 1)
            for m in range(TQ):
                k = h * TQ + m
                pool.indirect_dma_start(out, bass.IndirectOffsetOnAxis(ap=tok[0:TM, k:k + 1], axis=0),
                                        ob[0:TM, k * D:(k + 1) * D], None, bounds_check=N - 1,
                                        oob_is_err=False).then_inc(s_st[h], 16)
            pool.wait_ge(s_st[h], (i * 2 + (a // 2 + 1)) * (16 * TQ))
            pool.sem_inc(s_free, 1)
        halves(pool, half)


def kernel(x, src, dst, L0_gnn_W1, L0_gnn_b1, L0_gnn_W2, L0_gnn_b2, L0_mix_kln_weight, L0_mix_kln_bias,
           L0_mix_vln_weight, L0_mix_vln_bias, L0_ffn_gate_w, L0_ffn_gate_b, L0_ffn_w1, L0_ffn_b1, L0_ffn_w2,
           L0_ffn_b2):
    import numpy as np
    import concourse.bacc as bacc
    from concourse.bass_utils import run_bass_kernel_spmd

    arrays = {
        "x": x, "src": src, "dst": dst,
        "w1t": np.asarray(L0_gnn_W1).T, "w2t": np.asarray(L0_gnn_W2).T, "gb1": L0_gnn_b1, "gb2": L0_gnn_b2,
        "kw": L0_mix_kln_weight, "kb": L0_mix_kln_bias, "vw": L0_mix_vln_weight, "vb": L0_mix_vln_bias,
        "gate_w": L0_ffn_gate_w, "gate_b": L0_ffn_gate_b,
        "f1": L0_ffn_w1, "fb1": L0_ffn_b1, "f2": L0_ffn_w2, "fb2": L0_ffn_b2,
    }
    arrays = {name: np.ascontiguousarray(a) for name, a in arrays.items()}
    nc = bacc.Bacc("TRN2", target_bir_lowering=False, num_devices=1)
    args = {name: nc.dram_tensor(name, a.shape, mybir.dt.from_np(a.dtype), kind="ExternalInput").ap()
            for name, a in arrays.items()}
    out = nc.dram_tensor("out", (N, D), F32, kind="ExternalOutput").ap()
    build_program(nc, **args, out=out)
    r = run_bass_kernel_spmd(nc, [arrays], core_ids=[0])
    return r.results[0]["out"]
```
